# Optimizing a Trainium2 kernel written in Bass

```python
import numpy as np
import jax
import jax.numpy as jnp

def _softmax(x, axis=-1):
    return jax.nn.softmax(x, axis=axis)

def _gelu(x):
    return jax.nn.gelu(x, approximate=True)

def _silu(x):
    return jax.nn.silu(x)

def _sigmoid(x):
    return jax.nn.sigmoid(x)

def _layernorm(x, axis=-1, eps=1e-05):
    m = jnp.mean(x, axis=axis, keepdims=True)
    v = jnp.var(x, axis=axis, keepdims=True)
    return (x - m) / jnp.sqrt(v + eps)

def _scatter_add(tgt, idx, src, axis=0):
    return tgt.at[idx].add(src)

def _segment_sum(src, seg, n):
    return jax.ops.segment_sum(src, seg, n)
kernel_name = 'mk_hybrid_d2_jaxref_r8_d1a509'

def setup_inputs(seed: int=0):
    np.random.seed(seed)
    _w = jnp.asarray

    def _L0_attn_a_setup():
        import jax, jax.numpy as jnp
        import numpy as np
        DIM = 128
        D_INNER = 128
        N_STATE = 32
        N_BLOCKS = 4
        TOP_K = 2
        ROUTER_TEMP = 1.0
        INIT_BETA_BIAS = 2.0
        BATCH = 16
        T = 256

        def _xavier(key, shape):
            fan_out, fan_in = shape
            lim = jnp.sqrt(6.0 / (fan_in + fan_out))
            return jax.random.uniform(key, shape, jnp.float32, -lim, lim)

        def _cell_scan(x_rnn, W_router, W_kv, W_beta, b_beta, W_q):
            Tt, batch, D = x_rnn.shape
            n, nb = (N_STATE, N_BLOCKS)
            xf = x_rnn.reshape(Tt * batch, D)
            logits = (xf @ W_router.T).reshape(Tt, batch, nb) / ROUTER_TEMP
            kv = (xf @ W_kv.T).reshape(Tt, batch, nb, 2, n)
            beta = jax.nn.sigmoid((xf @ W_beta.T).reshape(Tt, batch, nb, n) + b_beta)
            q = (xf @ W_q.T).reshape(Tt, batch, n)
            S0 = jnp.zeros((batch, nb, n, n), x_rnn.dtype)
            rows = jnp.arange(batch)[:, None]

            def step(S, inp):
                logits_t, k_t, v_t, beta_t, q_t = inp
                _, idx = jax.lax.top_k(logits_t, TOP_K)
                mask = jnp.zeros_like(logits_t).at[rows, idx].set(1.0)
                sm = jax.nn.softmax(logits_t, axis=-1)
                uw = mask * sm
                uw = uw / (uw.sum(-1, keepdims=True) + 1e-08)
                kn = k_t / (jnp.linalg.norm(k_t, axis=-1, keepdims=True) + 1e-06)
                retrieved = jnp.einsum('bnij,bnj->bni', S, kn)
                delta = v_t - retrieved
                outer = delta[..., :, None] * kn[..., None, :]
                S_upd = jnp.tanh(beta_t[..., None] * S + outer)
                w = uw[..., None, None]
                S_new = (1.0 - w) * S + w * S_upd
                Sq = jnp.einsum('bnij,bj->bni', S_new, q_t)
                block_out = Sq * (Sq * jax.nn.sigmoid(Sq))
                out_t = jnp.einsum('bn,bnd->bd', sm, block_out)
                return (S_new, out_t)
            S_final, outs = jax.lax.scan(step, S0, (logits, kv[..., 0, :], kv[..., 1, :], beta, q))
            return (outs, S_final)

        def _reference_tuple_inner(x, W_in, W_router, W_kv, W_beta, b_beta, W_q, W_out):
            x_proj = jax.nn.silu(x @ W_in.T)
            x_rnn = jnp.transpose(x_proj, (1, 0, 2))
            cell_out, S_final = _cell_scan(x_rnn, W_router, W_kv, W_beta, b_beta, W_q)
            y = jnp.transpose(cell_out, (1, 0, 2)) @ W_out.T
            return (y, S_final)
        key = jax.random.key(seed)
        ks = jax.random.split(key, 7)
        x = jax.random.normal(ks[0], (BATCH, T, DIM), jnp.float32)
        W_in = _xavier(ks[1], (D_INNER, DIM))
        W_router = _xavier(ks[2], (N_BLOCKS, D_INNER))
        W_kv = _xavier(ks[3], (N_BLOCKS * 2 * N_STATE, D_INNER))
        W_beta = _xavier(ks[4], (N_BLOCKS * N_STATE, D_INNER))
        b_beta = jnp.full((N_BLOCKS, N_STATE), INIT_BETA_BIAS, jnp.float32)
        W_q = _xavier(ks[5], (N_STATE, D_INNER))
        W_out = _xavier(ks[6], (DIM, N_STATE))
        return {'x': x, 'W_in': W_in, 'W_router': W_router, 'W_kv': W_kv, 'W_beta': W_beta, 'b_beta': b_beta, 'W_q': W_q, 'W_out': W_out}
    _L0_attn_a_in = _L0_attn_a_setup()

    def _L0_attn_b_setup():
        import jax, jax.numpy as jnp
        import numpy as np
        B, S, D, H, NB = (2, 256, 128, 16, 32)
        DH = D // H
        MLP = 512
        CLUSTER_SCORE = 0.1
        LN_EPS = 1e-06

        def _layernorm(x, g, b):
            mu = jnp.mean(x, axis=-1, keepdims=True)
            var = jnp.mean(jnp.square(x - mu), axis=-1, keepdims=True)
            return (x - mu) * jax.lax.rsqrt(var + LN_EPS) * g + b

        def _lha_attention(x, Wq, Wk, Wv, Whq, Whk, Wo):
            q = jnp.einsum('bsd,dhf->bshf', x, Wq)
            k = jnp.einsum('bsd,dhf->bshf', x, Wk)
            v = jnp.einsum('bsd,dhf->bshf', x, Wv)
            qb = jax.nn.softmax(jnp.einsum('bshf,hfn->bshn', q, Whq), axis=-1)
            kb = jax.nn.softmax(jnp.einsum('bshf,hfn->bshn', k, Whk), axis=-1)
            logits = jnp.einsum('bqhf,bkhf->bhqk', q, k) / jnp.sqrt(jnp.float32(DH))
            aff = jnp.einsum('bqhn,bkhn->bhqk', qb, kb)
            logits = logits + CLUSTER_SCORE * aff
            attn = jax.nn.softmax(logits, axis=-1)
            out = jnp.einsum('bhqk,bkhf->bqhf', attn, v)
            out = jnp.einsum('bqhf,hfd->bqd', out, Wo)
            mq = jnp.mean(qb, axis=(0, 1))
            mk = jnp.mean(kb, axis=(0, 1))
            extra_loss = 0.5 * NB * (jnp.mean(jnp.sum(mq * mq, -1)) + jnp.mean(jnp.sum(mk * mk, -1)))
            return (out, extra_loss)

        def _reference_tuple_inner(inputs, ln1_g, ln1_b, Wq, Wk, Wv, Whq, Whk, Wo, ln2_g, ln2_b, W1, b1, W2, b2):
            x = _layernorm(inputs, ln1_g, ln1_b)
            attn_out, extra_loss = _lha_attention(x, Wq, Wk, Wv, Whq, Whk, Wo)
            x = attn_out + inputs
            y = _layernorm(x, ln2_g, ln2_b)
            y = jax.nn.relu(jnp.einsum('bsd,dm->bsm', y, W1) + b1)
            y = jnp.einsum('bsm,md->bsd', y, W2) + b2
            return (x + y, extra_loss)
        key = jax.random.key(seed)
        ks = jax.random.split(key, 10)
        std = 0.02
        return {'inputs': jax.random.normal(ks[0], (B, S, D), jnp.float32), 'ln1_g': jnp.ones((D,), jnp.float32), 'ln1_b': jnp.zeros((D,), jnp.float32), 'Wq': jax.random.normal(ks[1], (D, H, DH), jnp.float32) * std, 'Wk': jax.random.normal(ks[2], (D, H, DH), jnp.float32) * std, 'Wv': jax.random.normal(ks[3], (D, H, DH), jnp.float32) * std, 'Whq': jax.random.normal(ks[4], (H, DH, NB), jnp.float32) * std, 'Whk': jax.random.normal(ks[5], (H, DH, NB), jnp.float32) * std, 'Wo': jax.random.normal(ks[6], (H, DH, D), jnp.float32) * std, 'ln2_g': jnp.ones((D,), jnp.float32), 'ln2_b': jnp.zeros((D,), jnp.float32), 'W1': jax.random.normal(ks[7], (D, MLP), jnp.float32) * std, 'b1': jnp.zeros((MLP,), jnp.float32), 'W2': jax.random.normal(ks[8], (MLP, D), jnp.float32) * std, 'b2': jnp.zeros((D,), jnp.float32)}
    _L0_attn_b_in = _L0_attn_b_setup()

    def _L0_ffn_setup():
        import jax, jax.numpy as jnp
        import numpy as np
        B, S, H, F, G = (8, 256, 128, 512, 128)
        EPS = 1e-05

        def _dequant(q, scales, g):
            K, N = q.shape
            w = (q.astype(jnp.float32) - 128.0).reshape(K // g, g, N) * scales[:, None, :]
            return w.reshape(K, N)
        key = jax.random.key(seed)
        ks = jax.random.split(key, 8)
        x = jax.random.normal(ks[0], (B, S, H), dtype=jnp.float32)
        ln_gamma = jnp.ones((H,), jnp.float32)
        ln_beta = jnp.zeros((H,), jnp.float32)
        fc1_q = jax.random.randint(ks[1], (H, F), 0, 32, dtype=jnp.int32)
        fc2_q = jax.random.randint(ks[2], (F, H), 0, 32, dtype=jnp.int32)
        fc1_scales = jax.random.uniform(ks[3], (H // G, F), jnp.float32) * 0.02 + 0.001
        fc2_scales = jax.random.uniform(ks[4], (F // G, H), jnp.float32) * 0.02 + 0.001
        fc1_bias = jax.random.normal(ks[5], (F,), jnp.float32) * 0.02
        fc2_bias = jax.random.normal(ks[6], (H,), jnp.float32) * 0.02
        return {'x': x, 'ln_gamma': ln_gamma, 'ln_beta': ln_beta, 'fc1_q': fc1_q, 'fc1_scales': fc1_scales, 'fc1_bias': fc1_bias, 'fc2_q': fc2_q, 'fc2_scales': fc2_scales, 'fc2_bias': fc2_bias}
    _L0_ffn_in = _L0_ffn_setup()

    def _L1_attn_a_setup():
        import jax, jax.numpy as jnp
        import numpy as np
        SL, BS, E, H, PF, STRIDE, SHIFT = (256, 2, 128, 16, 16, 1, 0)
        DH = E // H

        def _layernorm(x, g, b, eps=1e-05):
            m = x.mean(-1, keepdims=True)
            v = jnp.var(x, axis=-1, keepdims=True)
            return (x - m) * jax.lax.rsqrt(v + eps) * g + b

        def _sparsify(context, h):
            c = context.shape[0]
            base = (jnp.arange(h) + 1) * STRIDE - PF + SHIFT
            idx = (base[None, :] + jnp.arange(PF)[:, None]) % c
            return context[idx.reshape(-1)].reshape(PF, h, context.shape[1], context.shape[2])
        key = jax.random.key(seed)
        ks = jax.random.split(key, 6)
        s = 0.02
        return {'x': jax.random.normal(ks[0], (SL, BS, E), jnp.float32), 'ln_g': jnp.ones((E,), jnp.float32), 'ln_b': jnp.zeros((E,), jnp.float32), 'Wq': jax.random.normal(ks[1], (E, E), jnp.float32) * s, 'bq': jnp.zeros((E,), jnp.float32), 'Wk': jax.random.normal(ks[2], (E, E), jnp.float32) * s, 'bk': jnp.zeros((E,), jnp.float32), 'Wv': jax.random.normal(ks[3], (E, E), jnp.float32) * s, 'bv': jnp.zeros((E,), jnp.float32), 'Wo': jax.random.normal(ks[4], (E, E), jnp.float32) * s, 'bo': jnp.zeros((E,), jnp.float32)}
    _L1_attn_a_in = _L1_attn_a_setup()

    def _L1_attn_b_setup():
        import jax, jax.numpy as jnp
        import numpy as np
        N_HEADS = 16

        def _rope_cos_sin(hs, T, dtype):
            t = jnp.arange(1, T + 1, dtype=dtype)[:, None]
            i = jnp.arange(hs // 2, dtype=dtype)
            theta = (1.0 / 10000.0) ** (2.0 * i / hs)
            ang = t * theta
            return (jnp.cos(ang), jnp.sin(ang))

        def _apply_rope(u, cos, sin):
            ue = u[..., ::2]
            uo = u[..., 1::2]
            real = cos * ue - sin * uo
            out = jnp.stack([real, jnp.zeros_like(real)], axis=-1)
            return out.reshape(u.shape)
        key = jax.random.key(seed)
        ks = jax.random.split(key, 6)
        B, T, H = (2, 256, 128)
        scale = 0.02
        return {'x': jax.random.normal(ks[0], (B, T, H), dtype=jnp.float32), 'Wq': jax.random.normal(ks[1], (H, H), dtype=jnp.float32) * scale, 'bq': jnp.zeros((H,), dtype=jnp.float32), 'Wk': jax.random.normal(ks[2], (H, H), dtype=jnp.float32) * scale, 'bk': jnp.zeros((H,), dtype=jnp.float32), 'Wv': jax.random.normal(ks[3], (H, H), dtype=jnp.float32) * scale, 'bv': jnp.zeros((H,), dtype=jnp.float32), 'Wo': jax.random.normal(ks[4], (H, H), dtype=jnp.float32) * scale, 'bo': jnp.zeros((H,), dtype=jnp.float32)}
    _L1_attn_b_in = _L1_attn_b_setup()

    def _L1_ffn_setup():
        import jax, jax.numpy as jnp
        import numpy as np
        CAP_FACTOR = 1.5
        key = jax.random.key(seed)
        ks = jax.random.split(key, 6)
        E, S, D, M = (48, 4, 128, 128)
        K = D // S
        x = jax.random.normal(ks[0], (4, 512, D), dtype=jnp.float32)
        Wr = jax.random.normal(ks[1], (E, D), dtype=jnp.float32) * 0.02
        W1 = jax.random.normal(ks[2], (E, S, D, M), dtype=jnp.float32) * (1.0 / np.sqrt(D))
        b1 = jnp.zeros((E, S, M), dtype=jnp.float32)
        W2 = jax.random.normal(ks[3], (E, S, M, K), dtype=jnp.float32) * (1.0 / np.sqrt(M))
        b2 = jnp.zeros((E, S, K), dtype=jnp.float32)
        return {'x': x, 'Wr': Wr, 'W1': W1, 'b1': b1, 'W2': W2, 'b2': b2}
    _L1_ffn_in = _L1_ffn_setup()
    _d = {'L0_attn_a_x': _L0_attn_a_in['x'], 'L0_attn_a_W_in': _L0_attn_a_in['W_in'], 'L0_attn_a_W_router': _L0_attn_a_in['W_router'], 'L0_attn_a_W_kv': _L0_attn_a_in['W_kv'], 'L0_attn_a_W_beta': _L0_attn_a_in['W_beta'], 'L0_attn_a_b_beta': _L0_attn_a_in['b_beta'], 'L0_attn_a_W_q': _L0_attn_a_in['W_q'], 'L0_attn_a_W_out': _L0_attn_a_in['W_out'], 'L0_attn_b_ln1_g': _L0_attn_b_in['ln1_g'], 'L0_attn_b_ln1_b': _L0_attn_b_in['ln1_b'], 'L0_attn_b_Wq': _L0_attn_b_in['Wq'], 'L0_attn_b_Wk': _L0_attn_b_in['Wk'], 'L0_attn_b_Wv': _L0_attn_b_in['Wv'], 'L0_attn_b_Whq': _L0_attn_b_in['Whq'], 'L0_attn_b_Whk': _L0_attn_b_in['Whk'], 'L0_attn_b_Wo': _L0_attn_b_in['Wo'], 'L0_attn_b_ln2_g': _L0_attn_b_in['ln2_g'], 'L0_attn_b_ln2_b': _L0_attn_b_in['ln2_b'], 'L0_attn_b_W1': _L0_attn_b_in['W1'], 'L0_attn_b_b1': _L0_attn_b_in['b1'], 'L0_attn_b_W2': _L0_attn_b_in['W2'], 'L0_attn_b_b2': _L0_attn_b_in['b2'], 'L0_ffn_ln_gamma': _L0_ffn_in['ln_gamma'], 'L0_ffn_ln_beta': _L0_ffn_in['ln_beta'], 'L0_ffn_fc1_q': _L0_ffn_in['fc1_q'], 'L0_ffn_fc1_scales': _L0_ffn_in['fc1_scales'], 'L0_ffn_fc1_bias': _L0_ffn_in['fc1_bias'], 'L0_ffn_fc2_q': _L0_ffn_in['fc2_q'], 'L0_ffn_fc2_scales': _L0_ffn_in['fc2_scales'], 'L0_ffn_fc2_bias': _L0_ffn_in['fc2_bias'], 'L1_attn_a_ln_g': _L1_attn_a_in['ln_g'], 'L1_attn_a_ln_b': _L1_attn_a_in['ln_b'], 'L1_attn_a_Wq': _L1_attn_a_in['Wq'], 'L1_attn_a_bq': _L1_attn_a_in['bq'], 'L1_attn_a_Wk': _L1_attn_a_in['Wk'], 'L1_attn_a_bk': _L1_attn_a_in['bk'], 'L1_attn_a_Wv': _L1_attn_a_in['Wv'], 'L1_attn_a_bv': _L1_attn_a_in['bv'], 'L1_attn_a_Wo': _L1_attn_a_in['Wo'], 'L1_attn_a_bo': _L1_attn_a_in['bo'], 'L1_attn_b_Wq': _L1_attn_b_in['Wq'], 'L1_attn_b_bq': _L1_attn_b_in['bq'], 'L1_attn_b_Wk': _L1_attn_b_in['Wk'], 'L1_attn_b_bk': _L1_attn_b_in['bk'], 'L1_attn_b_Wv': _L1_attn_b_in['Wv'], 'L1_attn_b_bv': _L1_attn_b_in['bv'], 'L1_attn_b_Wo': _L1_attn_b_in['Wo'], 'L1_attn_b_bo': _L1_attn_b_in['bo'], 'L1_ffn_Wr': _L1_ffn_in['Wr'], 'L1_ffn_W1': _L1_ffn_in['W1'], 'L1_ffn_b1': _L1_ffn_in['b1'], 'L1_ffn_W2': _L1_ffn_in['W2'], 'L1_ffn_b2': _L1_ffn_in['b2']}
    _x0 = _d['L0_attn_a_x']
    _d['L0_attn_a_x'] = jax.random.normal(jax.random.fold_in(jax.random.key(seed), 1), (16, 256, 128), dtype=_x0.dtype)
    del _x0
    return _d

def reference(L0_attn_a_x, L0_attn_a_W_in, L0_attn_a_W_router, L0_attn_a_W_kv, L0_attn_a_W_beta, L0_attn_a_b_beta, L0_attn_a_W_q, L0_attn_a_W_out, L0_attn_b_ln1_g, L0_attn_b_ln1_b, L0_attn_b_Wq, L0_attn_b_Wk, L0_attn_b_Wv, L0_attn_b_Whq, L0_attn_b_Whk, L0_attn_b_Wo, L0_attn_b_ln2_g, L0_attn_b_ln2_b, L0_attn_b_W1, L0_attn_b_b1, L0_attn_b_W2, L0_attn_b_b2, L0_ffn_ln_gamma, L0_ffn_ln_beta, L0_ffn_fc1_q, L0_ffn_fc1_scales, L0_ffn_fc1_bias, L0_ffn_fc2_q, L0_ffn_fc2_scales, L0_ffn_fc2_bias, L1_attn_a_ln_g, L1_attn_a_ln_b, L1_attn_a_Wq, L1_attn_a_bq, L1_attn_a_Wk, L1_attn_a_bk, L1_attn_a_Wv, L1_attn_a_bv, L1_attn_a_Wo, L1_attn_a_bo, L1_attn_b_Wq, L1_attn_b_bq, L1_attn_b_Wk, L1_attn_b_bk, L1_attn_b_Wv, L1_attn_b_bv, L1_attn_b_Wo, L1_attn_b_bo, L1_ffn_Wr, L1_ffn_W1, L1_ffn_b1, L1_ffn_W2, L1_ffn_b2):

    def _L0_attn_a_ref(x, W_in, W_router, W_kv, W_beta, b_beta, W_q, W_out):
        import jax, jax.numpy as jnp
        import numpy as np
        DIM = 128
        D_INNER = 128
        N_STATE = 32
        N_BLOCKS = 4
        TOP_K = 2
        ROUTER_TEMP = 1.0
        INIT_BETA_BIAS = 2.0
        BATCH = 16
        T = 256

        def _xavier(key, shape):
            fan_out, fan_in = shape
            lim = jnp.sqrt(6.0 / (fan_in + fan_out))
            return jax.random.uniform(key, shape, jnp.float32, -lim, lim)

        def _cell_scan(x_rnn, W_router, W_kv, W_beta, b_beta, W_q):
            Tt, batch, D = x_rnn.shape
            n, nb = (N_STATE, N_BLOCKS)
            xf = x_rnn.reshape(Tt * batch, D)
            logits = (xf @ W_router.T).reshape(Tt, batch, nb) / ROUTER_TEMP
            kv = (xf @ W_kv.T).reshape(Tt, batch, nb, 2, n)
            beta = jax.nn.sigmoid((xf @ W_beta.T).reshape(Tt, batch, nb, n) + b_beta)
            q = (xf @ W_q.T).reshape(Tt, batch, n)
            S0 = jnp.zeros((batch, nb, n, n), x_rnn.dtype)
            rows = jnp.arange(batch)[:, None]

            def step(S, inp):
                logits_t, k_t, v_t, beta_t, q_t = inp
                _, idx = jax.lax.top_k(logits_t, TOP_K)
                mask = jnp.zeros_like(logits_t).at[rows, idx].set(1.0)
                sm = jax.nn.softmax(logits_t, axis=-1)
                uw = mask * sm
                uw = uw / (uw.sum(-1, keepdims=True) + 1e-08)
                kn = k_t / (jnp.linalg.norm(k_t, axis=-1, keepdims=True) + 1e-06)
                retrieved = jnp.einsum('bnij,bnj->bni', S, kn)
                delta = v_t - retrieved
                outer = delta[..., :, None] * kn[..., None, :]
                S_upd = jnp.tanh(beta_t[..., None] * S + outer)
                w = uw[..., None, None]
                S_new = (1.0 - w) * S + w * S_upd
                Sq = jnp.einsum('bnij,bj->bni', S_new, q_t)
                block_out = Sq * (Sq * jax.nn.sigmoid(Sq))
                out_t = jnp.einsum('bn,bnd->bd', sm, block_out)
                return (S_new, out_t)
            S_final, outs = jax.lax.scan(step, S0, (logits, kv[..., 0, :], kv[..., 1, :], beta, q))
            return (outs, S_final)

        def _reference_tuple_inner(x, W_in, W_router, W_kv, W_beta, b_beta, W_q, W_out):
            x_proj = jax.nn.silu(x @ W_in.T)
            x_rnn = jnp.transpose(x_proj, (1, 0, 2))
            cell_out, S_final = _cell_scan(x_rnn, W_router, W_kv, W_beta, b_beta, W_q)
            y = jnp.transpose(cell_out, (1, 0, 2)) @ W_out.T
            return (y, S_final)
        return _reference_tuple_inner(x, W_in, W_router, W_kv, W_beta, b_beta, W_q, W_out)[0]

    def _L0_attn_b_ref(inputs, ln1_g, ln1_b, Wq, Wk, Wv, Whq, Whk, Wo, ln2_g, ln2_b, W1, b1, W2, b2):
        import jax, jax.numpy as jnp
        import numpy as np
        B, S, D, H, NB = (2, 256, 128, 16, 32)
        DH = D // H
        MLP = 512
        CLUSTER_SCORE = 0.1
        LN_EPS = 1e-06

        def _layernorm(x, g, b):
            mu = jnp.mean(x, axis=-1, keepdims=True)
            var = jnp.mean(jnp.square(x - mu), axis=-1, keepdims=True)
            return (x - mu) * jax.lax.rsqrt(var + LN_EPS) * g + b

        def _lha_attention(x, Wq, Wk, Wv, Whq, Whk, Wo):
            q = jnp.einsum('bsd,dhf->bshf', x, Wq)
            k = jnp.einsum('bsd,dhf->bshf', x, Wk)
            v = jnp.einsum('bsd,dhf->bshf', x, Wv)
            qb = jax.nn.softmax(jnp.einsum('bshf,hfn->bshn', q, Whq), axis=-1)
            kb = jax.nn.softmax(jnp.einsum('bshf,hfn->bshn', k, Whk), axis=-1)
            logits = jnp.einsum('bqhf,bkhf->bhqk', q, k) / jnp.sqrt(jnp.float32(DH))
            aff = jnp.einsum('bqhn,bkhn->bhqk', qb, kb)
            logits = logits + CLUSTER_SCORE * aff
            attn = jax.nn.softmax(logits, axis=-1)
            out = jnp.einsum('bhqk,bkhf->bqhf', attn, v)
            out = jnp.einsum('bqhf,hfd->bqd', out, Wo)
            mq = jnp.mean(qb, axis=(0, 1))
            mk = jnp.mean(kb, axis=(0, 1))
            extra_loss = 0.5 * NB * (jnp.mean(jnp.sum(mq * mq, -1)) + jnp.mean(jnp.sum(mk * mk, -1)))
            return (out, extra_loss)

        def _reference_tuple_inner(inputs, ln1_g, ln1_b, Wq, Wk, Wv, Whq, Whk, Wo, ln2_g, ln2_b, W1, b1, W2, b2):
            x = _layernorm(inputs, ln1_g, ln1_b)
            attn_out, extra_loss = _lha_attention(x, Wq, Wk, Wv, Whq, Whk, Wo)
            x = attn_out + inputs
            y = _layernorm(x, ln2_g, ln2_b)
            y = jax.nn.relu(jnp.einsum('bsd,dm->bsm', y, W1) + b1)
            y = jnp.einsum('bsm,md->bsd', y, W2) + b2
            return (x + y, extra_loss)
        return _reference_tuple_inner(inputs, ln1_g, ln1_b, Wq, Wk, Wv, Whq, Whk, Wo, ln2_g, ln2_b, W1, b1, W2, b2)[0]

    def _L0_ffn_ref(x, ln_gamma, ln_beta, fc1_q, fc1_scales, fc1_bias, fc2_q, fc2_scales, fc2_bias):
        import jax, jax.numpy as jnp
        import numpy as np
        B, S, H, F, G = (8, 256, 128, 512, 128)
        EPS = 1e-05

        def _dequant(q, scales, g):
            K, N = q.shape
            w = (q.astype(jnp.float32) - 128.0).reshape(K // g, g, N) * scales[:, None, :]
            return w.reshape(K, N)
        residual = x
        mu = jnp.mean(x, axis=-1, keepdims=True)
        var = jnp.mean(jnp.square(x - mu), axis=-1, keepdims=True)
        h = (x - mu) * jax.lax.rsqrt(var + EPS) * ln_gamma + ln_beta
        hf = h.reshape(-1, H)
        w1 = _dequant(fc1_q, fc1_scales, G)
        y = hf @ w1 + fc1_bias
        y = jax.nn.silu(y)
        w2 = _dequant(fc2_q, fc2_scales, G)
        z = y @ w2 + fc2_bias
        return residual + 0.5 * z.reshape(residual.shape)

    def _L1_attn_a_ref(x, ln_g, ln_b, Wq, bq, Wk, bk, Wv, bv, Wo, bo):
        import jax, jax.numpy as jnp
        import numpy as np
        SL, BS, E, H, PF, STRIDE, SHIFT = (256, 2, 128, 16, 16, 1, 0)
        DH = E // H

        def _layernorm(x, g, b, eps=1e-05):
            m = x.mean(-1, keepdims=True)
            v = jnp.var(x, axis=-1, keepdims=True)
            return (x - m) * jax.lax.rsqrt(v + eps) * g + b

        def _sparsify(context, h):
            c = context.shape[0]
            base = (jnp.arange(h) + 1) * STRIDE - PF + SHIFT
            idx = (base[None, :] + jnp.arange(PF)[:, None]) % c
            return context[idx.reshape(-1)].reshape(PF, h, context.shape[1], context.shape[2])
        sl, bs, e = x.shape
        residual = x
        xn = _layernorm(x, ln_g, ln_b)
        fetch = _sparsify(xn, sl)
        q = (xn @ Wq + bq).reshape(sl, bs, H, DH)
        k = (fetch @ Wk + bk).reshape(PF, sl, bs, H, DH)
        v = (fetch @ Wv + bv).reshape(PF, sl, bs, H, DH)
        scale = 1.0 / jnp.sqrt(jnp.float32(DH))
        scores = jnp.einsum('sbhd,psbhd->sbhp', q, k) * scale
        attn = jax.nn.softmax(scores, axis=-1)
        out = jnp.einsum('sbhp,psbhd->sbhd', attn, v).reshape(sl, bs, e)
        out = out @ Wo + bo
        return residual + out

    def _L1_attn_b_ref(x, Wq, bq, Wk, bk, Wv, bv, Wo, bo):
        import jax, jax.numpy as jnp
        import numpy as np
        N_HEADS = 16

        def _rope_cos_sin(hs, T, dtype):
            t = jnp.arange(1, T + 1, dtype=dtype)[:, None]
            i = jnp.arange(hs // 2, dtype=dtype)
            theta = (1.0 / 10000.0) ** (2.0 * i / hs)
            ang = t * theta
            return (jnp.cos(ang), jnp.sin(ang))

        def _apply_rope(u, cos, sin):
            ue = u[..., ::2]
            uo = u[..., 1::2]
            real = cos * ue - sin * uo
            out = jnp.stack([real, jnp.zeros_like(real)], axis=-1)
            return out.reshape(u.shape)
        B, T, H = x.shape
        nh = N_HEADS
        hs = H // nh

        def proj(W, b):
            y = jnp.einsum('bth,oh->bto', x, W) + b
            return y.reshape(B, T, nh, hs).transpose(0, 2, 1, 3)
        Q = proj(Wq, bq)
        K = proj(Wk, bk)
        V = proj(Wv, bv)
        cos, sin = _rope_cos_sin(hs, T, x.dtype)
        Q = _apply_rope(Q, cos, sin)
        K = _apply_rope(K, cos, sin)
        scores = jnp.einsum('bhqd,bhkd->bhqk', Q, K) * (1.0 / jnp.sqrt(jnp.asarray(hs, x.dtype)))
        causal = jnp.tril(jnp.ones((T, T), dtype=bool))
        scores = jnp.where(causal, scores, jnp.asarray(-10000000000.0, x.dtype))
        att = jax.nn.softmax(scores, axis=-1)
        y = jnp.einsum('bhqk,bhkd->bhqd', att, V)
        y = y.transpose(0, 2, 1, 3).reshape(B, T, H)
        return jnp.einsum('bth,oh->bto', y, Wo) + bo

    def _L1_ffn_ref(x, Wr, W1, b1, W2, b2):
        import jax, jax.numpy as jnp
        import numpy as np
        CAP_FACTOR = 1.5
        orig_shape = x.shape
        D = x.shape[-1]
        E = Wr.shape[0]
        xf = x.reshape(-1, D)
        T = xf.shape[0]
        cap = int(CAP_FACTOR * T / E)
        logits = xf @ Wr.T
        vals, idx = jax.lax.top_k(logits.T, cap)
        w = jax.nn.softmax(vals, axis=-1)
        xg = xf[idx]
        h = jax.nn.gelu(jnp.einsum('ecd,esdm->ecsm', xg, W1) + b1[:, None], approximate=False)
        y = jnp.einsum('ecsm,esmk->ecsk', h, W2) + b2[:, None]
        y = y.reshape(E, cap, D) * w[..., None]
        out = jnp.zeros_like(xf).at[idx.reshape(-1)].add(y.reshape(-1, D))
        return out.reshape(orig_shape)
    x = L0_attn_a_x
    x = x + _L0_attn_a_ref(_layernorm(x, axis=-1), L0_attn_a_W_in, L0_attn_a_W_router, L0_attn_a_W_kv, L0_attn_a_W_beta, L0_attn_a_b_beta, L0_attn_a_W_q, L0_attn_a_W_out)
    x = x + _L0_ffn_ref(_layernorm(x, axis=-1), L0_ffn_ln_gamma, L0_ffn_ln_beta, L0_ffn_fc1_q, L0_ffn_fc1_scales, L0_ffn_fc1_bias, L0_ffn_fc2_q, L0_ffn_fc2_scales, L0_ffn_fc2_bias)
    x = x + _L0_attn_b_ref(_layernorm(x, axis=-1), L0_attn_b_ln1_g, L0_attn_b_ln1_b, L0_attn_b_Wq, L0_attn_b_Wk, L0_attn_b_Wv, L0_attn_b_Whq, L0_attn_b_Whk, L0_attn_b_Wo, L0_attn_b_ln2_g, L0_attn_b_ln2_b, L0_attn_b_W1, L0_attn_b_b1, L0_attn_b_W2, L0_attn_b_b2)
    x = x + _L0_ffn_ref(_layernorm(x, axis=-1), L0_ffn_ln_gamma, L0_ffn_ln_beta, L0_ffn_fc1_q, L0_ffn_fc1_scales, L0_ffn_fc1_bias, L0_ffn_fc2_q, L0_ffn_fc2_scales, L0_ffn_fc2_bias)
    x = x + _L1_attn_a_ref(_layernorm(x, axis=-1), L1_attn_a_ln_g, L1_attn_a_ln_b, L1_attn_a_Wq, L1_attn_a_bq, L1_attn_a_Wk, L1_attn_a_bk, L1_attn_a_Wv, L1_attn_a_bv, L1_attn_a_Wo, L1_attn_a_bo)
    x = x + _L1_ffn_ref(_layernorm(x, axis=-1), L1_ffn_Wr, L1_ffn_W1, L1_ffn_b1, L1_ffn_W2, L1_ffn_b2)
    x = x + _L1_attn_b_ref(_layernorm(x, axis=-1), L1_attn_b_Wq, L1_attn_b_bq, L1_attn_b_Wk, L1_attn_b_bk, L1_attn_b_Wv, L1_attn_b_bv, L1_attn_b_Wo, L1_attn_b_bo)
    x = x + _L1_ffn_ref(_layernorm(x, axis=-1), L1_ffn_Wr, L1_ffn_W1, L1_ffn_b1, L1_ffn_W2, L1_ffn_b2)
    return x

_drawn_inputs = setup_inputs


def setup_inputs(seed=0):
    import zlib

    import numpy as np

    out = dict(_drawn_inputs(seed))
    spreads = {'L0_attn_a_b_beta': (2.0, 0.2),
     'L0_attn_b_ln1_g': (1.0, 0.6),
     'L0_attn_b_ln1_b': (0.0, 0.8),
     'L0_attn_b_ln2_g': (1.0, 0.6),
     'L0_attn_b_ln2_b': (0.0, 0.8),
     'L0_attn_b_b1': (0.0, 0.8),
     'L0_attn_b_b2': (0.0, 2.0),
     'L0_ffn_ln_gamma': (1.0, 0.2),
     'L0_ffn_ln_beta': (0.0, 0.1),
     'L1_attn_a_ln_g': (1.0, 0.6),
     'L1_attn_a_ln_b': (0.0, 2.0),
     'L1_attn_a_bq': (0.0, 2.0),
     'L1_attn_a_bk': (0.0, 0.8),
     'L1_attn_a_bv': (0.0, 2.0),
     'L1_attn_a_bo': (0.0, 2.0),
     'L1_attn_b_bq': (0.0, 2.0),
     'L1_attn_b_bk': (0.0, 2.0),
     'L1_attn_b_bv': (0.0, 2.0),
     'L1_attn_b_bo': (0.0, 2.0),
     'L1_ffn_b1': (0.0, 2.0),
     'L1_ffn_b2': (0.0, 2.0)}
    factors = {'L0_attn_b_Wq': 8.0,
     'L0_attn_b_Wk': 8.0,
     'L0_attn_b_Wv': 8.0,
     'L0_attn_b_Whq': 64.0,
     'L0_attn_b_Whk': 64.0,
     'L0_attn_b_Wo': 8.0,
     'L0_attn_b_W1': 8.0,
     'L0_attn_b_W2': 8.0,
     'L0_ffn_fc1_bias': 57.79,
     'L0_ffn_fc2_bias': 64.0,
     'L1_attn_a_Wq': 64.0,
     'L1_attn_a_Wk': 58.918,
     'L1_attn_a_Wv': 53.036,
     'L1_attn_a_Wo': 47.812,
     'L1_attn_b_Wq': 64.0,
     'L1_attn_b_Wk': 64.0,
     'L1_attn_b_Wv': 64.0,
     'L1_attn_b_Wo': 64.0,
     'L1_ffn_Wr': 64.0,
     'L1_ffn_W1': 64.0,
     'L1_ffn_W2': 64.0}
    for name, (base, spread) in spreads.items():
        noise = np.random.default_rng([zlib.crc32(name.encode()), seed]).standard_normal(out[name].shape)
        drawn = base * np.exp(spread * noise) if base else spread * noise
        out[name] = jnp.asarray(drawn.astype(out[name].dtype))
    for name, factor in factors.items():
        out[name] = (out[name] * factor).astype(out[name].dtype)
    return out
```

```python
from contextlib import ExitStack

import concourse.bass as bass
from concourse import mybir

F32 = mybir.dt.float32
I32 = mybir.dt.int32
U32 = mybir.dt.uint32
ALU = mybir.AluOpType
ACT = mybir.ActivationFunctionType
AX = mybir.AxisListType.X

P = 128
D = 128
B, T = 16, 256
NT = B * T // P
TPC = 4
NC = NT // TPC
CW = TPC * P
OUTER_EPS = 1e-5
NEG = -2.0 ** 100


class Chain:

    def __init__(self, eng, sem):
        self.eng, self.sem, self.base, self.k = eng, sem, 0, 0
        self.i, self.per = None, 0

    def loop(self, i, per):
        self.base, self.k, self.i, self.per = self.base + self.k, 0, i, per

    def end(self, trips):
        assert self.k == self.per, (self.k, self.per)
        self.base, self.k, self.i = self.base + trips * self.per, 0, None

    def value(self):
        if self.i is None:
            return self.base + self.k
        return self.i * self.per + (self.base + self.k)

    def __call__(self, ins):
        ins.then_inc(self.sem, 1)
        self.k += 1
        self.eng.wait_ge(self.sem, self.value())


class Stage:

    def __init__(self, nc, ctx, name):
        self.nc, self.ctx, self.name = nc, ctx, name

    def sb(self, name, shape, dt=F32):
        return self.ctx.enter_context(self.nc.sbuf_tensor(f"{self.name}_{name}", shape, dt))

    def ps(self, name, shape, dt=F32):
        return self.ctx.enter_context(self.nc.psum_tensor(f"{self.name}_{name}", shape, dt))

    def sem(self, name):
        return self.nc.alloc_semaphore(f"{self.name}_{name}")


class Norm:

    def __init__(self, st, inner_eps=None, eps=OUTER_EPS):
        self.inner_eps, self.eps = inner_eps, eps
        self.bn = st.sb("bn", [P, NT, 6])
        self.mean = st.sb("mean", [P, NT])
        self.var = st.sb("var", [P, NT])
        self.tmp = st.sb("normtmp", [P, NT])
        self.std = st.sb("std", [P, NT])
        self.rstd = st.sb("rstd", [P, NT])
        self.rboth = st.sb("rboth", [P, NT])
        self.var_ready = st.sem("var_ready")
        self.std_ready = st.sem("std_ready")

    def act(self, nc, act):
        for n in range(1 if self.inner_eps is None else 2):
            act.wait_ge(self.var_ready, n + 1)
            nc.scalar.activation(self.std[:], self.tmp[:], ACT.Sqrt).then_inc(self.std_ready, 1)

    def dve(self, nc, dve, chain, X):
        v = nc.vector
        with dve.Fori(0, NC) as i:
            chain.loop(i, 1)
            for j in range(TPC):
                last = v.bn_stats(self.bn[:, bass.ds(i * TPC + j, 1), :], X[:, bass.ds(i * TPC + j, 1), :])
            chain(last)
        chain.end(NC)
        bn = self.bn
        chain(v.tensor_tensor(self.mean[:], bn[:, :, 1], bn[:, :, 4], ALU.add))
        chain(v.tensor_scalar(self.mean[:], self.mean[:], 0.5, None, ALU.mult))
        chain(v.tensor_tensor(self.tmp[:], bn[:, :, 1], bn[:, :, 4], ALU.subtract))
        chain(v.tensor_tensor(self.tmp[:], self.tmp[:], self.tmp[:], ALU.mult))
        chain(v.tensor_tensor(self.var[:], bn[:, :, 2], bn[:, :, 5], ALU.add))
        chain(v.scalar_tensor_tensor(self.var[:], self.tmp[:], D / 4.0, self.var[:], ALU.mult, ALU.add))
        chain(v.tensor_scalar(self.var[:], self.var[:], 1.0 / D, None, ALU.mult))
        v.tensor_scalar(self.tmp[:], self.var[:], self.eps, None, ALU.add).then_inc(self.var_ready, 1)
        dve.wait_ge(self.std_ready, 1)
        chain(v.reciprocal(self.rstd[:], self.std[:]))
        if self.inner_eps is not None:
            chain(v.tensor_tensor(self.var[:], self.var[:], self.rstd[:], ALU.mult))
            chain(v.tensor_tensor(self.var[:], self.var[:], self.rstd[:], ALU.mult))
            v.tensor_scalar(self.tmp[:], self.var[:], self.inner_eps, None, ALU.add)\
                .then_inc(self.var_ready, 1)
            dve.wait_ge(self.std_ready, 2)
            chain(v.reciprocal(self.rboth[:], self.std[:]))
            chain(v.tensor_tensor(self.rboth[:], self.rboth[:], self.rstd[:], ALU.mult))


def bcast(ap, n):
    return ap.unsqueeze(2).to_broadcast([ap.shape[0], ap.shape[1], n])

STAGES = "afbfcmdm"


def normalise_loop(nc, pool, X, norm, tmp, xn, xn_free, xn_ready, res=None, res_free=None):
    g = nc.gpsimd
    r = norm.rstd if norm.inner_eps is None else norm.rboth
    step = Chain(pool, tmp[1])
    tmp = tmp[0]
    with pool.Fori(0, NC // 2) as i:
        step.loop(i, 2)
        for q in range(2):
            c = i * 2 + q
            tiles = bass.ds(c * TPC, TPC)
            pool.wait_ge(xn_free, c + 1)
            step(g.tensor_tensor(tmp[:, q], X[:, tiles, :], bcast(norm.mean[:, tiles], D), ALU.subtract))
            if res is not None:
                pool.wait_ge(res_free, c + 1)
                g.tensor_tensor(res[:, q], tmp[:, q], bcast(norm.rstd[:, tiles], D), ALU.mult)
            g.tensor_tensor(xn[:, q], tmp[:, q], bcast(r[:, tiles], D), ALU.mult).then_inc(xn_ready, 1)
    step.end(NC // 2)


AHEAD = 2


def give(eng, sem, n=AHEAD):
    for _ in range(n):
        eng.drain().then_inc(sem, 1)


def ffn_stage(nc, name, X, ident, a, XA=None):
    quantised = XA is None
    source = X if quantised else XA
    pre = "f_" if quantised else "b_mlp_"
    F = a[pre + "fc1"].shape[1]
    FM = F // P
    with nc.cleanup_on_exit(), ExitStack() as ctx:
        st = Stage(nc, ctx, name)
        norm = Norm(st, 1e-5) if quantised else Norm(st, None, 1e-6)
        w1q = st.sb("w1q", [P, F], I32)
        w1s = st.sb("w1s", [P, F])
        w1 = st.sb("w1", [P, F])
        w2q = st.sb("w2q", [P, FM, D], I32)
        w2s = st.sb("w2s", [P, FM, D])
        w2 = st.sb("w2", [P, FM, D])
        b1 = st.sb("b1", [P, FM])
        b2 = st.sb("b2", [P, D])
        gam = st.sb("gam", [P, 1])
        bet = st.sb("bet", [P, 1])
        tmp = st.sb("tmp", [P, 2, TPC, D])
        xn = st.sb("xn", [P, 2, TPC, D])
        res = st.sb("res", [P, 2, TPC, D])
        hT = st.sb("hT", [P, 2, CW])
        yT = st.sb("yT", [P, 2, FM, CW])
        upd = st.sb("upd", [P, TPC, D])
        psT = st.ps("psT", [P, CW])
        psA = st.ps("psA", [P, FM, CW])
        psZ = st.ps("psZ", [P, 2, TPC, D])
        loaded = st.sem("loaded")
        dve_step = st.sem("dve_step")
        pool_step = st.sem("pool_step")
        stats_done = st.sem("stats_done")
        weights_ready = st.sem("weights_ready")
        xn_ready, x_updated = st.sem("xn_ready"), st.sem("x_updated")
        xT_ready, h_ready = st.sem("xT_ready"), st.sem("h_ready")
        a_ready = st.sem("a_ready")
        y_ready = st.sem("y_ready")
        z_ready = st.sem("z_ready")
        LOADED = 16 * (8 if quantised else 6)
        with nc.Block() as block:

            @block.sync
            def _(sp):
                loads = [(b1[:], a[pre + "b1"]), (b2[:], a[pre + "b2"]), (gam[:], a[pre + "gam"]),
                         (bet[:], a[pre + "bet"])]
                w2_in = a[pre + "fc2"].rearrange("(m p) d -> p m d", p=P)
                if quantised:
                    loads += [(w1q[:], a["f_fc1"]), (w1s[:], a["f_fc1_s"]), (w2q[:], w2_in),
                              (w2s[:], a["f_fc2_s"])]
                else:
                    loads += [(w1[:], a[pre + "fc1"]), (w2[:], w2_in)]
                for dst, src in loads:
                    sp.dma_start(dst, src).then_inc(loaded, 16)

            @block.gpsimd
            def _(pool):
                pool.wait_ge(stats_done, 1)
                normalise_loop(nc, pool, source, norm, (tmp, pool_step), xn, xT_ready, xn_ready,
                               res if quantised else None, x_updated)

            @block.vector
            def _(dve):
                v = nc.vector
                step = Chain(dve, dve_step)
                give(dve, x_updated)
                norm.dve(nc, dve, step, source)
                give(dve, stats_done, 1)
                dve.wait_ge(loaded, LOADED)
                if quantised:
                    step(v.tensor_scalar(w1[:], w1q[:], -128.0, None, ALU.add))
                    v.tensor_tensor(w1[:], w1[:], w1s[:], ALU.mult)
                    step(v.tensor_scalar(w2[:], w2q[:], -128.0, None, ALU.add))
                    step(v.tensor_tensor(w2[:], w2[:], w2s[:], ALU.mult))
                    step(v.tensor_scalar(b2[:], b2[:], 0.5, None, ALU.mult))
                give(dve, weights_ready, 1)
                with dve.Fori(0, NC // 2) as i:
                    step.loop(i, 2)
                    for q in range(2):
                        c = i * 2 + q
                        tiles = bass.ds(c * TPC, TPC)
                        dve.wait_ge(z_ready, c + 1)
                        v.scalar_tensor_tensor(upd[:], psZ[:, q], 0.5 if quantised else 1.0,
                                               res[:, q] if quantised else XA[:, tiles, :], ALU.mult, ALU.add)
                        step(v.tensor_tensor(X[:, tiles, :], X[:, tiles, :],
                                             b2[:].unsqueeze(1).to_broadcast([P, TPC, D]), ALU.add))
                        v.tensor_tensor(X[:, tiles, :], X[:, tiles, :], upd[:], ALU.add).then_inc(x_updated, 1)
                        dve.wait_ge(x_updated, c + (1 + AHEAD))
                step.end(NC // 2)

            @block.scalar
            def _(act):
                norm.act(nc, act)
                act.wait_ge(loaded, LOADED)
                with act.Fori(0, NC // 2) as i:
                    for q in range(2):
                        c = i * 2 + q
                        act.wait_ge(xT_ready, c + (1 + AHEAD))
                        nc.scalar.activation(hT[:, q], psT[:], ACT.Identity, bias=bet[:], scale=gam[:])\
                            .then_inc(h_ready, 1)
                        for m in range(FM):
                            act.wait_ge(a_ready, c * FM + (m + 1))
                            nc.scalar.activation(yT[:, q, m], psA[:, m], ACT.Silu if quantised else ACT.Relu, bias=b1[:, m:m + 1])\
                                .then_inc(y_ready, 1)

            @block.tensor
            def _(pe):
                give(pe, xT_ready)
                pe.wait_ge(weights_ready, 1)
                with pe.Fori(0, NC // 2) as i:
                    for q in range(2):
                        c = i * 2 + q
                        pe.wait_ge(xn_ready, c + 1)
                        for j in range(TPC):
                            last = nc.tensor.transpose(psT[:, j * P:(j + 1) * P], xn[:, q, j], ident[:])
                        last.then_inc(xT_ready, 1)
                        pe.wait_ge(h_ready, c + 1)
                        for m in range(FM):
                            nc.tensor.matmul(psA[:, m], w1[:, m * P:(m + 1) * P], hT[:, q],
                                             start=True, stop=True).then_inc(a_ready, 1)
                        pe.wait_ge(y_ready, (c + 1) * FM)
                        pe.wait_ge(x_updated, c + 1)
                        for j in range(TPC):
                            for m in range(FM):
                                last = nc.tensor.matmul(psZ[:, q, j], yT[:, q, m, j * P:(j + 1) * P], w2[:, m],
                                                        start=(m == 0), stop=(m == FM - 1))
                        last.then_inc(z_ready, 1)


def transpose_chunk(nc, pe, psT, xn_q, ident):
    for j in range(TPC):
        last = nc.tensor.transpose(psT[:, j * P:(j + 1) * P], xn_q[:, j], ident[:])
    return last


def moe_stage(nc, name, X, ident, a, dest):
    E, S, _, M = a["m_w1"].shape
    K = D // S
    CAP = P
    assert 3 * B * T // 2 // E == CAP
    HALF = B * T // 2
    NB = 4
    H1 = 64
    R = H1 + E
    dest_tiles = dest.rearrange("(r p) d -> p r d", p=P)
    with ExitStack() as outer:
        so = Stage(nc, outer, name)
        xn_dram = nc.dram_tensor(f"{name}_xn", (B * T, D), F32, kind="Internal").ap()
        xn_tiles = xn_dram.rearrange("(r p) d -> p r d", p=P)
        tok = so.sb("tok", [P, E], U32)
        wgt = so.sb("wgt", [P, E])

        with nc.cleanup_on_exit(), ExitStack() as ctx:
            st = Stage(nc, ctx, name + "r")
            norm = Norm(st)
            tmp = st.sb("tmp", [P, 2, TPC, D])
            xn = st.sb("xn", [P, 2, TPC, D])
            xT = st.sb("xT", [P, 2, CW])
            wr = st.sb("wr", [P, E])
            score = st.sb("score", [R, HALF])
            best = st.sb("best", [R, CAP])
            at = st.sb("at", [R, CAP], U32)
            atf = st.sb("atf", [R, CAP])
            best1 = st.sb("best1", [E, CAP])
            at1 = st.sb("at1", [E, CAP])
            own = st.sb("own", [E, CAP])
            top = st.sb("top", [E, CAP])
            chosen = st.sb("chosen", [E, CAP])
            stat = st.sb("stat", [E, 4])
            psT = st.ps("psT", [P, 2, CW])
            psS = st.ps("psS", [P, 2, CW])
            psO = st.ps("psO", [P, 2, E])
            loaded, dve_step, pool_step = st.sem("loaded"), st.sem("dve_step"), st.sem("pool_step")
            stats_done, xn_ready, xn_kept = st.sem("stats_done"), st.sem("xn_ready"), [st.sem(f"xn_kept{q}") for q in range(2)]
            xT_ready, xT_copied, s_ready, s_copied = (st.sem("xT_ready"), st.sem("xT_copied"),
                                                      st.sem("s_ready"), st.sem("s_copied"))
            lists_ready, moved = st.sem("lists_ready"), st.sem("moved")
            top_ready, exp_ready, w_ready, out_ready = (st.sem("top_ready"), st.sem("exp_ready"),
                                                        st.sem("w_ready"), st.sem("out_ready"))
            with nc.Block() as block:

                @block.sync
                def _(sp):
                    sp.dma_start(wr[:], a["m_wr"]).then_inc(loaded, 16)
                    sp.dma_start(dest_tiles, X[:]).then_inc(loaded, 16)
                    sp.wait_ge(lists_ready, 1)
                    sp.dma_start(best1[:], best[H1:R, :]).then_inc(moved, 16)
                    sp.dma_start(at1[:], atf[H1:R, :]).then_inc(moved, 16)
                    sp.wait_ge(moved, 32)
                    sp.wait_ge(loaded, 32)

                @block.gpsimd
                def _(pool):
                    g = nc.gpsimd
                    pool.wait_ge(stats_done, 1)
                    step = Chain(pool, pool_step)
                    with pool.Fori(0, NC // 2) as i:
                        step.loop(i, 2)
                        for q in range(2):
                            c = i * 2 + q
                            tiles = bass.ds(c * TPC, TPC)
                            pool.wait_ge(xT_ready, c + 1)
                            pool.wait_ge(xn_kept[q], i * 16 + 16)
                            step(g.tensor_tensor(tmp[:, q], X[:, tiles, :], bcast(norm.mean[:, tiles], D),
                                                 ALU.subtract))
                            g.tensor_tensor(xn[:, q], tmp[:, q], bcast(norm.rstd[:, tiles], D), ALU.mult)\
                                .then_inc(xn_ready, 1)
                    step.end(NC // 2)

                @block.scalar
                def _(act):
                    norm.act(nc, act)
                    for q in range(2):
                        act.drain().then_inc(xn_kept[q], 16)
                    with act.Fori(0, NC // 2) as i:
                        for q in range(2):
                            c = i * 2 + q
                            act.wait_ge(xn_ready, c + 1)
                            act.dma_start(xn_tiles[:, bass.ds(c * TPC, TPC), :], xn[:, q])\
                                .then_inc(xn_kept[q], 16)
                            act.wait_ge(xT_ready, c + (1 + AHEAD))
                            nc.scalar.activation(xT[:, q], psT[:, q], ACT.Copy).then_inc(xT_copied, 1)
                    for q in range(2):
                        act.wait_ge(xn_kept[q], 16 * (NC // 2 + 1))
                    act.wait_ge(top_ready, 1)
                    nc.scalar.activation(own[:], top[:], ACT.Exp, bias=stat[:, 0:1],
                                         accum_out=stat[:, 1:2]).then_inc(exp_ready, 1)

                @block.vector
                def _(dve):
                    v = nc.vector
                    step = Chain(dve, dve_step)
                    norm.dve(nc, dve, step, X)
                    give(dve, stats_done, 1)
                    step(v.memset(score[:], 0.0))
                    for h in range(2):
                        with dve.Fori(0, NC // 4) as i:
                            step.loop(i, 2)
                            for q in range(2):
                                c = i * 2 + (q + h * NC // 2)
                                dve.wait_ge(s_ready, c + 1)
                                rows = slice(H1 * h, H1 * h + E)
                                step(v.tensor_copy(score[rows, bass.ds(i * (2 * CW) + q * CW, CW)],
                                                   psS[rows, q]))
                        step.end(NC // 4)
                    for k in range(CAP // 8):
                        eight = slice(8 * k, 8 * k + 8)
                        step(v.max(best[:, eight], score[:]))
                        step(v.max_index(at[:, eight], best[:, eight], score[:]))
                        step(v.match_replace(score[:], best[:, eight], score[:], -3.0e38))
                    step(v.tensor_copy(atf[:], at[:]))
                    step(v.tensor_scalar(atf[H1:R], atf[H1:R], float(HALF), None, ALU.add))
                    give(dve, lists_ready, 1)
                    dve.wait_ge(moved, 32)
                    step(v.tensor_tensor(top[:], best[0:E], best1[:, ::-1], ALU.max))
                    step(v.tensor_tensor(own[:], best[0:E], best1[:, ::-1], ALU.is_ge))
                    step(v.tensor_tensor(chosen[:], atf[0:E], at1[:, ::-1], ALU.subtract))
                    step(v.tensor_tensor(chosen[:], chosen[:], own[:], ALU.mult))
                    step(v.tensor_tensor(chosen[:], chosen[:], at1[:, ::-1], ALU.add))
                    step(v.tensor_reduce(stat[:, 2:3], top[:], AX, ALU.max))
                    v.tensor_scalar(stat[:, 0:1], stat[:, 2:3], -1.0, None, ALU.mult).then_inc(top_ready, 1)
                    dve.wait_ge(exp_ready, 1)
                    step(v.reciprocal(stat[:, 3:4], stat[:, 1:2]))
                    v.tensor_scalar(top[:], own[:], stat[:, 3:4], None, ALU.mult).then_inc(w_ready, 1)
                    dve.wait_ge(out_ready, 1)
                    v.tensor_copy(tok[:], psO[:, 0])
                    v.tensor_copy(wgt[:], psO[:, 1])

                @block.tensor
                def _(pe):
                    give(pe, xT_ready)
                    pe.wait_ge(loaded, 32)
                    for h in range(2):
                        with pe.Fori(0, NC // 4) as i:
                            for q in range(2):
                                c = i * 2 + (q + h * NC // 2)
                                pe.wait_ge(xn_ready, c + 1)
                                transpose_chunk(nc, pe, psT[:, q], xn[:, q], ident).then_inc(xT_ready, 1)
                                pe.wait_ge(xT_copied, c + 1)
                                pe.wait_ge(dve_step, c + norm_steps(False))
                                nc.tensor.matmul(psS[H1 * h:H1 * h + E, q], wr[:], xT[:, q], start=True,
                                                 stop=True).then_inc(s_ready, 1)
                    pe.wait_ge(w_ready, 1)
                    nc.tensor.transpose(psO[:, 0], chosen[:], ident[0:E, 0:E])
                    nc.tensor.transpose(psO[:, 1], top[:], ident[0:E, 0:E]).then_inc(out_ready, 1)

        with nc.cleanup_on_exit(), ExitStack() as ctx:
            st = Stage(nc, ctx, name + "e")
            w1 = st.sb("w1", [P, NB, S, M])
            w2 = st.sb("w2", [P, NB, S, K])
            b1 = st.sb("b1", [P, E, S])
            b2 = st.sb("b2", [1, E * D])
            ones = st.sb("ones", [1, P])
            carrier = st.sb("carrier", [1, 2 * NB])
            tokc = st.sb("tokc", [P, NB], U32)
            xg = st.sb("xg", [P, NB, D])
            xgT = st.sb("xgT", [P, NB, P])
            pre = st.sb("pre", [P, 2, S, P])
            hT = st.sb("hT", [P, 2, S, P])
            y = st.sb("y", [P, NB, D])
            psX = st.ps("psX", [P, 2, 512])
            psH = st.ps("psH", [P, 2, S, P])
            psY = st.ps("psY", [P, 2, 512])
            loaded = st.sem("loaded")
            w_loaded = [st.sem(f"w_loaded{q}") for q in range(NB)]
            gathered = [st.sem(f"gathered{q}") for q in range(NB)]
            added, tok_ready = st.sem("added"), st.sem("tok_ready")
            g_turned, g_copied = st.sem("g_turned"), st.sem("g_copied")
            h_ready, pre_ready, act_ready = st.sem("h_ready"), st.sem("pre_ready"), st.sem("act_ready")
            o_ready, y_ready, made = st.sem("o_ready"), st.sem("y_ready"), st.sem("made")

            def loop(eng, body, ahead=0, peel=0):
                for e in range(peel):
                    body(e, e % NB, True)
                with eng.Fori(peel // NB, E // NB - 1) as i:
                    for q in range(NB):
                        body(i * NB + q, q, True)
                for e in range(E - NB, E):
                    body(e, e % NB, e + ahead < E)

            with nc.Block() as block:

                @block.sync
                def _(sp):
                    sp.dma_start(b1[:], a["m_b1"]).then_inc(loaded, 16)
                    sp.dma_start(b2[:], a["m_b2"]).then_inc(loaded, 16)

                    def load(e, q, more):
                        sp.wait_ge(o_ready, e + 1)
                        sp.dma_start(w1[:, q], a["m_w1"][bass.ds(e, 1)].rearrange("e s d m -> d (e s) m"))\
                            .then_inc(w_loaded[q], 16)
                        sp.dma_start(w2[:, q], a["m_w2"][bass.ds(e, 1)].rearrange("e s m k -> m (e s) k"))\
                            .then_inc(w_loaded[q], 16)
                    loop(sp, load)

                @block.gpsimd
                def _(pool):
                    g = nc.gpsimd

                    def gather(e, q):
                        pool.wait_ge(g_turned, e + 1)
                        g.tensor_copy(tokc[:, q:q + 1], tok[:, bass.ds(e, 1)]).then_inc(tok_ready, 1)
                        pool.wait_ge(tok_ready, e + 1)
                        g.tensor_tensor(carrier[:, q:q + 1], ident[0:1, 0:1], ident[0:1, 0:1], ALU.mult)
                        g.indirect_dma_start(out=xg[:, q], out_offset=None, in_=xn_dram[:, :],
                                             in_offset=bass.IndirectOffsetOnAxis(ap=tokc[:, q:q + 1], axis=0))\
                            .then_inc(gathered[q], 16)

                    def body(e, q, more):
                        if more:
                            gather(e + 2, (q + 2) % NB)
                        pool.wait_ge(y_ready, e + (1 + NB))
                        if not isinstance(e, int) or e > 0:
                            pool.wait_ge(added, e * 16)
                        g.tensor_tensor(carrier[:, NB + q:NB + q + 1], ident[0:1, 0:1], ident[0:1, 0:1], ALU.mult)
                        g.indirect_dma_start(out=dest[:, :], in_=y[:, q], in_offset=None,
                                             out_offset=bass.IndirectOffsetOnAxis(ap=tokc[:, q:q + 1], axis=0),
                                             compute_op=ALU.add).then_inc(added, 16)

                    gather(0, 0)
                    gather(1, 1)
                    loop(pool, body, ahead=2, peel=NB)
                    pool.wait_ge(added, 16 * E)

                @block.scalar
                def _(act):
                    def body(e, q, more):
                        act.wait_ge(g_turned, e + (1 + NB))
                        nc.scalar.activation(xgT[:, q], psX[:, q % 2, 0:P], ACT.Copy).then_inc(g_copied, 1)
                        act.wait_ge(pre_ready, e + 1)
                        nc.scalar.activation(hT[:, q % 2], pre[:, q % 2], ACT.Gelu).then_inc(act_ready, 1)
                    loop(act, body)

                @block.vector
                def _(dve):
                    v = nc.vector
                    v.memset(ones[:], 1.0).then_inc(made, 1)
                    give(dve, y_ready, NB)
                    dve.wait_ge(loaded, 32)

                    def body(e, q, more):
                        dve.wait_ge(h_ready, e + 1)
                        v.tensor_tensor(pre[:, q % 2], psH[:, q % 2],
                                        b1[:, bass.ds(e, 1), :].rearrange("p a s -> p (a s)").unsqueeze(2)
                                        .to_broadcast([P, S, P]), ALU.add).then_inc(pre_ready, 1)
                        dve.wait_ge(o_ready, e + (1 + NB))
                        v.tensor_scalar(y[:, q], psY[:, q % 2, 0:D], wgt[:, bass.ds(e, 1)], None, ALU.mult)\
                            .then_inc(y_ready, 1)
                    loop(dve, body)

                @block.tensor
                def _(pe):
                    give(pe, g_turned, NB)
                    give(pe, o_ready, NB)
                    pe.wait_ge(made, 1)
                    pe.wait_ge(loaded, 32)

                    def turn(e, q, i):
                        pe.wait_ge(gathered[q], i * 16 + 16)
                        nc.tensor.transpose(psX[:, q % 2, 0:P], xg[:, q], ident[:]).then_inc(g_turned, 1)

                    def up(e, q, i):
                        pe.wait_ge(g_copied, e + 1)
                        pe.wait_ge(w_loaded[q], i * 32 + 32)
                        for s in range(S):
                            last = nc.tensor.matmul(psH[:, q % 2, s], w1[:, q, s], xgT[:, q],
                                                    start=True, stop=True)
                        last.then_inc(h_ready, 1)

                    def down(e, q):
                        pe.wait_ge(act_ready, e + 1)
                        nc.tensor.matmul(psY[:, q % 2, 0:D], ones[:], b2[:, bass.ds(e * D, D)],
                                         start=True, stop=False)
                        for s in range(S):
                            last = nc.tensor.matmul(psY[:, q % 2, s * K:(s + 1) * K], hT[:, q % 2, s],
                                                    w2[:, q, s], start=False, stop=(s == S - 1))
                        last.then_inc(o_ready, 1)

                    def body(e, q, i):
                        turn(e + 2, (q + 2) % NB, i + (q + 2) // NB)
                        up(e + 1, (q + 1) % NB, i + (q + 1) // NB)
                        down(e, q)

                    turn(0, 0, 0)
                    turn(1, 1, 0)
                    up(0, 0, 0)
                    with pe.Fori(0, E // NB - 1) as i:
                        for q in range(NB):
                            body(i * NB + q, q, i)
                    for e in range(E - NB, E):
                        if e + 2 < E:
                            turn(e + 2, (e + 2) % NB, (e + 2) // NB)
                        if e + 1 < E:
                            up(e + 1, (e + 1) % NB, (e + 1) // NB)
                        down(e, e % NB)


def norm_steps(twice):
    return NC + 8 + (4 if twice else 0)


def lay_more(i, a, rows):
    import numpy as np
    L = "L1_ffn_"
    a["m_wr"] = i[L + "Wr"].T
    a["m_w1"] = i[L + "W1"]
    a["m_w2"] = i[L + "W2"]
    a["m_b1"] = i[L + "b1"].transpose(2, 0, 1)
    a["m_b2"] = i[L + "b2"].reshape(1, -1)
    lay_attn(i, a, rows)
    lay_cell(i, a, rows)


def attention_stage(nc, name, kind, X, XA, ident, a):
    H, DH = 16, 8
    W = 64 if kind == "b" else 32
    NB = 32
    HPB = P // W
    NG = H // HPB
    PAIR = 2
    N = NT // PAIR
    SCALE = float(DH) ** -0.5
    widths = {"b": [256, 256], "c": [128, 128], "d": [128, 256]}[kind]
    units = []
    for t in range(PAIR):
        kw = widths[t]
        for h in range(0, H, 512 // kw):
            units.append((t, h, 512 // kw, kw, t * P if kind == "c" else 0))
    U = len(units)
    QG = NG // 4
    affine = kind in "bc"
    with nc.cleanup_on_exit(), ExitStack() as ctx:
        st = Stage(nc, ctx, name)
        norm = Norm(st, {"b": 1e-6, "c": 1e-5, "d": None}[kind])
        tmp = st.sb("tmp", [P, 2, PAIR, D])
        xn = st.sb("xn", [P, 2, PAIR, D])
        res = st.sb("res", [P, 2, PAIR, D])
        wqkv = st.sb("wqkv", [P, 3 * D])
        wo = st.sb("wo", [P, D])
        bqkv = st.sb("bqkv", [P, 3 * D])
        bo = st.sb("bo", [P, D])
        gam = st.sb("gam", [P, 1])
        bet = st.sb("bet", [P, 1])
        hT = st.sb("hT", [P, PAIR, P])
        qkv = st.sb("qkv", [P, PAIR, 3 * D])
        slots = st.sb("slots", [P, PAIR, 2, H * W])
        turned = st.sb("turned", [P, 2, NG, PAIR * P])
        prob = st.sb("prob", [P, 2, 512])
        probT = st.sb("probT", [P, 2, 4, P])
        nmax = st.sb("nmax", [P, PAIR, H])
        total = st.sb("total", [P, PAIR, H])
        inv = st.sb("inv", [P, PAIR, H])
        o = st.sb("o", [P, PAIR, D])
        oT = st.sb("oT", [P, PAIR, P])
        upd = st.sb("upd", [P, PAIR, D])
        if kind == "b":
            wcl = st.sb("wcl", [P, 2, H * NB])
            wh = st.sb("wh", [P, 2, H * NB])
            wT = st.sb("wT", [P, 2, P])
            cl = st.sb("cl", [P, H, NB])
            ce = st.sb("ce", [P, H, NB])
            cm = st.sb("cm", [P, 2, H])
        if kind == "c":
            group = st.sb("group", [P, 2, 8])
        if kind == "d":
            BF16 = mybir.dt.bfloat16
            rot = st.sb("rot", [P, 2, PAIR, 2, 4])
            maskf = st.sb("maskf", [P, 2 * P])
            causal = st.sb("causal", [P, 2 * P], BF16)
            ident16 = st.sb("ident16", [P, P], BF16)
            ra = st.sb("ra", [P, 2, H * 4])
            rb = st.sb("rb", [P, 2, H * 4])
        psS = st.ps("psS", [P, 2, 512])
        psT = st.ps("psT", [P, 2, 4, P])
        psP = st.ps("psP", [P, 2, 512])
        psO = st.ps("psO", [P, 512])
        psF = st.ps("psF", [P, 4, P])
        o_bank = [psO[:, 0:D], psP[:, 1, 0:D]]
        loaded, dve_step, pool_step = st.sem("loaded"), st.sem("dve_step"), st.sem("pool_step")
        stats_done, const_ready, slots_zero = st.sem("stats_done"), st.sem("const_ready"), st.sem("slots_zero")
        xn_ready, xT_ready, h_ready = st.sem("xn_ready"), st.sem("xT_ready"), st.sem("h_ready")
        proj_ready, prep_done = st.sem("proj_ready"), st.sem("prep_done")
        cl_ready, cl_exp = st.sem("cl_ready"), st.sem("cl_exp")
        q_slotted, k_slotted = st.sem("q_slotted"), st.sem("k_slotted")
        qt_ready, qt_copied = st.sem("qt_ready"), st.sem("qt_copied")
        s_ready, m_ready, p_ready = st.sem("s_ready"), st.sem("m_ready"), st.sem("p_ready")
        t_ready, pt_ready, av_done = st.sem("t_ready"), st.sem("pt_ready"), st.sem("av_done")
        o_ready, oT_ready, oT_copied = st.sem("o_ready"), st.sem("oT_ready"), st.sem("oT_copied")
        out_ready, x_updated = st.sem("out_ready"), st.sem("x_updated")
        wT_ready, wT_copied, wcl_made = st.sem("wT_ready"), st.sem("wT_copied"), st.sem("wcl_made")
        loads = [(wqkv[:], a[kind + "_wqkv"]), (wo[:], a[kind + "_wo"])]
        if kind in "cd":
            loads += [(bqkv[:], a[kind + "_bqkv"]), (bo[:], a[kind + "_bo"])]
        if affine:
            loads += [(gam[:], a[kind + "_gam"]), (bet[:], a[kind + "_bet"])]
        if kind == "b":
            loads += [(wh[:], a["b_wh"])]
        if kind == "c":
            loads += [(group[:], a["c_group"])]
        if kind == "d":
            loads += [(rot[:], a["d_rot"]), (maskf[:], a["d_mask"])]
        LOADED = 16 * len(loads)
        PER_PAIR = PAIR + 1 + {"b": PAIR * 7, "c": 1, "d": 0}[kind]
        PREP = 3 if kind == "b" else 1

        with nc.Block() as block:

            @block.sync
            def _(sp):
                for dst, src in loads:
                    sp.dma_start(dst, src).then_inc(loaded, 16)

            @block.gpsimd
            def _(pool):
                g = nc.gpsimd
                step = Chain(pool, pool_step)
                step(g.memset(slots[:], 0.0))
                pool.wait_ge(loaded, LOADED)
                if kind == "c":
                    for t in range(PAIR):
                        for side in range(2):
                            dst = slots[:, t, side].rearrange("p (h w) -> p h w", h=H)[:, :, DH:2 * DH]
                            step(g.tensor_copy(dst, group[:, side].unsqueeze(1).to_broadcast([P, H, 8])))
                if kind == "d":
                    g.tensor_copy(causal[:], maskf[:])
                    step(g.tensor_copy(ident16[:], ident[:]))
                give(pool, slots_zero, 1)
                pool.wait_ge(stats_done, 1)
                inner = norm.rstd if norm.inner_eps is None else norm.rboth
                with pool.Fori(0, N // 2) as i:
                    step.loop(i, 2 if kind != "d" else 2 * (1 + 4 * PAIR))
                    for q in range(2):
                        c = i * 2 + q
                        tiles = bass.ds(c * PAIR, PAIR)
                        pool.wait_ge(xT_ready, c + 1)
                        step(g.tensor_tensor(tmp[:, q], X[:, tiles, :], bcast(norm.mean[:, tiles], D),
                                             ALU.subtract))
                        if kind != "d":
                            pool.wait_ge(x_updated, c + 1)
                            g.tensor_tensor(res[:, q], tmp[:, q], bcast(norm.rstd[:, tiles], D), ALU.mult)
                        g.tensor_tensor(xn[:, q], tmp[:, q], bcast(inner[:, tiles], D), ALU.mult)\
                            .then_inc(xn_ready, 1)
                        if kind == "d":
                            for t in range(PAIR):
                                pool.wait_ge(prep_done, c * PAIR + (t + 1))
                                for side in range(2):
                                    pairs = qkv[:, t, side * D:(side + 1) * D]\
                                        .rearrange("p (h r e) -> p e h r", h=H, e=2)
                                    cs = [rot[:, side, t, x].unsqueeze(1).to_broadcast([P, H, 4])
                                          for x in range(2)]
                                    ra3 = ra[:, side].rearrange("p (h r) -> p h r", h=H)
                                    rb3 = rb[:, side].rearrange("p (h r) -> p h r", h=H)
                                    g.tensor_tensor(ra3, pairs[:, 0], cs[0], ALU.mult)
                                    step(g.tensor_tensor(rb3, pairs[:, 1], cs[1], ALU.mult))
                                    dst = slots[:, t, side].rearrange("p (h w) -> p h w", h=H)[:, :, 0:4]
                                    step(g.tensor_tensor(dst, ra3, rb3, ALU.subtract))
                step.end(N // 2)

            def rotated(c_half, q, t):
                return c_half * (2 * (1 + 4 * PAIR)) + (2 + q * (1 + 4 * PAIR) + 1 + 4 * (t + 1))

            @block.vector
            def _(dve):
                v = nc.vector
                step = Chain(dve, dve_step)
                give(dve, x_updated)
                give(dve, pt_ready)
                norm.dve(nc, dve, step, X)
                give(dve, stats_done, 1)
                dve.wait_ge(slots_zero, 1)
                if kind == "b":
                    for side in range(2):
                        dve.wait_ge(wcl_made, side + 1)
                        step(v.tensor_copy(wcl[:, side], psS[:, side]))
                    give(dve, const_ready, 1)

                def soften(t, side):
                    src = psP[:, 1 - side].rearrange("p (h n) -> p h n", h=H)
                    step(v.tensor_reduce(cm[:, side], src, AX, ALU.max))
                    v.tensor_tensor(cl[:], src, bcast(cm[:, side], NB), ALU.subtract).then_inc(cl_ready, 1)

                def spread(t, side, n):
                    dve.wait_ge(cl_exp, n)
                    step(v.tensor_reduce(cm[:, side], ce[:], AX, ALU.add))
                    step(v.reciprocal(cm[:, side], cm[:, side]))
                    if side == 0:
                        step(v.tensor_scalar(cm[:, side], cm[:, side], 0.1, None, ALU.mult))
                    dst = slots[:, t, side].rearrange("p (h w) -> p h w", h=H)[:, :, 0:NB]
                    v.tensor_tensor(dst, ce[:], bcast(cm[:, side], NB), ALU.mult).then_inc(prep_done, 1)

                with dve.Fori(0, N // 2) as i:
                    step.loop(i, 2 * PER_PAIR)
                    for q in range(2):
                        c = i * 2 + q
                        tiles = bass.ds(c * PAIR, PAIR)
                        for t in range(PAIR):
                            base = (c * PAIR + t) * PREP
                            dve.wait_ge(proj_ready, base + 1)
                            if kind == "b":
                                v.tensor_copy(qkv[:, t], psP[:, 0, 0:3 * D]).then_inc(prep_done, 1)
                                for side in range(2):
                                    dve.wait_ge(proj_ready, base + (2 + side))
                                    soften(t, side)
                                    spread(t, side, (c * PAIR + t) * 2 + (side + 1))
                                    dve.wait_ge(prep_done, base + (2 + side))
                            else:
                                v.tensor_tensor(qkv[:, t], psP[:, t, 0:3 * D], bqkv[:], ALU.add)\
                                    .then_inc(prep_done, 1)
                        for u in range(U + 1):
                            if u < U:
                                t, h, nh, kw, _ = units[u]
                                dve.wait_ge(s_ready, c * U + (u + 1))
                                v.tensor_reduce(nmax[:, t, h:h + nh], psS[:, u % 2].rearrange(
                                    "p (h k) -> p h k", h=nh), AX, ALU.max, negate=True).then_inc(m_ready, 1)
                            if u > 0:
                                dve.wait_ge(t_ready, c * U + (u + AHEAD))
                                v.tensor_copy(probT[:, (u - 1) % 2], psT[:, (u - 1) % 2]).then_inc(pt_ready, 1)
                        for t in range(PAIR):
                            last_u = max(n for n, x in enumerate(units) if x[0] == t) + 1
                            dve.wait_ge(p_ready, c * U + (last_u + AHEAD))
                            step(v.reciprocal(inv[:, t].rearrange("p (g r) -> p g r", r=HPB),
                                              total[:, t].rearrange("p (r g) -> p g r", r=HPB)))
                            dve.wait_ge(av_done, c * U + (last_u + AHEAD))
                            v.tensor_tensor(o[:, t].rearrange("p (h f) -> p h f", h=H),
                                            o_bank[t].rearrange("p (h f) -> p h f", h=H),
                                            bcast(inv[:, t], DH), ALU.mult).then_inc(o_ready, 1)
                        dve.wait_ge(out_ready, c + 1)
                        step(v.tensor_tensor(upd[:], psP[:, 0, 0:PAIR * D].rearrange("p (t d) -> p t d", d=D),
                                             bo[:].unsqueeze(1).to_broadcast([P, PAIR, D])
                                             if kind == "d" else res[:, q], ALU.add))
                        if kind == "b":
                            v.tensor_copy(XA[:, tiles, :], upd[:]).then_inc(x_updated, 1)
                        else:
                            if kind == "c":
                                step(v.tensor_tensor(upd[:], upd[:], bo[:].unsqueeze(1)
                                                     .to_broadcast([P, PAIR, D]), ALU.add))
                            v.tensor_tensor(X[:, tiles, :], X[:, tiles, :], upd[:], ALU.add).then_inc(x_updated, 1)
                        dve.wait_ge(x_updated, c + (1 + AHEAD))
                step.end(N // 2)

            @block.scalar
            def _(act):
                s = nc.scalar
                give(act, p_ready)
                norm.act(nc, act)
                act.wait_ge(loaded, LOADED)
                act.wait_ge(slots_zero, 1)
                if kind == "b":
                    for side in range(2):
                        act.wait_ge(wT_ready, side + 1)
                        s.activation(wT[:, side], psT[:, side, 0], ACT.Copy).then_inc(wT_copied, 1)
                with act.Fori(0, N) as c:
                    act.wait_ge(xT_ready, c + (1 + AHEAD))
                    xT = psF[:, 0:PAIR]
                    if affine:
                        s.activation(hT[:], xT, ACT.Identity, bias=bet[:], scale=gam[:]).then_inc(h_ready, 1)
                    else:
                        s.activation(hT[:], xT, ACT.Copy).then_inc(h_ready, 1)
                    for t in range(PAIR):
                        base = (c * PAIR + t) * PREP
                        if kind != "d":
                            act.wait_ge(prep_done, base + 1)
                            for side in range(2):
                                w0 = NB if kind == "b" else 0
                                dst = slots[:, t, side].rearrange("p (h w) -> p h w", h=H)[:, :, w0:w0 + DH]
                                src = qkv[:, t, side * D:(side + 1) * D].rearrange("p (h f) -> p h f", h=H)
                                s.activation(dst, src, ACT.Copy, scale=1.0 if side else SCALE)\
                                    .then_inc(k_slotted if side else q_slotted, 1)
                        if kind == "b":
                            for side in range(2):
                                act.wait_ge(cl_ready, (c * PAIR + t) * 2 + (side + 1))
                                s.activation(ce[:], cl[:], ACT.Exp).then_inc(cl_exp, 1)
                    for t in range(PAIR):
                        for side in range(2):
                            for b in range(QG):
                                n = (t * 2 + side) * QG + b
                                act.wait_ge(qt_ready, c * (PAIR * 2 * QG) + (n + 1))
                                s.activation(turned[:, side, 4 * b:4 * b + 4, t * P:(t + 1) * P],
                                             psT[:, n % 2], ACT.Copy).then_inc(qt_copied, 1)
                    for u, (t, h, nh, kw, _) in enumerate(units):
                        act.wait_ge(m_ready, c * U + (u + 1))
                        act.wait_ge(t_ready, c * U + (u + 1))
                        for j in range(nh):
                            last = s.activation(prob[:, u % 2, j * kw:(j + 1) * kw],
                                                psS[:, u % 2, j * kw:(j + 1) * kw], ACT.Exp,
                                                bias=nmax[:, t, h + j:h + j + 1],
                                                accum_out=total[:, t, h + j:h + j + 1])
                        last.then_inc(p_ready, 1)
                    act.wait_ge(oT_ready, c + 1)
                    s.activation(oT[:], psF[:, 2:2 + PAIR], ACT.Copy).then_inc(oT_copied, 1)

            @block.tensor
            def _(pe):
                mm, turn = nc.tensor.matmul, nc.tensor.transpose
                give(pe, xT_ready)
                give(pe, t_ready)
                give(pe, av_done)
                pe.wait_ge(loaded, LOADED)
                if kind == "b":
                    for side in range(2):
                        turn(psT[:, side, 0], wqkv[:, side * D:(side + 1) * D], ident[:]).then_inc(wT_ready, 1)
                    for side in range(2):
                        pe.wait_ge(wT_copied, side + 1)
                        mm(psS[:, side], wT[:, side], wh[:, side], start=True, stop=True).then_inc(wcl_made, 1)
                    pe.wait_ge(const_ready, 1)
                pe.wait_ge(slots_zero, 1)

                def scores(c, u):
                    t, h, nh, kw, k0 = units[u]
                    pe.wait_ge(p_ready, c * U + (u + 1))
                    if kind == "d":
                        mm(psS[:, u % 2].rearrange("p (h k) -> p h k", h=nh), ident16[:],
                           causal[:, 2 * P - kw:2 * P].unsqueeze(1).to_broadcast([P, nh, kw]),
                           start=True, stop=False)
                    for j in range(nh):
                        g, r = (h + j) % NG, (h + j) // NG
                        rows = slice(W * r, W * r + W)
                        qT = turned[rows, 0, g, t * P:(t + 1) * P]
                        last = mm(psS[:, u % 2, j * kw:(j + 1) * kw], qT, turned[rows, 1, g, k0:k0 + kw],
                                  start=(kind != "d"), stop=(kind != "d" or j == nh - 1))
                    last.then_inc(s_ready, 1)

                def turn_probs(c, u):
                    pe.wait_ge(p_ready, c * U + (u + 1 + AHEAD))
                    pe.wait_ge(pt_ready, c * U + (u + 1))
                    for j in range(4):
                        last = turn(psT[:, u % 2, j], prob[:, u % 2, j * P:(j + 1) * P], ident[:])
                    last.then_inc(t_ready, 1)

                def values(c, u):
                    t, h, nh, kw, k0 = units[u]
                    pe.wait_ge(pt_ready, c * U + (u + 1 + AHEAD))
                    nk = kw // P
                    for j in range(4):
                        place, kt = h + j // nk, (k0 // P) + j % nk
                        head = place % NG * HPB + place // NG
                        last = mm(o_bank[t][:, head * DH:(head + 1) * DH], probT[:, u % 2, j],
                                  qkv[:, kt, 2 * D + head * DH:2 * D + (head + 1) * DH],
                                  start=(j % nk == 0), stop=(j % nk == nk - 1))
                    last.then_inc(av_done, 1)

                with pe.Fori(0, N // 2) as i:
                    for q in range(2):
                        c = i * 2 + q
                        pe.wait_ge(xn_ready, c + 1)
                        for t in range(PAIR):
                            last = turn(psF[:, t], xn[:, q, t], ident[:])
                        last.then_inc(xT_ready, 1)
                        pe.wait_ge(h_ready, c + 1)
                        pe.wait_ge(x_updated, c + AHEAD)
                        for t in range(PAIR):
                            base = (c * PAIR + t) * PREP
                            if kind == "b":
                                if t:
                                    pe.wait_ge(prep_done, base)
                                mm(psP[:, 0, 0:3 * D], hT[:, t], wqkv[:], start=True, stop=True)\
                                    .then_inc(proj_ready, 1)
                                mm(psP[:, 1], hT[:, t], wcl[:, 0], start=True, stop=True)\
                                    .then_inc(proj_ready, 1)
                                pe.wait_ge(prep_done, base + 1)
                                mm(psP[:, 0], hT[:, t], wcl[:, 1], start=True, stop=True)\
                                    .then_inc(proj_ready, 1)
                            else:
                                mm(psP[:, t, 0:3 * D], hT[:, t], wqkv[:], start=True, stop=True)\
                                    .then_inc(proj_ready, 1)
                        pe.wait_ge(pt_ready, c * U + AHEAD)
                        for t in range(PAIR):
                            for side in range(2):
                                if kind == "d":
                                    pe.wait_ge(pool_step, rotated(i, q, t))
                                else:
                                    pe.wait_ge(k_slotted if side else q_slotted, c * PAIR + (t + 1))
                                if kind == "b":
                                    pe.wait_ge(prep_done, (c * PAIR + t) * PREP + (2 + side))
                                for b in range(QG):
                                    n = (t * 2 + side) * QG + b
                                    if n >= 2:
                                        pe.wait_ge(qt_copied, c * (PAIR * 2 * QG) + (n - 1))
                                    for j in range(4):
                                        g = 4 * b + j
                                        last = turn(psT[:, n % 2, j], slots[:, t, side, g * P:(g + 1) * P],
                                                    ident[:])
                                    last.then_inc(qt_ready, 1)
                        pe.wait_ge(qt_copied, c * (PAIR * 2 * QG) + PAIR * 2 * QG)
                        scores(c, 0)
                        for u in range(U):
                            if u + 1 < U:
                                scores(c, u + 1)
                            turn_probs(c, u)
                            if u:
                                values(c, u - 1)
                        values(c, U - 1)
                        pe.wait_ge(o_ready, c * PAIR + PAIR)
                        for t in range(PAIR):
                            last = turn(psF[:, 2 + t], o[:, t], ident[:])
                        last.then_inc(oT_ready, 1)
                        pe.wait_ge(oT_copied, c + 1)
                        for t in range(PAIR):
                            last = mm(psP[:, 0, t * P:(t + 1) * P], oT[:, t], wo[:], start=True, stop=True)
                        last.then_inc(out_ready, 1)


def lay_attn(i, a, rows):
    import numpy as np
    L = "L1_attn_a_"
    a["c_wqkv"] = np.concatenate([i[L + "W" + x] for x in "qkv"], axis=1)
    a["c_bqkv"] = rows(np.concatenate([i[L + "b" + x] for x in "qkv"]))
    a["c_wo"], a["c_bo"] = i[L + "Wo"], rows(i[L + "bo"])
    a["c_gam"], a["c_bet"] = i[L + "ln_g"].reshape(P, 1), i[L + "ln_b"].reshape(P, 1)
    own = (np.arange(P)[:, None] % 8 == np.arange(8)[None, :]).astype(np.float32)
    a["c_group"] = np.stack([own * np.float32(NEG), 1 - own], axis=1)
    L = "L1_attn_b_"
    a["d_wqkv"] = np.concatenate([i[L + "W" + x].T for x in "qkv"], axis=1)
    a["d_bqkv"] = rows(np.concatenate([i[L + "b" + x] for x in "qkv"]))
    a["d_wo"], a["d_bo"] = i[L + "Wo"].T, rows(i[L + "bo"])
    steps = np.arange(1, T + 1, dtype=np.float32)[:, None]
    theta = (np.float32(1.0 / 10000.0) ** (np.float32(2.0) * np.arange(4, dtype=np.float32) / np.float32(8)))
    angle = steps * theta
    cs = np.stack([np.cos(angle), np.sin(angle)], axis=1).astype(np.float32)
    cs = cs.reshape(2, P, 2, 4).transpose(1, 0, 2, 3)
    a["d_rot"] = np.stack([cs * np.float32(8.0 ** -0.5), cs], axis=1)
    a["d_mask"] = np.where(np.arange(2 * P)[None, :] - P > np.arange(P)[:, None], NEG, 0.0).astype(np.float32)
    L = "L0_attn_b_"
    a["b_wqkv"] = np.concatenate([i[L + "W" + x].reshape(D, D) for x in "qkv"], axis=1)
    a["b_wo"] = i[L + "Wo"].reshape(D, D)
    a["b_gam"], a["b_bet"] = i[L + "ln1_g"].reshape(P, 1), i[L + "ln1_b"].reshape(P, 1)
    wh = np.zeros((D, 2, 16, 32), np.float32)
    for h in range(16):
        wh[8 * h:8 * h + 8, 0, h] = i[L + "Whq"][h]
        wh[8 * h:8 * h + 8, 1, h] = i[L + "Whk"][h]
    a["b_wh"] = wh.reshape(D, 2, 512)
    a["b_mlp_fc1"], a["b_mlp_fc2"] = i[L + "W1"], i[L + "W2"]
    a["b_mlp_b1"], a["b_mlp_b2"] = i[L + "b1"].reshape(-1, P).T, rows(i[L + "b2"])
    a["b_mlp_gam"], a["b_mlp_bet"] = i[L + "ln2_g"].reshape(P, 1), i[L + "ln2_b"].reshape(P, 1)


def cell_stage(nc, name, X, ident, a):
    BL, NS = 4, 32
    HR = NS // 2
    KN, Q, V, BE, WU, OM, SM, REC = 0, NS, 2 * NS, 2 * NS + HR, 96, 97, 98, 100
    PK, PV, PB, PQ, PL, PROJ = 0, 128, 256, 384, 416, 420
    TC = 16
    NCH = T // TC
    rec_dram = nc.dram_tensor(f"{name}_rec", (B * T, 2 * BL * REC), F32, kind="Internal").ap()
    cell_dram = nc.dram_tensor(f"{name}_cell", (B, TC + T, NS), F32, kind="Internal").ap()

    with nc.cleanup_on_exit(), ExitStack() as ctx:
        st = Stage(nc, ctx, name + "p")
        norm = Norm(st)
        tmp = st.sb("tmp", [P, 2, TPC, D])
        xn = st.sb("xn", [P, 2, TPC, D])
        hT = st.sb("hT", [P, 2, CW])
        xp = st.sb("xp", [P, 2, CW])
        win = st.sb("win", [P, D])
        wcat = st.sb("wcat", [P, PROJ])
        bbeta = st.sb("bbeta", [P, BL * NS])
        lower = st.sb("lower", [P, BL, BL])
        raw = st.sb("raw", [P, 2, TPC, PROJ])
        sq = st.sb("sq", [P, TPC * BL, NS])
        ss = st.sb("ss", [P, TPC * BL])
        nrm = st.sb("nrm", [P, TPC * BL])
        bt = st.sb("bt", [P, TPC, BL * NS])
        lg = st.sb("lg", [P, TPC, BL])
        ex = st.sb("ex", [P, TPC, BL])
        gt = st.sb("gt", [P, TPC, BL, BL])
        eq = st.sb("eq", [P, TPC, BL, BL])
        rank = st.sb("rank", [P, TPC, BL])
        one = st.sb("one", [P, TPC])
        rec = st.sb("rec", [P, 2, TPC, 2 * BL * REC])
        psT = st.ps("psT", [P, CW])
        psA = st.ps("psA", [P, CW])
        psR = st.ps("psR", [P, TPC, 512])
        loaded, dve_step, pool_step = st.sem("loaded"), st.sem("dve_step"), st.sem("pool_step")
        stats_done, xn_ready, xT_ready = st.sem("stats_done"), st.sem("xn_ready"), st.sem("xT_ready")
        h_ready, a_ready, xp_ready = st.sem("h_ready"), st.sem("a_ready"), st.sem("xp_ready")
        r_ready, raw_ready, raw_read = st.sem("r_ready"), st.sem("raw_ready"), st.sem("raw_read")
        ss_ready, nrm_ready, bt_ready = st.sem("ss_ready"), st.sem("nrm_ready"), st.sem("bt_ready")
        lg_ready, ex_ready, kn_ready = st.sem("lg_ready"), st.sem("ex_ready"), st.sem("kn_ready")
        rec_act, rec_dve = st.sem("rec_act"), st.sem("rec_dve")
        kept = [st.sem(f"kept{q}") for q in range(2)]
        STEPS = 18

        def record(q, lo, n):
            return rec[:, q].rearrange("p j (n h f) -> p (j n) h f", h=2, f=REC)[:, :, :, lo:lo + n]

        with nc.Block() as block:

            @block.sync
            def _(sp):
                for dst, src in ((win[:], a["a_win"]), (wcat[:], a["a_wcat"]), (bbeta[:], a["a_bbeta"]),
                                 (lower[:], a["a_lower"])):
                    sp.dma_start(dst, src).then_inc(loaded, 16)
                tiles_of = rec_dram.rearrange("(r p) f -> p r f", p=P)
                for q in range(2):
                    sp.drain().then_inc(kept[q], 16)
                with sp.Fori(0, NC // 2) as i:
                    for q in range(2):
                        c = i * 2 + q
                        sp.wait_ge(rec_act, c + 1)
                        sp.wait_ge(rec_dve, c + 1)
                        sp.dma_start(tiles_of[:, bass.ds(c * TPC, TPC), :], rec[:, q]).then_inc(kept[q], 16)
                for q in range(2):
                    sp.wait_ge(kept[q], 16 * (NC // 2 + 1))

            @block.gpsimd
            def _(pool):
                g = nc.gpsimd
                g.memset(rec[:], 0.0)
                give(pool, pool_step, 1)
                pool.wait_ge(stats_done, 1)
                with pool.Fori(0, NC // 2) as i:
                    for q in range(2):
                        c = i * 2 + q
                        tiles = bass.ds(c * TPC, TPC)
                        pool.wait_ge(xT_ready, c + 1)
                        g.tensor_tensor(tmp[:, q], X[:, tiles, :], bcast(norm.mean[:, tiles], D), ALU.subtract)\
                            .then_inc(pool_step, 1)
                        pool.wait_ge(pool_step, c + 2)
                        g.tensor_tensor(xn[:, q], tmp[:, q], bcast(norm.rstd[:, tiles], D), ALU.mult)\
                            .then_inc(xn_ready, 1)

            @block.vector
            def _(dve):
                v = nc.vector
                step = Chain(dve, dve_step)
                norm.dve(nc, dve, step, X)
                give(dve, stats_done, 1)
                dve.wait_ge(loaded, 16 * 4)
                dve.wait_ge(pool_step, 1)
                with dve.Fori(0, NC // 2) as i:
                    step.loop(i, 2 * STEPS)
                    for q in range(2):
                        c = i * 2 + q
                        dve.wait_ge(raw_ready, c + 1)
                        k3 = raw[:, q, :, PK:PK + BL * NS].rearrange("p j (n r) -> p j n r", n=BL)
                        step(v.tensor_tensor(sq[:].rearrange("p (j n) r -> p j n r", n=BL), k3, k3, ALU.mult))
                        v.tensor_reduce(ss[:], sq[:], AX, ALU.add).then_inc(ss_ready, 1)
                        v.tensor_tensor(bt[:], raw[:, q, :, PB:PB + BL * NS],
                                        bbeta[:].unsqueeze(1).to_broadcast([P, TPC, BL * NS]), ALU.add)\
                            .then_inc(bt_ready, 1)
                        l = raw[:, q, :, PL:PL + BL]
                        step(v.tensor_reduce(one[:], l, AX, ALU.max))
                        v.tensor_tensor(lg[:], l, bcast(one[:], BL), ALU.subtract).then_inc(lg_ready, 1)
                        other = l.unsqueeze(2).to_broadcast([P, TPC, BL, BL])
                        own = l.unsqueeze(3).to_broadcast([P, TPC, BL, BL])
                        step(v.tensor_tensor(gt[:], other, own, ALU.is_gt))
                        step(v.tensor_tensor(eq[:], other, own, ALU.is_equal))
                        step(v.tensor_tensor(eq[:], eq[:], lower[:].unsqueeze(1).to_broadcast([P, TPC, BL, BL]),
                                             ALU.mult))
                        step(v.tensor_tensor(gt[:], gt[:], eq[:], ALU.add))
                        step(v.tensor_reduce(rank[:], gt[:], AX, ALU.add))
                        step(v.tensor_scalar(rank[:], rank[:], 1.5, None, ALU.is_lt))
                        dve.wait_ge(ex_ready, c + 1)
                        step(v.tensor_reduce(one[:], ex[:], AX, ALU.add))
                        step(v.reciprocal(one[:], one[:]))
                        step(v.tensor_tensor(ex[:], ex[:], bcast(one[:], BL), ALU.mult))
                        dve.wait_ge(kept[q], i * 16 + 16)
                        both = lambda t: t[:].rearrange("p j n -> p (j n)").unsqueeze(2)\
                            .to_broadcast([P, TPC * BL, 2])
                        place = lambda lo: record(q, lo, 1).rearrange("p x h f -> p x (h f)")
                        dst = rec[:, q].rearrange("p j (x f) -> p j x f", f=REC)[:, :, :, V:V + HR]
                        v.tensor_copy(dst, raw[:, q, :, PV:PV + BL * NS].rearrange("p j (x r) -> p j x r", r=HR))
                        v.tensor_copy(place(SM), both(ex))
                        step(v.tensor_tensor(rank[:], rank[:], ex[:], ALU.mult))
                        step(v.tensor_reduce(one[:], rank[:], AX, ALU.add))
                        step(v.tensor_scalar(one[:], one[:], 1e-8, None, ALU.add))
                        step(v.reciprocal(one[:], one[:]))
                        step(v.tensor_tensor(rank[:], rank[:], bcast(one[:], BL), ALU.mult))
                        v.tensor_copy(place(WU), both(rank))
                        v.tensor_scalar(place(OM), both(rank), -1.0, 1.0, ALU.mult, ALU.add)
                        dve.wait_ge(nrm_ready, c + 1)
                        step(v.tensor_scalar(ss[:], nrm[:], 1e-6, None, ALU.add))
                        step(v.reciprocal(ss[:], ss[:]))
                        for h in range(2):
                            last = v.tensor_tensor(record(q, KN, NS)[:, :, h].rearrange(
                                "p (j n) r -> p j n r", n=BL), k3,
                                ss[:].rearrange("p (j n) -> p j n", n=BL).unsqueeze(3)
                                .to_broadcast([P, TPC, BL, NS]), ALU.mult)
                        last.then_inc(rec_dve, 1)
                        dve.wait_ge(rec_dve, c + 1)
                step.end(NC // 2)

            @block.scalar
            def _(act):
                s = nc.scalar
                norm.act(nc, act)
                act.wait_ge(pool_step, 1)
                with act.Fori(0, NC // 2) as i:
                    for q in range(2):
                        c = i * 2 + q
                        act.wait_ge(xT_ready, c + (1 + AHEAD))
                        s.activation(hT[:, q], psT[:], ACT.Copy).then_inc(h_ready, 1)
                        act.wait_ge(a_ready, c + 1)
                        s.activation(xp[:, q], psA[:], ACT.Silu).then_inc(xp_ready, 1)
                        act.wait_ge(r_ready, c + 1)
                        act.wait_ge(kept[q], i * 16 + 16)
                        s.activation(raw[:, q], psR[:, :, 0:PROJ], ACT.Copy).then_inc(raw_ready, 1)
                        act.wait_ge(raw_ready, c + 1)
                        for j in range(TPC):
                            s.activation(rec[:, q, j].rearrange("p (x f) -> p x f", f=REC)[:, :, Q:Q + NS],
                                         raw[:, q, j, PQ:PQ + NS].unsqueeze(1).to_broadcast([P, 2 * BL, NS]),
                                         ACT.Copy)
                        act.wait_ge(ss_ready, c + 1)
                        s.activation(nrm[:], ss[:], ACT.Sqrt).then_inc(nrm_ready, 1)
                        act.wait_ge(lg_ready, c + 1)
                        s.activation(ex[:], lg[:], ACT.Exp).then_inc(ex_ready, 1)
                        act.wait_ge(bt_ready, c + 1)
                        dst = rec[:, q].rearrange("p j (x f) -> p j x f", f=REC)[:, :, :, BE:BE + HR]
                        s.activation(dst, bt[:].rearrange("p j (x r) -> p j x r", r=HR), ACT.Sigmoid)\
                            .then_inc(rec_act, 1)

            @block.tensor
            def _(pe):
                give(pe, xT_ready)
                pe.wait_ge(loaded, 16 * 4)
                with pe.Fori(0, NC // 2) as i:
                    for q in range(2):
                        c = i * 2 + q
                        pe.wait_ge(xn_ready, c + 1)
                        transpose_chunk(nc, pe, psT, xn[:, q], ident).then_inc(xT_ready, 1)
                        pe.wait_ge(h_ready, c + 1)
                        nc.tensor.matmul(psA[:], win[:], hT[:, q], start=True, stop=True).then_inc(a_ready, 1)
                        pe.wait_ge(xp_ready, c + 1)
                        for j in range(TPC):
                            last = nc.tensor.matmul(psR[:, j, 0:PROJ], xp[:, q, j * P:(j + 1) * P], wcat[:],
                                                    start=True, stop=True)
                        last.then_inc(r_ready, 1)

    with nc.cleanup_on_exit(), ExitStack() as ctx:
        st = Stage(nc, ctx, name + "s")
        R = st.sb("R", [P, 2, TC, REC])
        S = st.sb("S", [P, HR, NS])
        prod = st.sb("prod", [P, HR, NS])
        ret = st.sb("ret", [P, HR])
        delta = st.sb("delta", [P, HR])
        outer = st.sb("outer", [P, HR, NS])
        decay = st.sb("decay", [P, HR, NS])
        pre = st.sb("pre", [P, HR, NS])
        upd = st.sb("upd", [P, HR, NS])
        keep = st.sb("keep", [P, HR, NS])
        read = st.sb("read", [P, HR, NS])
        sq = st.sb("sq", [P, 2, TC, HR])
        smc = st.sb("smc", [P, 2, TC])
        ex = st.sb("ex", [P, TC * HR])
        sig = st.sb("sig", [P, TC * HR])
        g1 = st.sb("g1", [P, TC * HR])
        g2 = st.sb("g2", [P, TC * HR])
        zo = st.sb("zo", [NS, 2, TC, HR])
        sel = st.sb("sel", [P, NS])
        psZ = st.ps("psZ", [NS, TC * HR])
        loaded, zeroed = st.sem("loaded"), st.sem("zeroed")
        rec_in = [st.sem(f"rec_in{q}") for q in range(2)]
        s_ready, step_sem, ret_step = st.sem("s_ready"), st.sem("dve_step"), st.sem("pool_step")
        decay_ready, read_ready, sq_ready = st.sem("decay_ready"), st.sem("read_ready"), st.sem("sq_ready")
        pre_ready, upd_ready, keep_ready = st.sem("pre_ready"), st.sem("upd_ready"), st.sem("keep_ready")
        sm_kept, ex_ready, sig_ready = st.sem("sm_kept"), st.sem("ex_ready"), st.sem("sig_ready")
        g_ready, z_ready, zo_ready = st.sem("g_ready"), st.sem("z_ready"), st.sem("zo_ready")
        stored = [st.sem(f"stored{q}") for q in range(2)]
        K_EXP, K_SIG, K_GATE, K_OUT = 2, 4, 6, 8
        DVE_STEPS = TC * 4 + 1

        def out_chunk(n):
            return cell_dram.rearrange("b t (h r) -> h b t r", h=2)[:, :, bass.ds(n * TC, TC), :]

        with nc.Block() as block:

            @block.sync
            def _(sp):
                src = rec_dram.rearrange("(b t) (x f) -> x b t f", b=B, f=REC)

                def load(n, q):
                    for x in range(2 * BL):
                        sp.dma_start(R[x * B:(x + 1) * B, q], src[x, :, bass.ds(n * TC, TC), :])\
                            .then_inc(rec_in[q], 16)

                def store(n, q):
                    sp.wait_ge(zo_ready, n + 1)
                    for h in range(2):
                        sp.dma_start(out_chunk(n)[h], zo[h * B:(h + 1) * B, q]).then_inc(stored[q], 16)

                sp.dma_start(sel[:], a["a_sel"]).then_inc(loaded, 16)
                for q in range(2):
                    sp.drain().then_inc(stored[q], 32)
                load(0, 0)
                with sp.Fori(0, NCH // 2 - 1) as i:
                    for q in range(2):
                        n = i * 2 + q
                        sp.wait_ge(sm_kept, n + 1)
                        load(n + 1, 1 - q)
                        store(n, q)
                n = NCH - 2
                sp.wait_ge(sm_kept, n + 1)
                load(n + 1, 1)
                store(n, 0)
                store(n + 1, 1)
                store(n + 2, 0)
                for q in range(2):
                    sp.wait_ge(stored[q], 32 * (NCH // 2 + (2 if q == 0 else 1)))

            def chunk_loop(eng, body):
                with eng.Fori(0, NCH // 2) as i:
                    for q in range(2):
                        body(i, q)

            @block.gpsimd
            def _(pool):
                g = nc.gpsimd
                g.memset(R[:, 1], 0.0)
                g.memset(read[:], 0.0)
                g.memset(sq[:], 0.0)
                g.memset(smc[:], 0.0)
                give(pool, zeroed, 1)

                def read_state(q, k):
                    row = R[:, q if k else 1 - q, (k - 1) % TC, Q:Q + NS]
                    g.tensor_tensor(read[:], S[:], row.unsqueeze(1).to_broadcast([P, HR, NS]), ALU.mult)\
                        .then_inc(read_ready, 1)

                def gate_1(n, pq, count):
                    g.tensor_tensor(g1[:], sq[:, pq].rearrange("p t r -> p (t r)"),
                                    sq[:, pq].rearrange("p t r -> p (t r)"), ALU.mult).then_inc(ret_step, 1)
                    pool.wait_ge(ret_step, n * 2 + 1)
                    g.tensor_tensor(g2[:].rearrange("p (t r) -> p t r", r=HR),
                                    g1[:].rearrange("p (t r) -> p t r", r=HR), bcast(smc[:, pq], HR), ALU.mult)\
                        .then_inc(ret_step, 1)
                    pool.wait_ge(ret_step, n * 2 + 2)

                def gate_2(n):
                    pool.wait_ge(sig_ready, n + 1)
                    g.tensor_tensor(g1[:], g2[:], sig[:], ALU.mult).then_inc(g_ready, 1)

                def body(i, q):
                    n = i * 2 + q
                    pool.wait_ge(rec_in[q], i * (16 * 2 * BL) + 16 * 2 * BL)
                    for k in range(TC):
                        pool.wait_ge(s_ready, n * TC + (k + 1))
                        g.tensor_tensor(decay[:], S[:], bcast(R[:, q, k, BE:BE + HR], NS), ALU.mult)\
                            .then_inc(decay_ready, 1)
                        read_state(q, k)
                        if k == K_EXP:
                            pool.wait_ge(z_ready, n + 1)
                            gate_1(n, 1 - q, n)
                        if k == K_GATE:
                            gate_2(n)
                pool.wait_ge(zeroed, 1)
                chunk_loop(pool, body)
                pool.wait_ge(s_ready, T + 1)
                read_state(0, 0)
                pool.wait_ge(sq_ready, T + 1)
                pool.wait_ge(z_ready, NCH + 1)
                gate_1(NCH, 1, NCH)
                gate_2(NCH)

            @block.vector
            def _(dve):
                v = nc.vector
                step = Chain(dve, step_sem)
                v.memset(S[:], 0.0).then_inc(s_ready, 1)
                dve.wait_ge(zeroed, 1)

                def reduce_read(q, k, count):
                    dve.wait_ge(read_ready, count)
                    dst = sq[:, q if k else 1 - q, (k - 1) % TC]
                    v.tensor_reduce(dst, read[:], AX, ALU.add).then_inc(sq_ready, 1)

                def sigmoid(n):
                    dve.wait_ge(ex_ready, n + 1)
                    step(v.tensor_scalar(ex[:], ex[:], 1.0, None, ALU.add))
                    v.reciprocal(sig[:], ex[:]).then_inc(sig_ready, 1)

                def body(i, q):
                    n = i * 2 + q
                    dve.wait_ge(rec_in[q], i * (16 * 2 * BL) + 16 * 2 * BL)
                    for k in range(TC):
                        kn = R[:, q, k, KN:KN + NS].unsqueeze(1).to_broadcast([P, HR, NS])
                        dve.wait_ge(s_ready, n * TC + (k + 1))
                        step(v.tensor_tensor(prod[:], S[:], kn, ALU.mult))
                        step(v.tensor_reduce(ret[:], prod[:], AX, ALU.add))
                        step(v.tensor_tensor(delta[:], R[:, q, k, V:V + HR], ret[:], ALU.subtract))
                        step(v.tensor_tensor(outer[:], bcast(delta[:], NS), kn, ALU.mult))
                        dve.wait_ge(decay_ready, n * TC + (k + 1))
                        v.tensor_tensor(pre[:], decay[:], outer[:], ALU.add).then_inc(pre_ready, 1)
                        reduce_read(q, k, n * TC + (k + 1))
                        if k == K_SIG:
                            sigmoid(n)
                        dve.wait_ge(keep_ready, n * TC + (k + 1))
                        dve.wait_ge(upd_ready, n * TC + (k + 1))
                        v.scalar_tensor_tensor(S[:], upd[:], R[:, q, k, WU:WU + 1], keep[:], ALU.mult, ALU.add)\
                            .then_inc(s_ready, 1)
                with dve.Fori(0, NCH // 2) as i:
                    step.loop(i, 2 * DVE_STEPS)
                    for q in range(2):
                        body(i, q)
                step.end(NCH // 2)
                reduce_read(0, 0, T + 1)
                sigmoid(NCH)

            @block.scalar
            def _(act):
                s = nc.scalar
                act.wait_ge(zeroed, 1)

                def exponent(n, pq, count):
                    act.wait_ge(sq_ready, count)
                    s.activation(ex[:], sq[:, pq].rearrange("p t r -> p (t r)"), ACT.Exp, scale=-1.0)\
                        .then_inc(ex_ready, 1)

                def out(i, n, q):
                    act.wait_ge(z_ready, n + 2)
                    act.wait_ge(stored[q], i * 32 + 32)
                    s.activation(zo[:, q].rearrange("p t r -> p (t r)"), psZ[:], ACT.Copy).then_inc(zo_ready, 1)

                def body(i, q):
                    n = i * 2 + q
                    act.wait_ge(rec_in[q], i * (16 * 2 * BL) + 16 * 2 * BL)
                    for k in range(TC):
                        act.wait_ge(s_ready, n * TC + (k + 1))
                        s.activation(keep[:], S[:], ACT.Copy, scale=R[:, q, k, OM:OM + 1]).then_inc(keep_ready, 1)
                        act.wait_ge(pre_ready, n * TC + (k + 1))
                        s.activation(upd[:], pre[:], ACT.Tanh).then_inc(upd_ready, 1)
                        if k == K_EXP:
                            exponent(n, 1 - q, n * TC + 1)
                        if k == K_OUT:
                            out(i, n, q)
                            s.activation(smc[:, q], R[:, q, :, SM:SM + 1].rearrange("p t f -> p (t f)"),
                                         ACT.Copy).then_inc(sm_kept, 1)
                chunk_loop(act, body)
                exponent(NCH, 1, T + 1)
                out(NCH // 2, NCH, 0)

            @block.tensor
            def _(pe):
                pe.wait_ge(loaded, 16)
                give(pe, z_ready, 1)

                def gather(n):
                    pe.wait_ge(g_ready, n + 1)
                    pe.wait_ge(zo_ready, n)
                    nc.tensor.matmul(psZ[:], sel[:], g1[:], start=True, stop=True).then_inc(z_ready, 1)
                pe.wait_ge(g_ready, 1)
                nc.tensor.matmul(psZ[:], sel[:], g1[:], start=True, stop=True).then_inc(z_ready, 1)
                with pe.Fori(1, NCH + 1) as n:
                    gather(n)

    with nc.cleanup_on_exit(), ExitStack() as ctx:
        st = Stage(nc, ctx, name + "o")
        cell = st.sb("cell", [P, 2, TPC, NS])
        cT = st.sb("cT", [NS, 2, CW])
        wout = st.sb("wout", [NS, D])
        psT = st.ps("psT", [NS, 2, CW])
        psY = st.ps("psY", [P, 2, TPC, D])
        loaded, cT_ready, cT_copied = st.sem("loaded"), st.sem("cT_ready"), st.sem("cT_copied")
        y_ready, x_updated = st.sem("y_ready"), st.sem("x_updated")
        cell_in = [st.sem(f"cell_in{q}") for q in range(2)]
        with nc.Block() as block:

            @block.sync
            def _(sp):
                sp.dma_start(wout[:], a["a_wout"]).then_inc(loaded, 16)
                src = cell_dram[:, TC:TC + T, :].rearrange("b (h p) r -> p b h r", p=P)
                with sp.Fori(0, NC // 2) as i:
                    for q in range(2):
                        c = i * 2 + q
                        sp.wait_ge(cT_ready, c + 1)
                        for x in range(2):
                            sp.dma_start(cell[:, q, 2 * x:2 * x + 2], src[:, bass.ds(c * 2 + x, 1)]
                                         .rearrange("p b h r -> p (b h) r")).then_inc(cell_in[q], 16)

            @block.tensor
            def _(pe):
                give(pe, cT_ready)
                pe.wait_ge(loaded, 16)
                with pe.Fori(0, NC // 2) as i:
                    for q in range(2):
                        c = i * 2 + q
                        pe.wait_ge(cell_in[q], i * 32 + 32)
                        for j in range(TPC):
                            last = nc.tensor.transpose(psT[:, q, j * P:(j + 1) * P], cell[:, q, j], ident[:])
                        last.then_inc(cT_ready, 1)
                        pe.wait_ge(cT_copied, c + 1)
                        pe.wait_ge(x_updated, c + 1)
                        for j in range(TPC):
                            last = nc.tensor.matmul(psY[:, q, j], cT[:, q, j * P:(j + 1) * P], wout[:],
                                                    start=True, stop=True)
                        last.then_inc(y_ready, 1)

            @block.scalar
            def _(act):
                with act.Fori(0, NC // 2) as i:
                    for q in range(2):
                        act.wait_ge(cT_ready, i * 2 + (q + 1 + AHEAD))
                        nc.scalar.activation(cT[:, q], psT[:, q], ACT.Copy).then_inc(cT_copied, 1)

            @block.vector
            def _(dve):
                give(dve, x_updated)
                with dve.Fori(0, NC // 2) as i:
                    for q in range(2):
                        c = i * 2 + q
                        dve.wait_ge(y_ready, c + 1)
                        tiles = bass.ds(c * TPC, TPC)
                        nc.vector.tensor_tensor(X[:, tiles, :], X[:, tiles, :], psY[:, q], ALU.add)\
                            .then_inc(x_updated, 1)


def lay_cell(i, a, rows):
    import numpy as np
    L = "L0_attn_a_"
    a["a_win"] = i[L + "W_in"].T
    kv = i[L + "W_kv"].reshape(4, 2, 32, D)
    a["a_wcat"] = np.concatenate([kv[:, 0].reshape(128, D), kv[:, 1].reshape(128, D), i[L + "W_beta"],
                                  i[L + "W_q"], i[L + "W_router"]]).T
    a["a_bbeta"] = rows(i[L + "b_beta"].reshape(-1))
    a["a_lower"] = rows(np.tril(np.ones((4, 4), np.float32), -1))
    a["a_sel"] = np.tile(np.eye(32, dtype=np.float32), (4, 1))
    a["a_wout"] = i[L + "W_out"].T


def load_stage(nc, name, x, X, ident=None):
    with nc.cleanup_on_exit(), ExitStack() as ctx:
        st = Stage(nc, ctx, name)
        loaded, made = st.sem("loaded"), st.sem("made")
        with nc.Block() as block:

            @block.sync
            def _(sp):
                sp.dma_start(X[:], x.rearrange("b (h p) d -> p (b h) d", p=P)).then_inc(loaded, 16)
                sp.wait_ge(loaded, 16)

            if ident is None:
                return

            @block.gpsimd
            def _(pool):
                pool.memset(ident[:], 0.0).then_inc(made, 1)
                pool.wait_ge(made, 1)
                pool.affine_select(out=ident[:], in_=ident[:], compare_op=ALU.not_equal, fill=1.0, base=0,
                                   pattern=[[-1, P]], channel_multiplier=1).then_inc(made, 1)


def relay_stage(nc, name, X, group):
    with nc.cleanup_on_exit(), ExitStack() as ctx:
        st = Stage(nc, ctx, name)
        moved = st.sem("moved")
        kept = nc.dram_tensor(f"{name}_x", (B * T, D), F32, kind="Internal").ap()
        near = kept.rearrange("(r p) d -> p r d", p=P)
        far = kept.rearrange("(s g j) d -> s j g d", s=B, j=8)
        with nc.Block() as block:

            def move(eng, store, spread, done):
                if not spread:
                    dram = near
                    if store:
                        eng.dma_start(dram, X[:]).then_inc(moved, 16)
                    else:
                        eng.dma_start(X[:], dram).then_inc(moved, 16)
                    return done + 16
                for s in range(B):
                    tile = X[s * 8:s * 8 + 8]
                    if store:
                        eng.dma_start(far[s], tile).then_inc(moved, 16)
                    else:
                        eng.dma_start(tile, far[s]).then_inc(moved, 16)
                return done + 16 * B

            @block.sync
            def _(sp):
                done = move(sp, True, not group, 0)
                sp.wait_ge(moved, done)
                done = move(sp, False, group, done)
                sp.wait_ge(moved, done)


def store_stage(nc, X, out):
    with nc.cleanup_on_exit(), ExitStack() as ctx:
        st = Stage(nc, ctx, "store")
        stored = st.sem("stored")
        with nc.Block() as block:

            @block.sync
            def _(sp):
                sp.dma_start(out.rearrange("b (h p) d -> p (b h) d", p=P), X[:]).then_inc(stored, 16)
                sp.wait_ge(stored, 16)


def program(nc, a, out):
    with ExitStack() as ctx:
        X = ctx.enter_context(nc.sbuf_tensor("x_resident", [P, NT, D], F32))
        ident = ctx.enter_context(nc.sbuf_tensor("ident", [P, P], F32))
        load_stage(nc, "load", a["x"], X, ident)
        n = 0
        for s in STAGES:
            n += 1
            if s == "f":
                ffn_stage(nc, f"ffn{n}", X, ident, a)
            if s == "c":
                relay_stage(nc, f"group{n}", X, True)
                attention_stage(nc, f"rows{n}", "c", X, None, ident, a)
                relay_stage(nc, f"ungroup{n}", X, False)
            if s == "b":
                with nc.sbuf_tensor(f"xa{n}", [P, NT, D], F32) as XA:
                    attention_stage(nc, f"cluster{n}", "b", X, XA, ident, a)
                    ffn_stage(nc, f"mlp{n}", X, ident, a, XA)
            if s == "d":
                attention_stage(nc, f"causal{n}", "d", X, None, ident, a)
            if s == "m":
                last = n == len(STAGES)
                dest = out.rearrange("b t d -> (b t) d") if last else \
                    nc.dram_tensor(f"x_after{n}", (B * T, D), F32, kind="Internal").ap()
                moe_stage(nc, f"moe{n}", X, ident, a, dest)
                if not last:
                    load_stage(nc, f"load{n}", dest.rearrange("(b t) d -> b t d", b=B), X)
            if s == "a":
                cell_stage(nc, f"cell{n}", X, ident, a)
        if STAGES[-1] != "m":
            store_stage(nc, X, out)


def laid_out(i):
    import numpy as np
    i = {k: np.asarray(v) for k, v in i.items()}
    rows = lambda v: np.ascontiguousarray(np.broadcast_to(v, (P,) + v.shape))
    L = "L0_ffn_"
    a = {"x": i["L0_attn_a_x"],
         "f_fc1": i[L + "fc1_q"], "f_fc1_s": rows(i[L + "fc1_scales"][0]), "f_b1": i[L + "fc1_bias"].reshape(-1, P).T,
         "f_fc2": i[L + "fc2_q"], "f_fc2_s": rows(i[L + "fc2_scales"]), "f_b2": rows(i[L + "fc2_bias"]),
         "f_gam": i[L + "ln_gamma"].reshape(P, 1), "f_bet": i[L + "ln_beta"].reshape(P, 1)}
    lay_more(i, a, rows)
    return a


def kernel(**inputs):
    import numpy as np
    import concourse.bacc as bacc
    from concourse.bass_utils import run_bass_kernel_spmd

    nc = bacc.Bacc("TRN2", target_bir_lowering=False, num_devices=1)
    arrays, aps = {}, {}
    for name, a in laid_out(inputs).items():
        a = np.ascontiguousarray(a)
        arrays[f"in_{name}"] = a
        aps[name] = nc.dram_tensor(f"in_{name}", a.shape, mybir.dt.from_np(a.dtype), kind="ExternalInput").ap()
    out = nc.dram_tensor("out_0", (B, T, D), F32, kind="ExternalOutput").ap()
    program(nc, aps, out)
    r = run_bass_kernel_spmd(nc, [arrays], core_ids=[0])
    return r.results[0]["out_0"]
```

```python
from contextlib import ExitStack

import concourse.bass as bass
from concourse import mybir

F32 = mybir.dt.float32
I32 = mybir.dt.int32
U32 = mybir.dt.uint32
ALU = mybir.AluOpType
ACT = mybir.ActivationFunctionType
AX = mybir.AxisListType.X

P = 128
D = 128
B, T = 16, 256
NT = B * T // P
TPC = 4
NC = NT // TPC
CW = TPC * P
OUTER_EPS = 1e-5
NEG = -2.0 ** 100


class Chain:

    def __init__(self, eng, sem):
        self.eng, self.sem, self.base, self.k = eng, sem, 0, 0
        self.i, self.per = None, 0

    def loop(self, i, per):
        self.base, self.k, self.i, self.per = self.base + self.k, 0, i, per

    def end(self, trips):
        assert self.k == self.per, (self.k, self.per)
        self.base, self.k, self.i = self.base + trips * self.per, 0, None

    def value(self):
        if self.i is None:
            return self.base + self.k
        return self.i * self.per + (self.base + self.k)

    def __call__(self, ins):
        ins.then_inc(self.sem, 1)
        self.k += 1
        self.eng.wait_ge(self.sem, self.value())


class Stage:

    def __init__(self, nc, ctx, name):
        self.nc, self.ctx, self.name = nc, ctx, name

    def sb(self, name, shape, dt=F32):
        return self.ctx.enter_context(self.nc.sbuf_tensor(f"{self.name}_{name}", shape, dt))

    def ps(self, name, shape, dt=F32):
        return self.ctx.enter_context(self.nc.psum_tensor(f"{self.name}_{name}", shape, dt))

    def sem(self, name):
        return self.nc.alloc_semaphore(f"{self.name}_{name}")


class Norm:

    def __init__(self, st, inner_eps=None, eps=OUTER_EPS):
        self.inner_eps, self.eps = inner_eps, eps
        self.bn = st.sb("bn", [P, NT, 6])
        self.mean = st.sb("mean", [P, NT])
        self.var = st.sb("var", [P, NT])
        self.tmp = st.sb("normtmp", [P, NT])
        self.std = st.sb("std", [P, NT])
        self.rstd = st.sb("rstd", [P, NT])
        self.rboth = st.sb("rboth", [P, NT])
        self.var_ready = st.sem("var_ready")
        self.std_ready = st.sem("std_ready")

    def act(self, nc, act):
        for n in range(1 if self.inner_eps is None else 2):
            act.wait_ge(self.var_ready, n + 1)
            nc.scalar.activation(self.std[:], self.tmp[:], ACT.Sqrt).then_inc(self.std_ready, 1)

    def dve(self, nc, dve, chain, X):
        v = nc.vector
        with dve.Fori(0, NC) as i:
            chain.loop(i, 1)
            for j in range(TPC):
                last = v.bn_stats(self.bn[:, bass.ds(i * TPC + j, 1), :], X[:, bass.ds(i * TPC + j, 1), :])
            chain(last)
        chain.end(NC)
        bn = self.bn
        chain(v.tensor_tensor(self.mean[:], bn[:, :, 1], bn[:, :, 4], ALU.add))
        chain(v.tensor_scalar(self.mean[:], self.mean[:], 0.5, None, ALU.mult))
        chain(v.tensor_tensor(self.tmp[:], bn[:, :, 1], bn[:, :, 4], ALU.subtract))
        chain(v.tensor_tensor(self.tmp[:], self.tmp[:], self.tmp[:], ALU.mult))
        chain(v.tensor_tensor(self.var[:], bn[:, :, 2], bn[:, :, 5], ALU.add))
        chain(v.scalar_tensor_tensor(self.var[:], self.tmp[:], D / 4.0, self.var[:], ALU.mult, ALU.add))
        chain(v.tensor_scalar(self.var[:], self.var[:], 1.0 / D, None, ALU.mult))
        v.tensor_scalar(self.tmp[:], self.var[:], self.eps, None, ALU.add).then_inc(self.var_ready, 1)
        dve.wait_ge(self.std_ready, 1)
        chain(v.reciprocal(self.rstd[:], self.std[:]))
        if self.inner_eps is not None:
            chain(v.tensor_tensor(self.var[:], self.var[:], self.rstd[:], ALU.mult))
            chain(v.tensor_tensor(self.var[:], self.var[:], self.rstd[:], ALU.mult))
            v.tensor_scalar(self.tmp[:], self.var[:], self.inner_eps, None, ALU.add)\
                .then_inc(self.var_ready, 1)
            dve.wait_ge(self.std_ready, 2)
            chain(v.reciprocal(self.rboth[:], self.std[:]))
            chain(v.tensor_tensor(self.rboth[:], self.rboth[:], self.rstd[:], ALU.mult))


def bcast(ap, n):
    return ap.unsqueeze(2).to_broadcast([ap.shape[0], ap.shape[1], n])

STAGES = "afbfcmdm"


def normalise_loop(nc, pool, X, norm, tmp, xn, xn_free, xn_ready, res=None, res_free=None):
    g = nc.gpsimd
    r = norm.rstd if norm.inner_eps is None else norm.rboth
    step = Chain(pool, tmp[1])
    tmp = tmp[0]
    with pool.Fori(0, NC // 2) as i:
        step.loop(i, 2)
        for q in range(2):
            c = i * 2 + q
            tiles = bass.ds(c * TPC, TPC)
            pool.wait_ge(xn_free, c + 1)
            step(g.tensor_tensor(tmp[:, q], X[:, tiles, :], bcast(norm.mean[:, tiles], D), ALU.subtract))
            if res is not None:
                pool.wait_ge(res_free, c + 1)
                g.tensor_tensor(res[:, q], tmp[:, q], bcast(norm.rstd[:, tiles], D), ALU.mult)
            g.tensor_tensor(xn[:, q], tmp[:, q], bcast(r[:, tiles], D), ALU.mult).then_inc(xn_ready, 1)
    step.end(NC // 2)


AHEAD = 2


def give(eng, sem, n=AHEAD):
    for _ in range(n):
        eng.drain().then_inc(sem, 1)


def ffn_stage(nc, name, X, ident, a, XA=None):
    quantised = XA is None
    source = X if quantised else XA
    pre = "f_" if quantised else "b_mlp_"
    F = a[pre + "fc1"].shape[1]
    FM = F // P
    with nc.cleanup_on_exit(), ExitStack() as ctx:
        st = Stage(nc, ctx, name)
        norm = Norm(st, 1e-5) if quantised else Norm(st, None, 1e-6)
        w1q = st.sb("w1q", [P, F], I32)
        w1s = st.sb("w1s", [P, F])
        w1 = st.sb("w1", [P, F])
        w2q = st.sb("w2q", [P, FM, D], I32)
        w2s = st.sb("w2s", [P, FM, D])
        w2 = st.sb("w2", [P, FM, D])
        b1 = st.sb("b1", [P, FM])
        b2 = st.sb("b2", [P, D])
        gam = st.sb("gam", [P, 1])
        bet = st.sb("bet", [P, 1])
        tmp = st.sb("tmp", [P, 2, TPC, D])
        xn = st.sb("xn", [P, 2, TPC, D])
        res = st.sb("res", [P, 2, TPC, D])
        hT = st.sb("hT", [P, 2, CW])
        yT = st.sb("yT", [P, 2, FM, CW])
        upd = st.sb("upd", [P, TPC, D])
        psT = st.ps("psT", [P, CW])
        psA = st.ps("psA", [P, FM, CW])
        psZ = st.ps("psZ", [P, 2, TPC, D])
        loaded = st.sem("loaded")
        dve_step = st.sem("dve_step")
        pool_step = st.sem("pool_step")
        stats_done = st.sem("stats_done")
        weights_ready = st.sem("weights_ready")
        xn_ready, x_updated = st.sem("xn_ready"), st.sem("x_updated")
        xT_ready, h_ready = st.sem("xT_ready"), st.sem("h_ready")
        a_ready = st.sem("a_ready")
        y_ready = st.sem("y_ready")
        z_ready = st.sem("z_ready")
        LOADED = 16 * (8 if quantised else 6)
        with nc.Block() as block:

            @block.sync
            def _(sp):
                loads = [(b1[:], a[pre + "b1"]), (b2[:], a[pre + "b2"]), (gam[:], a[pre + "gam"]),
                         (bet[:], a[pre + "bet"])]
                w2_in = a[pre + "fc2"].rearrange("(m p) d -> p m d", p=P)
                if quantised:
                    loads += [(w1q[:], a["f_fc1"]), (w1s[:], a["f_fc1_s"]), (w2q[:], w2_in),
                              (w2s[:], a["f_fc2_s"])]
                else:
                    loads += [(w1[:], a[pre + "fc1"]), (w2[:], w2_in)]
                for dst, src in loads:
                    sp.dma_start(dst, src).then_inc(loaded, 16)

            @block.gpsimd
            def _(pool):
                pool.wait_ge(stats_done, 1)
                normalise_loop(nc, pool, source, norm, (tmp, pool_step), xn, xT_ready, xn_ready,
                               res if quantised else None, x_updated)

            @block.vector
            def _(dve):
                v = nc.vector
                step = Chain(dve, dve_step)
                give(dve, x_updated)
                norm.dve(nc, dve, step, source)
                give(dve, stats_done, 1)
                dve.wait_ge(loaded, LOADED)
                if quantised:
                    step(v.tensor_scalar(w1[:], w1q[:], -128.0, None, ALU.add))
                    v.tensor_tensor(w1[:], w1[:], w1s[:], ALU.mult)
                    step(v.tensor_scalar(w2[:], w2q[:], -128.0, None, ALU.add))
                    step(v.tensor_tensor(w2[:], w2[:], w2s[:], ALU.mult))
                    step(v.tensor_scalar(b2[:], b2[:], 0.5, None, ALU.mult))
                give(dve, weights_ready, 1)
                with dve.Fori(0, NC // 2) as i:
                    step.loop(i, 2)
                    for q in range(2):
                        c = i * 2 + q
                        tiles = bass.ds(c * TPC, TPC)
                        dve.wait_ge(z_ready, c + 1)
                        v.scalar_tensor_tensor(upd[:], psZ[:, q], 0.5 if quantised else 1.0,
                                               res[:, q] if quantised else XA[:, tiles, :], ALU.mult, ALU.add)
                        step(v.tensor_tensor(X[:, tiles, :], X[:, tiles, :],
                                             b2[:].unsqueeze(1).to_broadcast([P, TPC, D]), ALU.add))
                        v.tensor_tensor(X[:, tiles, :], X[:, tiles, :], upd[:], ALU.add).then_inc(x_updated, 1)
                        dve.wait_ge(x_updated, c + (1 + AHEAD))
                step.end(NC // 2)

            @block.scalar
            def _(act):
                norm.act(nc, act)
                act.wait_ge(loaded, LOADED)
                with act.Fori(0, NC // 2) as i:
                    for q in range(2):
                        c = i * 2 + q
                        act.wait_ge(xT_ready, c + (1 + AHEAD))
                        nc.scalar.activation(hT[:, q], psT[:], ACT.Identity, bias=bet[:], scale=gam[:])\
                            .then_inc(h_ready, 1)
                        for m in range(FM):
                            act.wait_ge(a_ready, c * FM + (m + 1))
                            nc.scalar.activation(yT[:, q, m], psA[:, m], ACT.Silu if quantised else ACT.Relu, bias=b1[:, m:m + 1])\
                                .then_inc(y_ready, 1)

            @block.tensor
            def _(pe):
                give(pe, xT_ready)
                pe.wait_ge(weights_ready, 1)
                with pe.Fori(0, NC // 2) as i:
                    for q in range(2):
                        c = i * 2 + q
                        pe.wait_ge(xn_ready, c + 1)
                        for j in range(TPC):
                            last = nc.tensor.transpose(psT[:, j * P:(j + 1) * P], xn[:, q, j], ident[:])
                        last.then_inc(xT_ready, 1)
                        pe.wait_ge(h_ready, c + 1)
                        for m in range(FM):
                            nc.tensor.matmul(psA[:, m], w1[:, m * P:(m + 1) * P], hT[:, q],
                                             start=True, stop=True).then_inc(a_ready, 1)
                        pe.wait_ge(y_ready, (c + 1) * FM)
                        pe.wait_ge(x_updated, c + 1)
                        for j in range(TPC):
                            for m in range(FM):
                                last = nc.tensor.matmul(psZ[:, q, j], yT[:, q, m, j * P:(j + 1) * P], w2[:, m],
                                                        start=(m == 0), stop=(m == FM - 1))
                        last.then_inc(z_ready, 1)


def transpose_chunk(nc, pe, psT, xn_q, ident):
    for j in range(TPC):
        last = nc.tensor.transpose(psT[:, j * P:(j + 1) * P], xn_q[:, j], ident[:])
    return last


def moe_stage(nc, name, X, ident, a, dest):
    E, S, _, M = a["m_w1"].shape
    K = D // S
    CAP = P
    assert 3 * B * T // 2 // E == CAP
    HALF = B * T // 2
    NB = 6
    FETCH = 4
    H1 = 64
    R = H1 + E
    dest_tiles = dest.rearrange("(r p) d -> p r d", p=P)
    with ExitStack() as outer:
        so = Stage(nc, outer, name)
        xn_dram = nc.dram_tensor(f"{name}_xn", (B * T, D), F32, kind="Internal").ap()
        xn_tiles = xn_dram.rearrange("(r p) d -> p r d", p=P)
        tok = so.sb("tok", [P, E], U32)
        wgt = so.sb("wgt", [P, E])

        with nc.cleanup_on_exit(), ExitStack() as ctx:
            st = Stage(nc, ctx, name + "r")
            norm = Norm(st)
            tmp = st.sb("tmp", [P, 2, TPC, D])
            xn = st.sb("xn", [P, 2, TPC, D])
            xT = st.sb("xT", [P, 2, CW])
            wr = st.sb("wr", [P, E])
            score = st.sb("score", [R, HALF])
            best = st.sb("best", [R, CAP])
            at = st.sb("at", [R, CAP], U32)
            atf = st.sb("atf", [R, CAP])
            best1 = st.sb("best1", [E, CAP])
            at1 = st.sb("at1", [E, CAP])
            own = st.sb("own", [E, CAP])
            top = st.sb("top", [E, CAP])
            chosen = st.sb("chosen", [E, CAP])
            stat = st.sb("stat", [E, 4])
            psT = st.ps("psT", [P, 2, CW])
            psS = st.ps("psS", [P, 2, CW])
            psO = st.ps("psO", [P, 2, E])
            loaded, dve_step, pool_step = st.sem("loaded"), st.sem("dve_step"), st.sem("pool_step")
            stats_done, xn_ready, xn_kept = st.sem("stats_done"), st.sem("xn_ready"), [st.sem(f"xn_kept{q}") for q in range(2)]
            xT_ready, xT_copied, s_ready, s_copied = (st.sem("xT_ready"), st.sem("xT_copied"),
                                                      st.sem("s_ready"), st.sem("s_copied"))
            lists_ready, moved = st.sem("lists_ready"), st.sem("moved")
            top_ready, exp_ready, w_ready, out_ready = (st.sem("top_ready"), st.sem("exp_ready"),
                                                        st.sem("w_ready"), st.sem("out_ready"))
            with nc.Block() as block:

                @block.sync
                def _(sp):
                    sp.dma_start(wr[:], a["m_wr"]).then_inc(loaded, 16)
                    sp.dma_start(dest_tiles, X[:]).then_inc(loaded, 16)
                    sp.wait_ge(lists_ready, 1)
                    sp.dma_start(best1[:], best[H1:R, :]).then_inc(moved, 16)
                    sp.dma_start(at1[:], atf[H1:R, :]).then_inc(moved, 16)
                    sp.wait_ge(moved, 32)
                    sp.wait_ge(loaded, 32)

                @block.gpsimd
                def _(pool):
                    g = nc.gpsimd
                    pool.wait_ge(stats_done, 1)
                    step = Chain(pool, pool_step)
                    with pool.Fori(0, NC // 2) as i:
                        step.loop(i, 2)
                        for q in range(2):
                            c = i * 2 + q
                            tiles = bass.ds(c * TPC, TPC)
                            pool.wait_ge(xT_ready, c + 1)
                            pool.wait_ge(xn_kept[q], i * 16 + 16)
                            step(g.tensor_tensor(tmp[:, q], X[:, tiles, :], bcast(norm.mean[:, tiles], D),
                                                 ALU.subtract))
                            g.tensor_tensor(xn[:, q], tmp[:, q], bcast(norm.rstd[:, tiles], D), ALU.mult)\
                                .then_inc(xn_ready, 1)
                    step.end(NC // 2)

                @block.scalar
                def _(act):
                    norm.act(nc, act)
                    for q in range(2):
                        act.drain().then_inc(xn_kept[q], 16)
                    with act.Fori(0, NC // 2) as i:
                        for q in range(2):
                            c = i * 2 + q
                            act.wait_ge(xn_ready, c + 1)
                            act.dma_start(xn_tiles[:, bass.ds(c * TPC, TPC), :], xn[:, q])\
                                .then_inc(xn_kept[q], 16)
                            act.wait_ge(xT_ready, c + (1 + AHEAD))
                            nc.scalar.activation(xT[:, q], psT[:, q], ACT.Copy).then_inc(xT_copied, 1)
                    for q in range(2):
                        act.wait_ge(xn_kept[q], 16 * (NC // 2 + 1))
                    act.wait_ge(top_ready, 1)
                    nc.scalar.activation(own[:], top[:], ACT.Exp, bias=stat[:, 0:1],
                                         accum_out=stat[:, 1:2]).then_inc(exp_ready, 1)

                @block.vector
                def _(dve):
                    v = nc.vector
                    step = Chain(dve, dve_step)
                    norm.dve(nc, dve, step, X)
                    give(dve, stats_done, 1)
                    step(v.memset(score[:], 0.0))
                    for h in range(2):
                        with dve.Fori(0, NC // 4) as i:
                            step.loop(i, 2)
                            for q in range(2):
                                c = i * 2 + (q + h * NC // 2)
                                dve.wait_ge(s_ready, c + 1)
                                rows = slice(H1 * h, H1 * h + E)
                                step(v.tensor_copy(score[rows, bass.ds(i * (2 * CW) + q * CW, CW)],
                                                   psS[rows, q]))
                        step.end(NC // 4)
                    for k in range(CAP // 8):
                        eight = slice(8 * k, 8 * k + 8)
                        step(v.max(best[:, eight], score[:]))
                        step(v.max_index(at[:, eight], best[:, eight], score[:]))
                        step(v.match_replace(score[:], best[:, eight], score[:], -3.0e38))
                    step(v.tensor_copy(atf[:], at[:]))
                    step(v.tensor_scalar(atf[H1:R], atf[H1:R], float(HALF), None, ALU.add))
                    give(dve, lists_ready, 1)
                    dve.wait_ge(moved, 32)
                    step(v.tensor_tensor(top[:], best[0:E], best1[:, ::-1], ALU.max))
                    step(v.tensor_tensor(own[:], best[0:E], best1[:, ::-1], ALU.is_ge))
                    step(v.tensor_tensor(chosen[:], atf[0:E], at1[:, ::-1], ALU.subtract))
                    step(v.tensor_tensor(chosen[:], chosen[:], own[:], ALU.mult))
                    step(v.tensor_tensor(chosen[:], chosen[:], at1[:, ::-1], ALU.add))
                    step(v.tensor_reduce(stat[:, 2:3], top[:], AX, ALU.max))
                    v.tensor_scalar(stat[:, 0:1], stat[:, 2:3], -1.0, None, ALU.mult).then_inc(top_ready, 1)
                    dve.wait_ge(exp_ready, 1)
                    step(v.reciprocal(stat[:, 3:4], stat[:, 1:2]))
                    v.tensor_scalar(top[:], own[:], stat[:, 3:4], None, ALU.mult).then_inc(w_ready, 1)
                    dve.wait_ge(out_ready, 1)
                    v.tensor_copy(tok[:], psO[:, 0])
                    v.tensor_copy(wgt[:], psO[:, 1])

                @block.tensor
                def _(pe):
                    give(pe, xT_ready)
                    pe.wait_ge(loaded, 32)
                    for h in range(2):
                        with pe.Fori(0, NC // 4) as i:
                            for q in range(2):
                                c = i * 2 + (q + h * NC // 2)
                                pe.wait_ge(xn_ready, c + 1)
                                transpose_chunk(nc, pe, psT[:, q], xn[:, q], ident).then_inc(xT_ready, 1)
                                pe.wait_ge(xT_copied, c + 1)
                                pe.wait_ge(dve_step, c + norm_steps(False))
                                nc.tensor.matmul(psS[H1 * h:H1 * h + E, q], wr[:], xT[:, q], start=True,
                                                 stop=True).then_inc(s_ready, 1)
                    pe.wait_ge(w_ready, 1)
                    nc.tensor.transpose(psO[:, 0], chosen[:], ident[0:E, 0:E])
                    nc.tensor.transpose(psO[:, 1], top[:], ident[0:E, 0:E]).then_inc(out_ready, 1)

        with nc.cleanup_on_exit(), ExitStack() as ctx:
            st = Stage(nc, ctx, name + "e")
            w1 = st.sb("w1", [P, NB, S, M])
            w2 = st.sb("w2", [P, NB, S, K])
            b1 = st.sb("b1", [P, E, S])
            b2 = st.sb("b2", [1, E * D])
            ones = st.sb("ones", [1, P])
            carrier = st.sb("carrier", [1, 2 * NB])
            tokc = st.sb("tokc", [P, NB], U32)
            xg = st.sb("xg", [P, NB, D])
            xgT = st.sb("xgT", [P, NB, P])
            pre = st.sb("pre", [P, 2, S, P])
            hT = st.sb("hT", [P, 2, S, P])
            y = st.sb("y", [P, NB, D])
            psX = st.ps("psX", [P, 2, 512])
            psH = st.ps("psH", [P, 2, S, P])
            psY = st.ps("psY", [P, 2, 512])
            loaded = st.sem("loaded")
            w_loaded = [st.sem(f"w_loaded{q}") for q in range(NB)]
            gathered = [st.sem(f"gathered{q}") for q in range(NB)]
            added, tok_ready = st.sem("added"), st.sem("tok_ready")
            g_turned, g_copied = st.sem("g_turned"), st.sem("g_copied")
            h_ready, pre_ready, act_ready = st.sem("h_ready"), st.sem("pre_ready"), st.sem("act_ready")
            o_ready, y_ready, made = st.sem("o_ready"), st.sem("y_ready"), st.sem("made")

            def loop(eng, body, ahead=0, peel=0):
                for e in range(peel):
                    body(e, e % NB, True)
                with eng.Fori(0, (E - peel) // NB - 1) as i:
                    for q in range(NB):
                        body(i * NB + (peel + q), q, True)
                for e in range(E - NB, E):
                    body(e, e % NB, e + ahead < E)

            with nc.Block() as block:

                @block.sync
                def _(sp):
                    sp.dma_start(b1[:], a["m_b1"]).then_inc(loaded, 16)
                    sp.dma_start(b2[:], a["m_b2"]).then_inc(loaded, 16)

                    def load(e, q, more):
                        sp.wait_ge(o_ready, e + 1)
                        sp.dma_start(w1[:, q], a["m_w1"][bass.ds(e, 1)].rearrange("e s d m -> d (e s) m"))\
                            .then_inc(w_loaded[q], 16)
                        sp.dma_start(w2[:, q], a["m_w2"][bass.ds(e, 1)].rearrange("e s m k -> m (e s) k"))\
                            .then_inc(w_loaded[q], 16)
                    loop(sp, load)

                @block.gpsimd
                def _(pool):
                    g = nc.gpsimd

                    def gather(e, q):
                        pool.wait_ge(g_turned, e + 1)
                        g.tensor_copy(tokc[:, q:q + 1], tok[:, bass.ds(e, 1)]).then_inc(tok_ready, 1)
                        pool.wait_ge(tok_ready, e + 1)
                        g.tensor_tensor(carrier[:, q:q + 1], ident[0:1, 0:1], ident[0:1, 0:1], ALU.mult)
                        g.indirect_dma_start(out=xg[:, q], out_offset=None, in_=xn_dram[:, :],
                                             in_offset=bass.IndirectOffsetOnAxis(ap=tokc[:, q:q + 1], axis=0))\
                            .then_inc(gathered[q], 16)

                    def body(e, q, more):
                        if more:
                            gather(e + FETCH, (q + FETCH) % NB)
                        pool.wait_ge(y_ready, e + (1 + NB))
                        if not isinstance(e, int) or e > 0:
                            pool.wait_ge(added, e * 16)
                        g.tensor_tensor(carrier[:, NB + q:NB + q + 1], ident[0:1, 0:1], ident[0:1, 0:1], ALU.mult)
                        g.indirect_dma_start(out=dest[:, :], in_=y[:, q], in_offset=None,
                                             out_offset=bass.IndirectOffsetOnAxis(ap=tokc[:, q:q + 1], axis=0),
                                             compute_op=ALU.add).then_inc(added, 16)

                    for e in range(FETCH):
                        gather(e, e)
                    loop(pool, body, ahead=FETCH, peel=NB)
                    pool.wait_ge(added, 16 * E)

                @block.scalar
                def _(act):
                    def body(e, q, more):
                        act.wait_ge(g_turned, e + (1 + NB))
                        nc.scalar.activation(xgT[:, q], psX[:, q % 2, 0:P], ACT.Copy).then_inc(g_copied, 1)
                        act.wait_ge(pre_ready, e + 1)
                        nc.scalar.activation(hT[:, q % 2], pre[:, q % 2], ACT.Gelu).then_inc(act_ready, 1)
                    loop(act, body)

                @block.vector
                def _(dve):
                    v = nc.vector
                    v.memset(ones[:], 1.0).then_inc(made, 1)
                    give(dve, y_ready, NB)
                    dve.wait_ge(loaded, 32)

                    def body(e, q, more):
                        dve.wait_ge(h_ready, e + 1)
                        v.tensor_tensor(pre[:, q % 2], psH[:, q % 2],
                                        b1[:, bass.ds(e, 1), :].rearrange("p a s -> p (a s)").unsqueeze(2)
                                        .to_broadcast([P, S, P]), ALU.add).then_inc(pre_ready, 1)
                        dve.wait_ge(o_ready, e + (1 + NB))
                        v.tensor_scalar(y[:, q], psY[:, q % 2, 0:D], wgt[:, bass.ds(e, 1)], None, ALU.mult)\
                            .then_inc(y_ready, 1)
                    loop(dve, body)

                @block.tensor
                def _(pe):
                    give(pe, g_turned, NB)
                    give(pe, o_ready, NB)
                    pe.wait_ge(made, 1)
                    pe.wait_ge(loaded, 32)

                    def turn(e, q, i):
                        pe.wait_ge(gathered[q], i * 16 + 16)
                        nc.tensor.transpose(psX[:, q % 2, 0:P], xg[:, q], ident[:]).then_inc(g_turned, 1)

                    def up(e, q, i):
                        pe.wait_ge(g_copied, e + 1)
                        pe.wait_ge(w_loaded[q], i * 32 + 32)
                        for s in range(S):
                            last = nc.tensor.matmul(psH[:, q % 2, s], w1[:, q, s], xgT[:, q],
                                                    start=True, stop=True)
                        last.then_inc(h_ready, 1)

                    def down(e, q):
                        pe.wait_ge(act_ready, e + 1)
                        nc.tensor.matmul(psY[:, q % 2, 0:D], ones[:], b2[:, bass.ds(e * D, D)],
                                         start=True, stop=False)
                        for s in range(S):
                            last = nc.tensor.matmul(psY[:, q % 2, s * K:(s + 1) * K], hT[:, q % 2, s],
                                                    w2[:, q, s], start=False, stop=(s == S - 1))
                        last.then_inc(o_ready, 1)

                    def body(e, q, i):
                        turn(e + 2, (q + 2) % NB, i + (q + 2) // NB)
                        up(e + 1, (q + 1) % NB, i + (q + 1) // NB)
                        down(e, q)

                    turn(0, 0, 0)
                    turn(1, 1, 0)
                    up(0, 0, 0)
                    with pe.Fori(0, E // NB - 1) as i:
                        for q in range(NB):
                            body(i * NB + q, q, i)
                    for e in range(E - NB, E):
                        if e + 2 < E:
                            turn(e + 2, (e + 2) % NB, (e + 2) // NB)
                        if e + 1 < E:
                            up(e + 1, (e + 1) % NB, (e + 1) // NB)
                        down(e, e % NB)


def norm_steps(twice):
    return NC + 8 + (4 if twice else 0)


def lay_more(i, a, rows):
    import numpy as np
    L = "L1_ffn_"
    a["m_wr"] = i[L + "Wr"].T
    a["m_w1"] = i[L + "W1"]
    a["m_w2"] = i[L + "W2"]
    a["m_b1"] = i[L + "b1"].transpose(2, 0, 1)
    a["m_b2"] = i[L + "b2"].reshape(1, -1)
    lay_attn(i, a, rows)
    lay_cell(i, a, rows)


def attention_stage(nc, name, kind, X, XA, ident, a):
    H, DH = 16, 8
    W = {"b": 256, "c": 64, "d": 32}[kind]
    NB = 32
    HPB = max(1, P // W)
    BPH = max(1, W // P)
    NG = H * W // P
    PAIR = 2
    N = NT // PAIR
    SCALE = float(DH) ** -0.5
    widths = {"b": [256, 256], "c": [128, 128], "d": [128, 256]}[kind]
    units = []
    for t in range(PAIR):
        kw = widths[t]
        for h in range(0, H, 512 // kw):
            units.append((t, h, 512 // kw, kw, t * P if kind == "c" else 0))
    U = len(units)
    PW = {"b": NB + DH, "c": DH, "d": 4}[kind]
    assert 6 * PW <= W
    BPB = min(NG, 8)
    QG = NG // BPB
    affine = kind in "bc"
    with nc.cleanup_on_exit(), ExitStack() as ctx:
        st = Stage(nc, ctx, name)
        norm = Norm(st, {"b": 1e-6, "c": 1e-5, "d": None}[kind])
        tmp = st.sb("tmp", [P, 2, PAIR, D])
        xn = st.sb("xn", [P, 2, PAIR, D])
        res = st.sb("res", [P, 2, PAIR, D])
        rtmp = st.sb("rtmp", [P, 2, PAIR, D])
        carrier = st.sb("carrier", [1, 4])
        wqkv = st.sb("wqkv", [P, 3 * D])
        wo = st.sb("wo", [P, D])
        bqkv = st.sb("bqkv", [P, 3 * D])
        bo = st.sb("bo", [P, D])
        gam = st.sb("gam", [P, 1])
        bet = st.sb("bet", [P, 1])
        hT = st.sb("hT", [P, PAIR, P])
        qkv = st.sb("qkv", [P, 2, PAIR, 3 * D])
        BF16 = mybir.dt.bfloat16
        slots = st.sb("slots", [P, PAIR, 2, H * W], BF16)
        turned = st.sb("turned", [P, 2, 2, NG, PAIR * P], BF16)
        prob = st.sb("prob", [P, 2, 512])
        probT = st.sb("probT", [P, 2, 4, P])
        nmax = st.sb("nmax", [P, PAIR, H])
        total = st.sb("total", [P, 2, PAIR, H])
        inv = st.sb("inv", [P, PAIR, H])
        o = st.sb("o", [P, PAIR, D])
        oT = st.sb("oT", [P, PAIR, P])
        upd = st.sb("upd", [P, PAIR, D])
        if kind == "b":
            wcl = st.sb("wcl", [P, 2, H * NB])
            wh = st.sb("wh", [P, 2, H * NB])
            wT = st.sb("wT", [P, 2, P])
            cl = st.sb("cl", [P, H, NB])
            ce = st.sb("ce", [P, H, NB])
            cm = st.sb("cm", [P, 2, H])
        if kind == "c":
            group = st.sb("group", [P, 2, 8])
        whole = st.sb("whole", [P, PAIR, 2, H * PW])
        one = st.sb("one", [P, 1])
        ident16 = st.sb("ident16", [P, P], BF16)
        if kind == "d":
            rot = st.sb("rot", [P, 2, PAIR, 2, 4])
            maskf = st.sb("maskf", [P, 2 * P])
            causal = st.sb("causal", [P, 2 * P], BF16)
            ra = st.sb("ra", [P, 2, H * 4])
            rb = st.sb("rb", [P, 2, H * 4])
        psS = st.ps("psS", [P, 2, 512])
        psT = st.ps("psT", [P, 2, 4, P])
        psP = st.ps("psP", [P, 512])
        psO = st.ps("psO", [P, PAIR, 512])
        psF = st.ps("psF", [P, 4, P])
        loaded, dve_step, pool_step = st.sem("loaded"), st.sem("dve_step"), st.sem("pool_step")
        stats_done, const_ready, slots_zero = st.sem("stats_done"), st.sem("const_ready"), st.sem("slots_zero")
        xn_ready, xT_ready, h_ready = st.sem("xn_ready"), st.sem("xT_ready"), st.sem("h_ready")
        proj_ready, prep_done = st.sem("proj_ready"), st.sem("prep_done")
        cl_ready, cl_exp = st.sem("cl_ready"), st.sem("cl_exp")
        q_slotted, k_slotted = st.sem("q_slotted"), st.sem("k_slotted")
        qt_ready, qt_copied = st.sem("qt_ready"), st.sem("qt_copied")
        s_ready, m_ready, p_ready = st.sem("s_ready"), st.sem("m_ready"), st.sem("p_ready")
        t_ready, pt_ready, av_done = st.sem("t_ready"), st.sem("pt_ready"), st.sem("av_done")
        o_ready, oT_ready, oT_copied = st.sem("o_ready"), st.sem("oT_ready"), st.sem("oT_copied")
        out_ready, x_updated = st.sem("out_ready"), st.sem("x_updated")
        res_ready, filled = st.sem("res_ready"), st.sem("filled")
        wT_ready, wT_copied, wcl_made = st.sem("wT_ready"), st.sem("wT_copied"), st.sem("wcl_made")
        loads = [(wqkv[:], a[kind + "_wqkv"]), (wo[:], a[kind + "_wo"])]
        if kind in "cd":
            loads += [(bqkv[:], a[kind + "_bqkv"]), (bo[:], a[kind + "_bo"])]
        if affine:
            loads += [(gam[:], a[kind + "_gam"]), (bet[:], a[kind + "_bet"])]
        if kind == "b":
            loads += [(wh[:], a["b_wh"])]
        if kind == "c":
            loads += [(group[:], a["c_group"])]
        if kind == "d":
            loads += [(rot[:], a["d_rot"]), (maskf[:], a["d_mask"])]
        LOADED = 16 * len(loads)
        PER_PAIR = PAIR + 1 + {"b": PAIR * 7, "c": 1, "d": 0}[kind]
        PREP = 3 if kind == "b" else 1
        SIDES = PAIR * 2 * QG
        X_AT, PROJ_AT = 0, 1
        TURN_AT = {"b": PROJ_AT + PAIR * PREP, "c": 3, "d": 7}[kind]
        TURNS = 2 if kind == "b" else 1
        assert TURN_AT + SIDES // TURNS < U
        SUMS_AT, OUT_AT = 2, 3
        LAST = [max(n for n, x in enumerate(units) if x[0] == t) for t in range(PAIR)]
        FIRST = [min(n for n, x in enumerate(units) if x[0] == t) for t in range(PAIR)]
        assert LAST[0] + 2 > OUT_AT and LAST[1] == U - 1

        def pairs(eng, body, step=None, per=0):
            body(0, 0, True, False)
            with eng.Fori(0, N // 2 - 1) as i:
                if step is not None:
                    step.loop(i, 2 * per)
                for q in (1, 2):
                    body(i * 2 + q, q % 2, False, False)
            if step is not None:
                step.end(N // 2 - 1)
            body(N - 1, 1, False, True)

        def turned_behind(u, m):
            n = (u - TURN_AT) * TURNS + m
            return n if 0 <= n < SIDES and m < TURNS else None

        def turn_place(n):
            return n // (2 * QG), n // QG % 2, n % QG

        with nc.Block() as block:

            @block.sync
            def _(sp):
                for dst, src in loads:
                    sp.dma_start(dst, src).then_inc(loaded, 16)

            @block.gpsimd
            def _(pool):
                g = nc.gpsimd
                step = Chain(pool, pool_step)
                step(g.memset(slots[:], 0.0))
                pool.wait_ge(loaded, LOADED)
                if kind == "c":
                    for t in range(PAIR):
                        for side in range(2):
                            dst = slots[:, t, side].rearrange("p (h w) -> p h w", h=H)[:, :, 6 * DH:7 * DH]
                            step(g.tensor_copy(dst, group[:, side].unsqueeze(1).to_broadcast([P, H, 8])))
                if kind == "d":
                    g.tensor_copy(causal[:], maskf[:])
                g.memset(one[:], 1.0)
                step(g.tensor_copy(ident16[:], ident[:]))
                give(pool, slots_zero, 1)
                pool.wait_ge(stats_done, 1)
                inner = norm.rstd if norm.inner_eps is None else norm.rboth

                def carry(n):
                    g.tensor_tensor(carrier[:, n:n + 1], ident[0:1, 0:1], ident[0:1, 0:1], ALU.mult)

                def normalise(k, p):
                    tiles = bass.ds(k * PAIR, PAIR)
                    pool.wait_ge(xT_ready, k + 1)
                    carry(p)
                    step(g.tensor_tensor(tmp[:, p], X[:, tiles, :], bcast(norm.mean[:, tiles], D), ALU.subtract))
                    g.tensor_tensor(xn[:, p], tmp[:, p], bcast(inner[:, tiles], D), ALU.mult)\
                        .then_inc(xn_ready, 1)

                def residual(c, p):
                    tiles = bass.ds(c * PAIR, PAIR)
                    pool.wait_ge(x_updated, c + 1)
                    carry(2 + p)
                    step(g.tensor_tensor(rtmp[:, p], X[:, tiles, :], bcast(norm.mean[:, tiles], D), ALU.subtract))
                    g.tensor_tensor(res[:, p], rtmp[:, p], bcast(norm.rstd[:, tiles], D), ALU.mult)\
                        .then_inc(res_ready, 1)

                def split(t, side):
                    src = whole[:, t, side].rearrange("p (h w) -> p h w", h=H)
                    slot = slots[:, t, side].rearrange("p (h w) -> p h w", h=H)[:, :, 0:6 * PW]\
                        .rearrange("p h (n w) -> p h n w", n=6)

                    def into(places):
                        shape = [P, H, len(range(6)[places]), PW]
                        return g.tensor_tensor(slot[:, :, places], src.unsqueeze(2).to_broadcast(shape),
                                               one[:].unsqueeze(2).unsqueeze(3).to_broadcast(shape), ALU.mult)
                    if side == 0:
                        step(into(slice(0, 3)))
                        step(g.tensor_tensor(src, src, slot[:, :, 0], ALU.subtract))
                        step(into(slice(3, 5)))
                        return g.tensor_tensor(slot[:, :, 5], src, slot[:, :, 3], ALU.subtract)
                    into(slice(0, 4, 3))
                    step(into(slice(5, 6)))
                    step(g.tensor_tensor(src, src, slot[:, :, 0], ALU.subtract))
                    step(into(slice(1, 5, 3)))
                    return g.tensor_tensor(slot[:, :, 2], src, slot[:, :, 1], ALU.subtract)

                def fill(k, p):
                    for t in range(PAIR):
                        if kind == "d":
                            pool.wait_ge(prep_done, k * PAIR + (t + 1))
                            for side in range(2):
                                pairwise = qkv[:, p, t, side * D:(side + 1) * D]\
                                    .rearrange("p (h r e) -> p e h r", h=H, e=2)
                                cs = [rot[:, side, t, x].unsqueeze(1).to_broadcast([P, H, 4]) for x in range(2)]
                                ra3 = ra[:, side].rearrange("p (h r) -> p h r", h=H)
                                rb3 = rb[:, side].rearrange("p (h r) -> p h r", h=H)
                                g.tensor_tensor(ra3, pairwise[:, 0], cs[0], ALU.mult)
                                step(g.tensor_tensor(rb3, pairwise[:, 1], cs[1], ALU.mult))
                                step(g.tensor_tensor(whole[:, t, side], ra[:, side], rb[:, side], ALU.subtract))
                        for side in range(2):
                            if kind != "d":
                                pool.wait_ge(k_slotted if side else q_slotted, k * PAIR + (t + 1))
                            if kind == "b":
                                pool.wait_ge(prep_done, (k * PAIR + t) * PREP + (2 + side))
                            split(t, side).then_inc(filled, 1)
                            pool.wait_ge(filled, (k * PAIR + t) * 2 + (side + 1))

                def body(c, p, first, last):
                    if not last:
                        normalise(c + 1, 1 - p)
                        fill(c + 1, 1 - p)
                    if kind != "d":
                        residual(c, p)

                normalise(0, 0)
                fill(0, 0)
                pairs(pool, body, step, {"b": 2 + 6 * PAIR, "c": 2 + 6 * PAIR, "d": 1 + 10 * PAIR}[kind])

            @block.vector
            def _(dve):
                v = nc.vector
                step = Chain(dve, dve_step)
                give(dve, x_updated)
                give(dve, pt_ready)
                norm.dve(nc, dve, step, X)
                give(dve, stats_done, 1)
                dve.wait_ge(slots_zero, 1)
                if kind == "b":
                    for side in range(2):
                        dve.wait_ge(wcl_made, side + 1)
                        step(v.tensor_copy(wcl[:, side], psS[:, side]))
                    give(dve, const_ready, 1)

                def soften(t, side):
                    src = psP[:].rearrange("p (h n) -> p h n", h=H)
                    step(v.tensor_reduce(cm[:, side], src, AX, ALU.max))
                    v.tensor_tensor(cl[:], src, bcast(cm[:, side], NB), ALU.subtract).then_inc(cl_ready, 1)

                def spread(t, side, n):
                    dve.wait_ge(cl_exp, n)
                    step(v.tensor_reduce(cm[:, side], ce[:], AX, ALU.add))
                    step(v.reciprocal(cm[:, side], cm[:, side]))
                    if side == 0:
                        step(v.tensor_scalar(cm[:, side], cm[:, side], 0.1, None, ALU.mult))
                    dst = whole[:, t, side].rearrange("p (h w) -> p h w", h=H)[:, :, 0:NB]
                    v.tensor_tensor(dst, ce[:], bcast(cm[:, side], NB), ALU.mult).then_inc(prep_done, 1)

                def prepare(k, p, u):
                    if PROJ_AT <= u < PROJ_AT + PAIR * PREP:
                        n = u - PROJ_AT
                        t, part = n // PREP, n % PREP
                        dve.wait_ge(proj_ready, k * (PAIR * PREP) + (n + 1))
                        if part > 0:
                            soften(t, part - 1)
                        elif kind == "b":
                            v.tensor_copy(qkv[:, p, t], psP[:, 0:3 * D]).then_inc(prep_done, 1)
                        else:
                            v.tensor_tensor(qkv[:, p, t], psP[:, 0:3 * D], bqkv[:], ALU.add)\
                                .then_inc(prep_done, 1)

                def prepare_clusters(k, u):
                    if kind == "b" and PROJ_AT <= u < PROJ_AT + PAIR * PREP and (u - PROJ_AT) % PREP:
                        n = u - PROJ_AT
                        t, side = n // PREP, n % PREP - 1
                        spread(t, side, (k * PAIR + t) * 2 + (side + 1))
                        dve.wait_ge(prep_done, k * (PAIR * PREP) + (n + 1))

                def highest(c, u):
                    t, h, nh, kw, _ = units[u]
                    dve.wait_ge(s_ready, c * U + (u + 1))
                    v.tensor_reduce(nmax[:, t, h:h + nh], psS[:, u % 2].rearrange("p (h k) -> p h k", h=nh),
                                    AX, ALU.max, negate=True).then_inc(m_ready, 1)

                def scale(c, p, t):
                    dve.wait_ge(p_ready, c * U + (LAST[t] + 1 + AHEAD))
                    step(v.reciprocal(inv[:, t].rearrange("p (g r) -> p g r", r=HPB),
                                      total[:, p, t].rearrange("p (r g) -> p g r", r=HPB)))
                    dve.wait_ge(av_done, c * U + (LAST[t] + 1 + AHEAD))
                    v.tensor_tensor(o[:, t].rearrange("p (h f) -> p h f", h=H),
                                    psO[:, t, 0:D].rearrange("p (h f) -> p h f", h=H),
                                    bcast(inv[:, t], DH), ALU.mult).then_inc(o_ready, 1)

                def update(c, p):
                    tiles = bass.ds(c * PAIR, PAIR)
                    if kind != "d":
                        dve.wait_ge(res_ready, c + 1)
                    dve.wait_ge(out_ready, c + 1)
                    bias = bo[:].unsqueeze(1).to_broadcast([P, PAIR, D])
                    step(v.tensor_tensor(upd[:], psF[:, 0:PAIR], bias if kind == "d" else res[:, p], ALU.add))
                    if kind == "b":
                        v.tensor_copy(XA[:, tiles, :], upd[:]).then_inc(x_updated, 1)
                    else:
                        if kind == "c":
                            step(v.tensor_tensor(upd[:], upd[:], bias, ALU.add))
                        v.tensor_tensor(X[:, tiles, :], X[:, tiles, :], upd[:], ALU.add).then_inc(x_updated, 1)
                    dve.wait_ge(x_updated, c + (1 + AHEAD))

                def body(c, p, first, last):
                    for u in range(U):
                        if u == 1 and not first:
                            scale(c - 1, 1 - p, 1)
                        if u == LAST[0] + 2:
                            scale(c, p, 0)
                        if u + 1 < U:
                            highest(c, u + 1)
                        elif not last:
                            highest(c + 1, 0)
                        if not last:
                            prepare(c + 1, 1 - p, u)
                        dve.wait_ge(t_ready, c * U + (u + 1 + AHEAD))
                        v.tensor_copy(probT[:, u % 2], psT[:, u % 2]).then_inc(pt_ready, 1)
                        if not last:
                            prepare_clusters(c + 1, u)
                        if u == OUT_AT and not first:
                            update(c - 1, 1 - p)

                for u in range(U):
                    prepare(0, 0, u)
                    prepare_clusters(0, u)
                highest(0, 0)
                pairs(dve, body, step, PER_PAIR)
                scale(N - 1, 1, 1)
                update(N - 1, 1)

            @block.scalar
            def _(act):
                s = nc.scalar
                give(act, p_ready)
                norm.act(nc, act)
                act.wait_ge(loaded, LOADED)
                act.wait_ge(slots_zero, 1)
                if kind == "b":
                    for side in range(2):
                        act.wait_ge(wT_ready, side + 1)
                        s.activation(wT[:, side], psT[:, side, 0], ACT.Copy).then_inc(wT_copied, 1)
                def prepare(k, p, u):
                    if u == X_AT:
                        act.wait_ge(xT_ready, k + (1 + AHEAD))
                        xT = psF[:, 0:PAIR]
                        if affine:
                            s.activation(hT[:], xT, ACT.Identity, bias=bet[:], scale=gam[:]).then_inc(h_ready, 1)
                        else:
                            s.activation(hT[:], xT, ACT.Copy).then_inc(h_ready, 1)
                    if PROJ_AT <= u < PROJ_AT + PAIR * PREP:
                        n = u - PROJ_AT
                        t, part = n // PREP, n % PREP
                        if part:
                            act.wait_ge(cl_ready, (k * PAIR + t) * 2 + part)
                            s.activation(ce[:], cl[:], ACT.Exp).then_inc(cl_exp, 1)
                        elif kind != "d":
                            act.wait_ge(prep_done, k * (PAIR * PREP) + (n + 1))
                            for side in range(2):
                                dst = whole[:, t, side].rearrange("p (h w) -> p h w", h=H)[:, :, PW - DH:PW]
                                src = qkv[:, p, t, side * D:(side + 1) * D].rearrange("p (h f) -> p h f", h=H)
                                s.activation(dst, src, ACT.Copy, scale=1.0 if side else SCALE)\
                                    .then_inc(k_slotted if side else q_slotted, 1)

                def take_turned(k, p, u, m):
                    n = turned_behind(u, m)
                    if n is not None:
                        t, side, b = turn_place(n)
                        act.wait_ge(qt_ready, k * SIDES + (n + 1))
                        src = psP[:].bitcast(BF16)[:, 0:BPB * P]
                        s.activation(turned[:, p, side, BPB * b:BPB * b + BPB, t * P:(t + 1) * P],
                                     src.rearrange("p (b n) -> p b n", b=BPB), ACT.Copy)\
                            .then_inc(qt_copied, 1)

                def exponentials(c, p, u):
                    t, h, nh, kw, _ = units[u]
                    act.wait_ge(m_ready, c * U + (u + 1))
                    act.wait_ge(t_ready, c * U + (u + 1))
                    for j in range(nh):
                        last = s.activation(prob[:, u % 2, j * kw:(j + 1) * kw],
                                            psS[:, u % 2, j * kw:(j + 1) * kw], ACT.Exp,
                                            bias=nmax[:, t, h + j:h + j + 1],
                                            accum_out=total[:, p, t, h + j:h + j + 1])
                    last.then_inc(p_ready, 1)

                def sums(c):
                    act.wait_ge(oT_ready, c + 1)
                    s.activation(oT[:], psF[:, 2:2 + PAIR], ACT.Copy).then_inc(oT_copied, 1)

                def body(c, p, first, last):
                    for u in range(U):
                        if not last and kind != "d":
                            take_turned(c + 1, 1 - p, u, 0)
                        if u + 1 < U:
                            exponentials(c, p, u + 1)
                        elif not last:
                            exponentials(c + 1, 1 - p, 0)
                        if not last:
                            prepare(c + 1, 1 - p, u)
                            take_turned(c + 1, 1 - p, u, 0 if kind == "d" else 1)
                        if u == SUMS_AT and not first:
                            sums(c - 1)

                for u in range(U):
                    prepare(0, 0, u)
                    for m in range(TURNS):
                        take_turned(0, 0, u, m)
                exponentials(0, 0, 0)
                pairs(act, body)
                sums(N - 1)

            @block.tensor
            def _(pe):
                mm, turn = nc.tensor.matmul, nc.tensor.transpose
                give(pe, xT_ready)
                give(pe, t_ready)
                give(pe, av_done)
                pe.wait_ge(loaded, LOADED)
                if kind == "b":
                    for side in range(2):
                        turn(psT[:, side, 0], wqkv[:, side * D:(side + 1) * D], ident[:]).then_inc(wT_ready, 1)
                    for side in range(2):
                        pe.wait_ge(wT_copied, side + 1)
                        mm(psS[:, side], wT[:, side], wh[:, side], start=True, stop=True).then_inc(wcl_made, 1)
                    pe.wait_ge(const_ready, 1)
                pe.wait_ge(slots_zero, 1)

                def prepare(k, p, u):
                    if u == X_AT:
                        pe.wait_ge(xn_ready, k + 1)
                        if not isinstance(k, int) or k:
                            pe.wait_ge(x_updated, k)
                        for t in range(PAIR):
                            last = turn(psF[:, t], xn[:, p, t], ident[:])
                        last.then_inc(xT_ready, 1)
                    if PROJ_AT <= u < PROJ_AT + PAIR * PREP:
                        n = u - PROJ_AT
                        t, part = n // PREP, n % PREP
                        if n == 0:
                            pe.wait_ge(h_ready, k + 1)
                            if not isinstance(k, int) or k:
                                pe.wait_ge(qt_copied, k * SIDES)
                        elif part == 1 or kind != "b":
                            pe.wait_ge(prep_done, k * (PAIR * PREP) + n)
                        else:
                            pe.wait_ge(cl_ready, k * (PAIR * 2) + (n - n // PREP - (part > 0)))
                        w = wcl[:, part - 1] if part else wqkv[:]
                        mm(psP[:] if part else psP[:, 0:3 * D], hT[:, t], w, start=True, stop=True)\
                            .then_inc(proj_ready, 1)

                def turn_slots(k, u, m):
                    n = turned_behind(u, m)
                    if n is not None:
                        t, side, b = turn_place(n)
                        pe.wait_ge(filled, (k * PAIR + t) * 2 + (side + 1))
                        if n == 0:
                            pe.wait_ge(prep_done, (k + 1) * (PAIR * PREP))
                        else:
                            pe.wait_ge(qt_copied, k * SIDES + n)
                        bank = psP[:].bitcast(BF16)
                        for j in range(BPB):
                            g = BPB * b + j
                            last = turn(bank[:, j * P:(j + 1) * P], slots[:, t, side, g * P:(g + 1) * P],
                                        ident16[:])
                        last.then_inc(qt_ready, 1)

                def scores(c, p, u):
                    t, h, nh, kw, k0 = units[u]
                    if u == 0:
                        pe.wait_ge(qt_copied, (c + 1) * SIDES)
                    pe.wait_ge(p_ready, c * U + (u + 1))
                    if kind == "d":
                        mm(psS[:, u % 2].rearrange("p (h k) -> p h k", h=nh), ident16[:],
                           causal[:, 2 * P - kw:2 * P].unsqueeze(1).to_broadcast([P, nh, kw]),
                           start=True, stop=False)
                    for j in range(nh):
                        for n in range(BPH):
                            g, r = (h + j) * BPH % NG + n, (h + j) // NG
                            rows = slice(W * r, W * r + W) if HPB > 1 else slice(0, P)
                            qT = turned[rows, p, 0, g, t * P:(t + 1) * P]
                            last = mm(psS[:, u % 2, j * kw:(j + 1) * kw], qT, turned[rows, p, 1, g, k0:k0 + kw],
                                      start=(kind != "d" and n == 0),
                                      stop=(n == BPH - 1 and (kind != "d" or j == nh - 1)))
                    last.then_inc(s_ready, 1)

                def turn_probs(c, u):
                    pe.wait_ge(p_ready, c * U + (u + 1 + AHEAD))
                    pe.wait_ge(pt_ready, c * U + (u + 1))
                    for j in range(4):
                        last = turn(psT[:, u % 2, j], prob[:, u % 2, j * P:(j + 1) * P], ident[:])
                    last.then_inc(t_ready, 1)

                def values(c, p, u, first=False):
                    t, h, nh, kw, k0 = units[u]
                    pe.wait_ge(pt_ready, c * U + (u + 1 + AHEAD))
                    if u == FIRST[t] and not first:
                        pe.wait_ge(o_ready, c * PAIR + (t + 1 - PAIR))
                    nk = kw // P
                    for j in range(4):
                        place, kt = h + j // nk, (k0 // P) + j % nk
                        head = place % NG * HPB + place // NG
                        last = mm(psO[:, t, head * DH:(head + 1) * DH], probT[:, u % 2, j],
                                  qkv[:, p, kt, 2 * D + head * DH:2 * D + (head + 1) * DH],
                                  start=(j % nk == 0), stop=(j % nk == nk - 1))
                    last.then_inc(av_done, 1)

                def sums(c):
                    pe.wait_ge(o_ready, c * PAIR + PAIR)
                    pe.wait_ge(x_updated, c + AHEAD)
                    for t in range(PAIR):
                        last = turn(psF[:, 2 + t], o[:, t], ident[:])
                    last.then_inc(oT_ready, 1)

                def output(c):
                    pe.wait_ge(oT_copied, c + 1)
                    for t in range(PAIR):
                        last = mm(psF[:, t], oT[:, t], wo[:], start=True, stop=True)
                    last.then_inc(out_ready, 1)

                def body(c, p, first, last):
                    for u in range(U):
                        if u + 1 < U:
                            scores(c, p, u + 1)
                        elif not last:
                            scores(c + 1, 1 - p, 0)
                        if not last:
                            prepare(c + 1, 1 - p, u)
                            turn_slots(c + 1, u, 0)
                        if u == SUMS_AT and not first:
                            if not last:
                                pe.wait_ge(h_ready, c + 2)
                            sums(c - 1)
                        if u == OUT_AT and not first:
                            output(c - 1)
                        turn_probs(c, u)
                        if u:
                            values(c, p, u - 1, first)
                        elif not first:
                            values(c - 1, 1 - p, U - 1)
                        if not last:
                            turn_slots(c + 1, u, 1)

                for u in range(U):
                    prepare(0, 0, u)
                    for m in range(TURNS):
                        turn_slots(0, u, m)
                scores(0, 0, 0)
                pairs(pe, body)
                values(N - 1, 1, U - 1)
                sums(N - 1)
                output(N - 1)


def lay_attn(i, a, rows):
    import numpy as np
    L = "L1_attn_a_"
    a["c_wqkv"] = np.concatenate([i[L + "W" + x] for x in "qkv"], axis=1)
    a["c_bqkv"] = rows(np.concatenate([i[L + "b" + x] for x in "qkv"]))
    a["c_wo"], a["c_bo"] = i[L + "Wo"], rows(i[L + "bo"])
    a["c_gam"], a["c_bet"] = i[L + "ln_g"].reshape(P, 1), i[L + "ln_b"].reshape(P, 1)
    own = (np.arange(P)[:, None] % 8 == np.arange(8)[None, :]).astype(np.float32)
    a["c_group"] = np.stack([own * np.float32(NEG), 1 - own], axis=1)
    L = "L1_attn_b_"
    a["d_wqkv"] = np.concatenate([i[L + "W" + x].T for x in "qkv"], axis=1)
    a["d_bqkv"] = rows(np.concatenate([i[L + "b" + x] for x in "qkv"]))
    a["d_wo"], a["d_bo"] = i[L + "Wo"].T, rows(i[L + "bo"])
    steps = np.arange(1, T + 1, dtype=np.float32)[:, None]
    theta = (np.float32(1.0 / 10000.0) ** (np.float32(2.0) * np.arange(4, dtype=np.float32) / np.float32(8)))
    angle = steps * theta
    cs = np.stack([np.cos(angle), np.sin(angle)], axis=1).astype(np.float32)
    cs = cs.reshape(2, P, 2, 4).transpose(1, 0, 2, 3)
    a["d_rot"] = np.stack([cs * np.float32(8.0 ** -0.5), cs], axis=1)
    a["d_mask"] = np.where(np.arange(2 * P)[None, :] - P > np.arange(P)[:, None], NEG, 0.0).astype(np.float32)
    L = "L0_attn_b_"
    a["b_wqkv"] = np.concatenate([i[L + "W" + x].reshape(D, D) for x in "qkv"], axis=1)
    a["b_wo"] = i[L + "Wo"].reshape(D, D)
    a["b_gam"], a["b_bet"] = i[L + "ln1_g"].reshape(P, 1), i[L + "ln1_b"].reshape(P, 1)
    wh = np.zeros((D, 2, 16, 32), np.float32)
    for h in range(16):
        wh[8 * h:8 * h + 8, 0, h] = i[L + "Whq"][h]
        wh[8 * h:8 * h + 8, 1, h] = i[L + "Whk"][h]
    a["b_wh"] = wh.reshape(D, 2, 512)
    a["b_mlp_fc1"], a["b_mlp_fc2"] = i[L + "W1"], i[L + "W2"]
    a["b_mlp_b1"], a["b_mlp_b2"] = i[L + "b1"].reshape(-1, P).T, rows(i[L + "b2"])
    a["b_mlp_gam"], a["b_mlp_bet"] = i[L + "ln2_g"].reshape(P, 1), i[L + "ln2_b"].reshape(P, 1)


def cell_stage(nc, name, X, ident, a):
    BL, NS = 4, 32
    HR = NS // 2
    KN, Q, V, BE, WU, OM, SM, REC = 0, NS, 2 * NS, 2 * NS + HR, 96, 97, 98, 100
    PK, PV, PB, PQ, PL, PROJ = 0, 128, 256, 384, 416, 420
    TC = 16
    NCH = T // TC
    rec_dram = nc.dram_tensor(f"{name}_rec", (B * T, 2 * BL * REC), F32, kind="Internal").ap()
    cell_dram = nc.dram_tensor(f"{name}_cell", (B, TC + T, NS), F32, kind="Internal").ap()

    with nc.cleanup_on_exit(), ExitStack() as ctx:
        st = Stage(nc, ctx, name + "p")
        norm = Norm(st)
        tmp = st.sb("tmp", [P, 2, TPC, D])
        xn = st.sb("xn", [P, 2, TPC, D])
        hT = st.sb("hT", [P, 2, CW])
        xp = st.sb("xp", [P, 2, CW])
        win = st.sb("win", [P, D])
        wcat = st.sb("wcat", [P, PROJ])
        bbeta = st.sb("bbeta", [P, BL * NS])
        lower = st.sb("lower", [P, BL, BL])
        raw = st.sb("raw", [P, 2, TPC, PROJ])
        sq = st.sb("sq", [P, TPC * BL, NS])
        ss = st.sb("ss", [P, TPC * BL])
        nrm = st.sb("nrm", [P, TPC * BL])
        bt = st.sb("bt", [P, TPC, BL * NS])
        lg = st.sb("lg", [P, TPC, BL])
        ex = st.sb("ex", [P, TPC, BL])
        gt = st.sb("gt", [P, TPC, BL, BL])
        eq = st.sb("eq", [P, TPC, BL, BL])
        rank = st.sb("rank", [P, TPC, BL])
        one = st.sb("one", [P, TPC])
        rec = st.sb("rec", [P, 2, TPC, 2 * BL * REC])
        psT = st.ps("psT", [P, CW])
        psA = st.ps("psA", [P, CW])
        psR = st.ps("psR", [P, TPC, 512])
        loaded, dve_step, pool_step = st.sem("loaded"), st.sem("dve_step"), st.sem("pool_step")
        stats_done, xn_ready, xT_ready = st.sem("stats_done"), st.sem("xn_ready"), st.sem("xT_ready")
        h_ready, a_ready, xp_ready = st.sem("h_ready"), st.sem("a_ready"), st.sem("xp_ready")
        r_ready, raw_ready, raw_read = st.sem("r_ready"), st.sem("raw_ready"), st.sem("raw_read")
        ss_ready, nrm_ready, bt_ready = st.sem("ss_ready"), st.sem("nrm_ready"), st.sem("bt_ready")
        lg_ready, ex_ready, kn_ready = st.sem("lg_ready"), st.sem("ex_ready"), st.sem("kn_ready")
        rec_act, rec_dve = st.sem("rec_act"), st.sem("rec_dve")
        kept = [st.sem(f"kept{q}") for q in range(2)]
        STEPS = 18

        def record(q, lo, n):
            return rec[:, q].rearrange("p j (n h f) -> p (j n) h f", h=2, f=REC)[:, :, :, lo:lo + n]

        with nc.Block() as block:

            @block.sync
            def _(sp):
                for dst, src in ((win[:], a["a_win"]), (wcat[:], a["a_wcat"]), (bbeta[:], a["a_bbeta"]),
                                 (lower[:], a["a_lower"])):
                    sp.dma_start(dst, src).then_inc(loaded, 16)
                tiles_of = rec_dram.rearrange("(r p) f -> p r f", p=P)
                for q in range(2):
                    sp.drain().then_inc(kept[q], 16)
                with sp.Fori(0, NC // 2) as i:
                    for q in range(2):
                        c = i * 2 + q
                        sp.wait_ge(rec_act, c + 1)
                        sp.wait_ge(rec_dve, c + 1)
                        sp.dma_start(tiles_of[:, bass.ds(c * TPC, TPC), :], rec[:, q]).then_inc(kept[q], 16)
                for q in range(2):
                    sp.wait_ge(kept[q], 16 * (NC // 2 + 1))

            @block.gpsimd
            def _(pool):
                g = nc.gpsimd
                g.memset(rec[:], 0.0)
                give(pool, pool_step, 1)
                pool.wait_ge(stats_done, 1)
                with pool.Fori(0, NC // 2) as i:
                    for q in range(2):
                        c = i * 2 + q
                        tiles = bass.ds(c * TPC, TPC)
                        pool.wait_ge(xT_ready, c + 1)
                        g.tensor_tensor(tmp[:, q], X[:, tiles, :], bcast(norm.mean[:, tiles], D), ALU.subtract)\
                            .then_inc(pool_step, 1)
                        pool.wait_ge(pool_step, c + 2)
                        g.tensor_tensor(xn[:, q], tmp[:, q], bcast(norm.rstd[:, tiles], D), ALU.mult)\
                            .then_inc(xn_ready, 1)

            @block.vector
            def _(dve):
                v = nc.vector
                step = Chain(dve, dve_step)
                norm.dve(nc, dve, step, X)
                give(dve, stats_done, 1)
                dve.wait_ge(loaded, 16 * 4)
                dve.wait_ge(pool_step, 1)
                with dve.Fori(0, NC // 2) as i:
                    step.loop(i, 2 * STEPS)
                    for q in range(2):
                        c = i * 2 + q
                        dve.wait_ge(raw_ready, c + 1)
                        k3 = raw[:, q, :, PK:PK + BL * NS].rearrange("p j (n r) -> p j n r", n=BL)
                        step(v.tensor_tensor(sq[:].rearrange("p (j n) r -> p j n r", n=BL), k3, k3, ALU.mult))
                        v.tensor_reduce(ss[:], sq[:], AX, ALU.add).then_inc(ss_ready, 1)
                        v.tensor_tensor(bt[:], raw[:, q, :, PB:PB + BL * NS],
                                        bbeta[:].unsqueeze(1).to_broadcast([P, TPC, BL * NS]), ALU.add)\
                            .then_inc(bt_ready, 1)
                        l = raw[:, q, :, PL:PL + BL]
                        step(v.tensor_reduce(one[:], l, AX, ALU.max))
                        v.tensor_tensor(lg[:], l, bcast(one[:], BL), ALU.subtract).then_inc(lg_ready, 1)
                        other = l.unsqueeze(2).to_broadcast([P, TPC, BL, BL])
                        own = l.unsqueeze(3).to_broadcast([P, TPC, BL, BL])
                        step(v.tensor_tensor(gt[:], other, own, ALU.is_gt))
                        step(v.tensor_tensor(eq[:], other, own, ALU.is_equal))
                        step(v.tensor_tensor(eq[:], eq[:], lower[:].unsqueeze(1).to_broadcast([P, TPC, BL, BL]),
                                             ALU.mult))
                        step(v.tensor_tensor(gt[:], gt[:], eq[:], ALU.add))
                        step(v.tensor_reduce(rank[:], gt[:], AX, ALU.add))
                        step(v.tensor_scalar(rank[:], rank[:], 1.5, None, ALU.is_lt))
                        dve.wait_ge(ex_ready, c + 1)
                        step(v.tensor_reduce(one[:], ex[:], AX, ALU.add))
                        step(v.reciprocal(one[:], one[:]))
                        step(v.tensor_tensor(ex[:], ex[:], bcast(one[:], BL), ALU.mult))
                        dve.wait_ge(kept[q], i * 16 + 16)
                        both = lambda t: t[:].rearrange("p j n -> p (j n)").unsqueeze(2)\
                            .to_broadcast([P, TPC * BL, 2])
                        place = lambda lo: record(q, lo, 1).rearrange("p x h f -> p x (h f)")
                        dst = rec[:, q].rearrange("p j (x f) -> p j x f", f=REC)[:, :, :, V:V + HR]
                        v.tensor_copy(dst, raw[:, q, :, PV:PV + BL * NS].rearrange("p j (x r) -> p j x r", r=HR))
                        v.tensor_copy(place(SM), both(ex))
                        step(v.tensor_tensor(rank[:], rank[:], ex[:], ALU.mult))
                        step(v.tensor_reduce(one[:], rank[:], AX, ALU.add))
                        step(v.tensor_scalar(one[:], one[:], 1e-8, None, ALU.add))
                        step(v.reciprocal(one[:], one[:]))
                        step(v.tensor_tensor(rank[:], rank[:], bcast(one[:], BL), ALU.mult))
                        v.tensor_copy(place(WU), both(rank))
                        v.tensor_scalar(place(OM), both(rank), -1.0, 1.0, ALU.mult, ALU.add)
                        dve.wait_ge(nrm_ready, c + 1)
                        step(v.tensor_scalar(ss[:], nrm[:], 1e-6, None, ALU.add))
                        step(v.reciprocal(ss[:], ss[:]))
                        for h in range(2):
                            last = v.tensor_tensor(record(q, KN, NS)[:, :, h].rearrange(
                                "p (j n) r -> p j n r", n=BL), k3,
                                ss[:].rearrange("p (j n) -> p j n", n=BL).unsqueeze(3)
                                .to_broadcast([P, TPC, BL, NS]), ALU.mult)
                        last.then_inc(rec_dve, 1)
                        dve.wait_ge(rec_dve, c + 1)
                step.end(NC // 2)

            @block.scalar
            def _(act):
                s = nc.scalar
                norm.act(nc, act)
                act.wait_ge(pool_step, 1)
                with act.Fori(0, NC // 2) as i:
                    for q in range(2):
                        c = i * 2 + q
                        act.wait_ge(xT_ready, c + (1 + AHEAD))
                        s.activation(hT[:, q], psT[:], ACT.Copy).then_inc(h_ready, 1)
                        act.wait_ge(a_ready, c + 1)
                        s.activation(xp[:, q], psA[:], ACT.Silu).then_inc(xp_ready, 1)
                        act.wait_ge(r_ready, c + 1)
                        act.wait_ge(kept[q], i * 16 + 16)
                        s.activation(raw[:, q], psR[:, :, 0:PROJ], ACT.Copy).then_inc(raw_ready, 1)
                        act.wait_ge(raw_ready, c + 1)
                        for j in range(TPC):
                            s.activation(rec[:, q, j].rearrange("p (x f) -> p x f", f=REC)[:, :, Q:Q + NS],
                                         raw[:, q, j, PQ:PQ + NS].unsqueeze(1).to_broadcast([P, 2 * BL, NS]),
                                         ACT.Copy)
                        act.wait_ge(ss_ready, c + 1)
                        s.activation(nrm[:], ss[:], ACT.Sqrt).then_inc(nrm_ready, 1)
                        act.wait_ge(lg_ready, c + 1)
                        s.activation(ex[:], lg[:], ACT.Exp).then_inc(ex_ready, 1)
                        act.wait_ge(bt_ready, c + 1)
                        dst = rec[:, q].rearrange("p j (x f) -> p j x f", f=REC)[:, :, :, BE:BE + HR]
                        s.activation(dst, bt[:].rearrange("p j (x r) -> p j x r", r=HR), ACT.Sigmoid)\
                            .then_inc(rec_act, 1)

            @block.tensor
            def _(pe):
                give(pe, xT_ready)
                pe.wait_ge(loaded, 16 * 4)
                with pe.Fori(0, NC // 2) as i:
                    for q in range(2):
                        c = i * 2 + q
                        pe.wait_ge(xn_ready, c + 1)
                        transpose_chunk(nc, pe, psT, xn[:, q], ident).then_inc(xT_ready, 1)
                        pe.wait_ge(h_ready, c + 1)
                        nc.tensor.matmul(psA[:], win[:], hT[:, q], start=True, stop=True).then_inc(a_ready, 1)
                        pe.wait_ge(xp_ready, c + 1)
                        for j in range(TPC):
                            last = nc.tensor.matmul(psR[:, j, 0:PROJ], xp[:, q, j * P:(j + 1) * P], wcat[:],
                                                    start=True, stop=True)
                        last.then_inc(r_ready, 1)

    with nc.cleanup_on_exit(), ExitStack() as ctx:
        st = Stage(nc, ctx, name + "s")
        R = st.sb("R", [P, 2, TC, REC])
        S = st.sb("S", [P, HR, NS])
        prod = st.sb("prod", [P, HR, NS])
        ret = st.sb("ret", [P, HR])
        delta = st.sb("delta", [P, HR])
        outer = st.sb("outer", [P, HR, NS])
        decay = st.sb("decay", [P, HR, NS])
        pre = st.sb("pre", [P, HR, NS])
        upd = st.sb("upd", [P, HR, NS])
        keep = st.sb("keep", [P, HR, NS])
        read = st.sb("read", [P, HR, NS])
        sq = st.sb("sq", [P, 2, TC, HR])
        smc = st.sb("smc", [P, 2, TC])
        ex = st.sb("ex", [P, TC * HR])
        sig = st.sb("sig", [P, TC * HR])
        g1 = st.sb("g1", [P, TC * HR])
        g2 = st.sb("g2", [P, TC * HR])
        zo = st.sb("zo", [NS, 2, TC, HR])
        sel = st.sb("sel", [P, NS])
        psZ = st.ps("psZ", [NS, TC * HR])
        loaded, zeroed = st.sem("loaded"), st.sem("zeroed")
        rec_in = [st.sem(f"rec_in{q}") for q in range(2)]
        s_ready, step_sem, ret_step = st.sem("s_ready"), st.sem("dve_step"), st.sem("pool_step")
        decay_ready, read_ready, sq_ready = st.sem("decay_ready"), st.sem("read_ready"), st.sem("sq_ready")
        pre_ready, upd_ready, keep_ready = st.sem("pre_ready"), st.sem("upd_ready"), st.sem("keep_ready")
        sm_kept, ex_ready, sig_ready = st.sem("sm_kept"), st.sem("ex_ready"), st.sem("sig_ready")
        g_ready, z_ready, zo_ready = st.sem("g_ready"), st.sem("z_ready"), st.sem("zo_ready")
        stored = [st.sem(f"stored{q}") for q in range(2)]
        K_EXP, K_SIG, K_GATE, K_OUT = 2, 4, 6, 8
        DVE_STEPS = TC * 4 + 1

        def out_chunk(n):
            return cell_dram.rearrange("b t (h r) -> h b t r", h=2)[:, :, bass.ds(n * TC, TC), :]

        with nc.Block() as block:

            @block.sync
            def _(sp):
                src = rec_dram.rearrange("(b t) (x f) -> x b t f", b=B, f=REC)

                def load(n, q):
                    for x in range(2 * BL):
                        sp.dma_start(R[x * B:(x + 1) * B, q], src[x, :, bass.ds(n * TC, TC), :])\
                            .then_inc(rec_in[q], 16)

                def store(n, q):
                    sp.wait_ge(zo_ready, n + 1)
                    for h in range(2):
                        sp.dma_start(out_chunk(n)[h], zo[h * B:(h + 1) * B, q]).then_inc(stored[q], 16)

                sp.dma_start(sel[:], a["a_sel"]).then_inc(loaded, 16)
                for q in range(2):
                    sp.drain().then_inc(stored[q], 32)
                load(0, 0)
                with sp.Fori(0, NCH // 2 - 1) as i:
                    for q in range(2):
                        n = i * 2 + q
                        sp.wait_ge(sm_kept, n + 1)
                        load(n + 1, 1 - q)
                        store(n, q)
                n = NCH - 2
                sp.wait_ge(sm_kept, n + 1)
                load(n + 1, 1)
                store(n, 0)
                store(n + 1, 1)
                store(n + 2, 0)
                for q in range(2):
                    sp.wait_ge(stored[q], 32 * (NCH // 2 + (2 if q == 0 else 1)))

            def chunk_loop(eng, body):
                with eng.Fori(0, NCH // 2) as i:
                    for q in range(2):
                        body(i, q)

            @block.gpsimd
            def _(pool):
                g = nc.gpsimd
                g.memset(R[:, 1], 0.0)
                g.memset(read[:], 0.0)
                g.memset(sq[:], 0.0)
                g.memset(smc[:], 0.0)
                give(pool, zeroed, 1)

                def read_state(q, k):
                    row = R[:, q if k else 1 - q, (k - 1) % TC, Q:Q + NS]
                    g.tensor_tensor(read[:], S[:], row.unsqueeze(1).to_broadcast([P, HR, NS]), ALU.mult)\
                        .then_inc(read_ready, 1)

                def gate_1(n, pq, count):
                    g.tensor_tensor(g1[:], sq[:, pq].rearrange("p t r -> p (t r)"),
                                    sq[:, pq].rearrange("p t r -> p (t r)"), ALU.mult).then_inc(ret_step, 1)
                    pool.wait_ge(ret_step, n * 2 + 1)
                    g.tensor_tensor(g2[:].rearrange("p (t r) -> p t r", r=HR),
                                    g1[:].rearrange("p (t r) -> p t r", r=HR), bcast(smc[:, pq], HR), ALU.mult)\
                        .then_inc(ret_step, 1)
                    pool.wait_ge(ret_step, n * 2 + 2)

                def gate_2(n):
                    pool.wait_ge(sig_ready, n + 1)
                    g.tensor_tensor(g1[:], g2[:], sig[:], ALU.mult).then_inc(g_ready, 1)

                def body(i, q):
                    n = i * 2 + q
                    pool.wait_ge(rec_in[q], i * (16 * 2 * BL) + 16 * 2 * BL)
                    for k in range(TC):
                        pool.wait_ge(s_ready, n * TC + (k + 1))
                        g.tensor_tensor(decay[:], S[:], bcast(R[:, q, k, BE:BE + HR], NS), ALU.mult)\
                            .then_inc(decay_ready, 1)
                        read_state(q, k)
                        if k == K_EXP:
                            pool.wait_ge(z_ready, n + 1)
                            gate_1(n, 1 - q, n)
                        if k == K_GATE:
                            gate_2(n)
                pool.wait_ge(zeroed, 1)
                chunk_loop(pool, body)
                pool.wait_ge(s_ready, T + 1)
                read_state(0, 0)
                pool.wait_ge(sq_ready, T + 1)
                pool.wait_ge(z_ready, NCH + 1)
                gate_1(NCH, 1, NCH)
                gate_2(NCH)

            @block.vector
            def _(dve):
                v = nc.vector
                step = Chain(dve, step_sem)
                v.memset(S[:], 0.0).then_inc(s_ready, 1)
                dve.wait_ge(zeroed, 1)

                def reduce_read(q, k, count):
                    dve.wait_ge(read_ready, count)
                    dst = sq[:, q if k else 1 - q, (k - 1) % TC]
                    v.tensor_reduce(dst, read[:], AX, ALU.add).then_inc(sq_ready, 1)

                def sigmoid(n):
                    dve.wait_ge(ex_ready, n + 1)
                    step(v.tensor_scalar(ex[:], ex[:], 1.0, None, ALU.add))
                    v.reciprocal(sig[:], ex[:]).then_inc(sig_ready, 1)

                def body(i, q):
                    n = i * 2 + q
                    dve.wait_ge(rec_in[q], i * (16 * 2 * BL) + 16 * 2 * BL)
                    for k in range(TC):
                        kn = R[:, q, k, KN:KN + NS].unsqueeze(1).to_broadcast([P, HR, NS])
                        dve.wait_ge(s_ready, n * TC + (k + 1))
                        step(v.tensor_tensor(prod[:], S[:], kn, ALU.mult))
                        step(v.tensor_reduce(ret[:], prod[:], AX, ALU.add))
                        step(v.tensor_tensor(delta[:], R[:, q, k, V:V + HR], ret[:], ALU.subtract))
                        step(v.tensor_tensor(outer[:], bcast(delta[:], NS), kn, ALU.mult))
                        dve.wait_ge(decay_ready, n * TC + (k + 1))
                        v.tensor_tensor(pre[:], decay[:], outer[:], ALU.add).then_inc(pre_ready, 1)
                        reduce_read(q, k, n * TC + (k + 1))
                        if k == K_SIG:
                            sigmoid(n)
                        dve.wait_ge(keep_ready, n * TC + (k + 1))
                        dve.wait_ge(upd_ready, n * TC + (k + 1))
                        v.scalar_tensor_tensor(S[:], upd[:], R[:, q, k, WU:WU + 1], keep[:], ALU.mult, ALU.add)\
                            .then_inc(s_ready, 1)
                with dve.Fori(0, NCH // 2) as i:
                    step.loop(i, 2 * DVE_STEPS)
                    for q in range(2):
                        body(i, q)
                step.end(NCH // 2)
                reduce_read(0, 0, T + 1)
                sigmoid(NCH)

            @block.scalar
            def _(act):
                s = nc.scalar
                act.wait_ge(zeroed, 1)

                def exponent(n, pq, count):
                    act.wait_ge(sq_ready, count)
                    s.activation(ex[:], sq[:, pq].rearrange("p t r -> p (t r)"), ACT.Exp, scale=-1.0)\
                        .then_inc(ex_ready, 1)

                def out(i, n, q):
                    act.wait_ge(z_ready, n + 2)
                    act.wait_ge(stored[q], i * 32 + 32)
                    s.activation(zo[:, q].rearrange("p t r -> p (t r)"), psZ[:], ACT.Copy).then_inc(zo_ready, 1)

                def body(i, q):
                    n = i * 2 + q
                    act.wait_ge(rec_in[q], i * (16 * 2 * BL) + 16 * 2 * BL)
                    for k in range(TC):
                        act.wait_ge(s_ready, n * TC + (k + 1))
                        s.activation(keep[:], S[:], ACT.Copy, scale=R[:, q, k, OM:OM + 1]).then_inc(keep_ready, 1)
                        act.wait_ge(pre_ready, n * TC + (k + 1))
                        s.activation(upd[:], pre[:], ACT.Tanh).then_inc(upd_ready, 1)
                        if k == K_EXP:
                            exponent(n, 1 - q, n * TC + 1)
                        if k == K_OUT:
                            out(i, n, q)
                            s.activation(smc[:, q], R[:, q, :, SM:SM + 1].rearrange("p t f -> p (t f)"),
                                         ACT.Copy).then_inc(sm_kept, 1)
                chunk_loop(act, body)
                exponent(NCH, 1, T + 1)
                out(NCH // 2, NCH, 0)

            @block.tensor
            def _(pe):
                pe.wait_ge(loaded, 16)
                give(pe, z_ready, 1)

                def gather(n):
                    pe.wait_ge(g_ready, n + 1)
                    pe.wait_ge(zo_ready, n)
                    nc.tensor.matmul(psZ[:], sel[:], g1[:], start=True, stop=True).then_inc(z_ready, 1)
                pe.wait_ge(g_ready, 1)
                nc.tensor.matmul(psZ[:], sel[:], g1[:], start=True, stop=True).then_inc(z_ready, 1)
                with pe.Fori(1, NCH + 1) as n:
                    gather(n)

    with nc.cleanup_on_exit(), ExitStack() as ctx:
        st = Stage(nc, ctx, name + "o")
        cell = st.sb("cell", [P, 2, TPC, NS])
        cT = st.sb("cT", [NS, 2, CW])
        wout = st.sb("wout", [NS, D])
        psT = st.ps("psT", [NS, 2, CW])
        psY = st.ps("psY", [P, 2, TPC, D])
        loaded, cT_ready, cT_copied = st.sem("loaded"), st.sem("cT_ready"), st.sem("cT_copied")
        y_ready, x_updated = st.sem("y_ready"), st.sem("x_updated")
        cell_in = [st.sem(f"cell_in{q}") for q in range(2)]
        with nc.Block() as block:

            @block.sync
            def _(sp):
                sp.dma_start(wout[:], a["a_wout"]).then_inc(loaded, 16)
                src = cell_dram[:, TC:TC + T, :].rearrange("b (h p) r -> p b h r", p=P)
                with sp.Fori(0, NC // 2) as i:
                    for q in range(2):
                        c = i * 2 + q
                        sp.wait_ge(cT_ready, c + 1)
                        for x in range(2):
                            sp.dma_start(cell[:, q, 2 * x:2 * x + 2], src[:, bass.ds(c * 2 + x, 1)]
                                         .rearrange("p b h r -> p (b h) r")).then_inc(cell_in[q], 16)

            @block.tensor
            def _(pe):
                give(pe, cT_ready)
                pe.wait_ge(loaded, 16)
                with pe.Fori(0, NC // 2) as i:
                    for q in range(2):
                        c = i * 2 + q
                        pe.wait_ge(cell_in[q], i * 32 + 32)
                        for j in range(TPC):
                            last = nc.tensor.transpose(psT[:, q, j * P:(j + 1) * P], cell[:, q, j], ident[:])
                        last.then_inc(cT_ready, 1)
                        pe.wait_ge(cT_copied, c + 1)
                        pe.wait_ge(x_updated, c + 1)
                        for j in range(TPC):
                            last = nc.tensor.matmul(psY[:, q, j], cT[:, q, j * P:(j + 1) * P], wout[:],
                                                    start=True, stop=True)
                        last.then_inc(y_ready, 1)

            @block.scalar
            def _(act):
                with act.Fori(0, NC // 2) as i:
                    for q in range(2):
                        act.wait_ge(cT_ready, i * 2 + (q + 1 + AHEAD))
                        nc.scalar.activation(cT[:, q], psT[:, q], ACT.Copy).then_inc(cT_copied, 1)

            @block.vector
            def _(dve):
                give(dve, x_updated)
                with dve.Fori(0, NC // 2) as i:
                    for q in range(2):
                        c = i * 2 + q
                        dve.wait_ge(y_ready, c + 1)
                        tiles = bass.ds(c * TPC, TPC)
                        nc.vector.tensor_tensor(X[:, tiles, :], X[:, tiles, :], psY[:, q], ALU.add)\
                            .then_inc(x_updated, 1)


def lay_cell(i, a, rows):
    import numpy as np
    L = "L0_attn_a_"
    a["a_win"] = i[L + "W_in"].T
    kv = i[L + "W_kv"].reshape(4, 2, 32, D)
    a["a_wcat"] = np.concatenate([kv[:, 0].reshape(128, D), kv[:, 1].reshape(128, D), i[L + "W_beta"],
                                  i[L + "W_q"], i[L + "W_router"]]).T
    a["a_bbeta"] = rows(i[L + "b_beta"].reshape(-1))
    a["a_lower"] = rows(np.tril(np.ones((4, 4), np.float32), -1))
    a["a_sel"] = np.tile(np.eye(32, dtype=np.float32), (4, 1))
    a["a_wout"] = i[L + "W_out"].T


def load_stage(nc, name, x, X, ident=None):
    with nc.cleanup_on_exit(), ExitStack() as ctx:
        st = Stage(nc, ctx, name)
        loaded, made = st.sem("loaded"), st.sem("made")
        with nc.Block() as block:

            @block.sync
            def _(sp):
                sp.dma_start(X[:], x.rearrange("b (h p) d -> p (b h) d", p=P)).then_inc(loaded, 16)
                sp.wait_ge(loaded, 16)

            if ident is None:
                return

            @block.gpsimd
            def _(pool):
                pool.memset(ident[:], 0.0).then_inc(made, 1)
                pool.wait_ge(made, 1)
                pool.affine_select(out=ident[:], in_=ident[:], compare_op=ALU.not_equal, fill=1.0, base=0,
                                   pattern=[[-1, P]], channel_multiplier=1).then_inc(made, 1)


def relay_stage(nc, name, X, group):
    with nc.cleanup_on_exit(), ExitStack() as ctx:
        st = Stage(nc, ctx, name)
        moved = st.sem("moved")
        kept = nc.dram_tensor(f"{name}_x", (B * T, D), F32, kind="Internal").ap()
        near = kept.rearrange("(r p) d -> p r d", p=P)
        far = kept.rearrange("(s g j) d -> s j g d", s=B, j=8)
        with nc.Block() as block:

            def move(eng, store, spread, done):
                if not spread:
                    dram = near
                    if store:
                        eng.dma_start(dram, X[:]).then_inc(moved, 16)
                    else:
                        eng.dma_start(X[:], dram).then_inc(moved, 16)
                    return done + 16
                for s in range(B):
                    tile = X[s * 8:s * 8 + 8]
                    if store:
                        eng.dma_start(far[s], tile).then_inc(moved, 16)
                    else:
                        eng.dma_start(tile, far[s]).then_inc(moved, 16)
                return done + 16 * B

            @block.sync
            def _(sp):
                done = move(sp, True, not group, 0)
                sp.wait_ge(moved, done)
                done = move(sp, False, group, done)
                sp.wait_ge(moved, done)


def store_stage(nc, X, out):
    with nc.cleanup_on_exit(), ExitStack() as ctx:
        st = Stage(nc, ctx, "store")
        stored = st.sem("stored")
        with nc.Block() as block:

            @block.sync
            def _(sp):
                sp.dma_start(out.rearrange("b (h p) d -> p (b h) d", p=P), X[:]).then_inc(stored, 16)
                sp.wait_ge(stored, 16)


def program(nc, a, out):
    with ExitStack() as ctx:
        X = ctx.enter_context(nc.sbuf_tensor("x_resident", [P, NT, D], F32))
        ident = ctx.enter_context(nc.sbuf_tensor("ident", [P, P], F32))
        load_stage(nc, "load", a["x"], X, ident)
        n = 0
        for s in STAGES:
            n += 1
            if s == "f":
                ffn_stage(nc, f"ffn{n}", X, ident, a)
            if s == "c":
                relay_stage(nc, f"group{n}", X, True)
                attention_stage(nc, f"rows{n}", "c", X, None, ident, a)
                relay_stage(nc, f"ungroup{n}", X, False)
            if s == "b":
                with nc.sbuf_tensor(f"xa{n}", [P, NT, D], F32) as XA:
                    attention_stage(nc, f"cluster{n}", "b", X, XA, ident, a)
                    ffn_stage(nc, f"mlp{n}", X, ident, a, XA)
            if s == "d":
                attention_stage(nc, f"causal{n}", "d", X, None, ident, a)
            if s == "m":
                last = n == len(STAGES)
                dest = out.rearrange("b t d -> (b t) d") if last else \
                    nc.dram_tensor(f"x_after{n}", (B * T, D), F32, kind="Internal").ap()
                moe_stage(nc, f"moe{n}", X, ident, a, dest)
                if not last:
                    load_stage(nc, f"load{n}", dest.rearrange("(b t) d -> b t d", b=B), X)
            if s == "a":
                cell_stage(nc, f"cell{n}", X, ident, a)
        if STAGES[-1] != "m":
            store_stage(nc, X, out)


def laid_out(i):
    import numpy as np
    i = {k: np.asarray(v) for k, v in i.items()}
    rows = lambda v: np.ascontiguousarray(np.broadcast_to(v, (P,) + v.shape))
    L = "L0_ffn_"
    a = {"x": i["L0_attn_a_x"],
         "f_fc1": i[L + "fc1_q"], "f_fc1_s": rows(i[L + "fc1_scales"][0]), "f_b1": i[L + "fc1_bias"].reshape(-1, P).T,
         "f_fc2": i[L + "fc2_q"], "f_fc2_s": rows(i[L + "fc2_scales"]), "f_b2": rows(i[L + "fc2_bias"]),
         "f_gam": i[L + "ln_gamma"].reshape(P, 1), "f_bet": i[L + "ln_beta"].reshape(P, 1)}
    lay_more(i, a, rows)
    return a


def kernel(**inputs):
    import numpy as np
    import concourse.bacc as bacc
    from concourse.bass_utils import run_bass_kernel_spmd

    nc = bacc.Bacc("TRN2", target_bir_lowering=False, num_devices=1)
    arrays, aps = {}, {}
    for name, a in laid_out(inputs).items():
        a = np.ascontiguousarray(a)
        arrays[f"in_{name}"] = a
        aps[name] = nc.dram_tensor(f"in_{name}", a.shape, mybir.dt.from_np(a.dtype), kind="ExternalInput").ap()
    out = nc.dram_tensor("out_0", (B, T, D), F32, kind="ExternalOutput").ap()
    program(nc, aps, out)
    r = run_bass_kernel_spmd(nc, [arrays], core_ids=[0])
    return r.results[0]["out_0"]
```
